# Optimizing a Trainium2 kernel written in Bass

```python
import numpy as np
import jax
import jax.numpy as jnp

def _softmax(x, axis=-1):
    return jax.nn.softmax(x, axis=axis)

def _gelu(x):
    return jax.nn.gelu(x, approximate=True)

def _silu(x):
    return jax.nn.silu(x)

def _sigmoid(x):
    return jax.nn.sigmoid(x)

def _layernorm(x, axis=-1, eps=1e-05):
    m = jnp.mean(x, axis=axis, keepdims=True)
    v = jnp.var(x, axis=axis, keepdims=True)
    return (x - m) / jnp.sqrt(v + eps)

def _scatter_add(tgt, idx, src, axis=0):
    return tgt.at[idx].add(src)

def _segment_sum(src, seg, n):
    return jax.ops.segment_sum(src, seg, n)
kernel_name = 'mk_gnn_resnorm_d4_gnn_r64_20ba9a'

def setup_inputs(seed: int=0):
    np.random.seed(seed)
    _w = jnp.asarray

    def _rec_inputs():
        import jax
        import jax.numpy as jnp
        _gk = jax.random.key(seed)
        x = -0.000202 + 1 * jax.random.normal(jax.random.fold_in(_gk, 1), (50000, 128), jnp.float32)
        src = jax.random.randint(jax.random.fold_in(_gk, 2), (25000,), 0, 50000, jnp.int32)
        dst = jnp.minimum((50000 * jax.random.uniform(jax.random.fold_in(_gk, 3), (25000,)) ** 2.0).astype(jnp.int32), 49999)
        _o = jnp.argsort(dst, stable=True)
        src = src[_o]
        dst = dst[_o]
        edge_attr_50 = jax.random.uniform(jax.random.fold_in(_gk, 13), (25000, 50), jnp.float32, 0.0, 1)
        edge_weight = jax.random.uniform(jax.random.fold_in(_gk, 15), (25000,), jnp.float32, 0.0, 0.999999)
        return (x, src, dst, edge_attr_50, edge_weight)
    x, src, dst, edge_attr_50, edge_weight = _rec_inputs()

    def _L0_gnn_setup():
        import jax, jax.numpy as jnp
        import numpy as np
        N_NODES = 50000
        N_EDGES = 9375
        D = 128
        EPS = 1e-05

        def layer_norm(x, gamma, beta):
            mu = jnp.mean(x, axis=-1, keepdims=True)
            var = jnp.mean(jnp.square(x - mu), axis=-1, keepdims=True)
            return (x - mu) * jax.lax.rsqrt(var + EPS) * gamma + beta
        key = jax.random.key(seed)
        ks = jax.random.split(key, 12)
        s = 1.0 / np.sqrt(D)
        return {'h': jax.random.normal(ks[0], (N_NODES, D), dtype=jnp.float32), 'src': jax.random.randint(ks[1], (N_EDGES,), 0, N_NODES), 'dst': jax.random.randint(ks[2], (N_EDGES,), 0, N_NODES), 'W_pre': jax.random.uniform(ks[3], (D, D), jnp.float32, -s, s), 'b_pre': jax.random.uniform(ks[4], (D,), jnp.float32, -s, s), 'W1': jax.random.uniform(ks[5], (D, D), jnp.float32, -s, s), 'b1': jax.random.uniform(ks[6], (D,), jnp.float32, -s, s), 'W2': jax.random.uniform(ks[7], (D, D), jnp.float32, -s, s), 'b2': jax.random.uniform(ks[8], (D,), jnp.float32, -s, s), 'gamma': jnp.ones((D,), jnp.float32), 'beta': jnp.zeros((D,), jnp.float32)}
    _L0_gnn_all = _L0_gnn_setup()
    _L0_gnn_in = {k: v for k, v in _L0_gnn_all.items() if k in ('W_pre', 'b_pre', 'W1', 'b1', 'W2', 'b2', 'gamma', 'beta')}
    del _L0_gnn_all

    def _L1_gnn_setup():
        import jax, jax.numpy as jnp
        import numpy as np
        N_NODES = 100000
        N_EDGES = 25000
        D_IN = 128
        D_OUT = 128
        BN_EPS = 1e-05
        key = jax.random.key(seed)
        ks = jax.random.split(key, 6)
        x = jax.random.normal(ks[0], (N_NODES, D_IN), dtype=jnp.float32)
        edge_index = jax.random.randint(ks[1], (2, N_EDGES), 0, N_NODES, dtype=jnp.int32)
        edge_weight = jax.random.uniform(ks[2], (N_EDGES,), dtype=jnp.float32)
        W = jax.random.normal(ks[3], (D_IN, D_OUT), dtype=jnp.float32) / np.sqrt(D_IN)
        b = jax.random.normal(ks[4], (D_OUT,), dtype=jnp.float32) * 0.01
        gamma = jnp.ones((D_OUT,), dtype=jnp.float32)
        beta = jnp.zeros((D_OUT,), dtype=jnp.float32)
        return {'x': x, 'edge_index': edge_index, 'edge_weight': edge_weight, 'W': W, 'b': b, 'gamma': gamma, 'beta': beta}
    _L1_gnn_all = _L1_gnn_setup()
    _L1_gnn_in = {k: v for k, v in _L1_gnn_all.items() if k in ('W', 'b', 'gamma', 'beta')}
    del _L1_gnn_all

    def _L2_gnn_setup():
        import jax, jax.numpy as jnp
        import numpy as np
        N = 50000
        E = 12500
        D_NODE = 128
        D_MSG = 64
        R = 50
        H = 4
        C = D_MSG // H

        def _segment_softmax(alpha, seg, num_segments):
            amax = jax.ops.segment_max(alpha, seg, num_segments=num_segments)
            amax = jnp.where(jnp.isfinite(amax), amax, 0.0)
            ex = jnp.exp(alpha - amax[seg])
            den = jax.ops.segment_sum(ex, seg, num_segments=num_segments)
            return ex / den[seg]
        key = jax.random.key(seed)
        ks = jax.random.split(key, 16)
        s = 0.05
        inp = {'x': jax.random.normal(ks[0], (N, D_NODE), dtype=jnp.float32), 'edge_attr': jax.random.uniform(ks[1], (E, R), dtype=jnp.float32), 'edge_index': jax.random.randint(ks[2], (2, E), 0, N, dtype=jnp.int64), 'batch': jnp.zeros((N,), dtype=jnp.int64), 'W_n2m': jax.random.normal(ks[3], (D_NODE, D_MSG), dtype=jnp.float32) * s, 'W_edge': jax.random.normal(ks[4], (R, D_MSG), dtype=jnp.float32) * s, 'W_q': jax.random.normal(ks[5], (D_MSG, D_MSG), dtype=jnp.float32) * s, 'b_q': jnp.zeros((D_MSG,), dtype=jnp.float32), 'W_k': jax.random.normal(ks[6], (D_MSG, D_MSG), dtype=jnp.float32) * s, 'b_k': jnp.zeros((D_MSG,), dtype=jnp.float32), 'W_v': jax.random.normal(ks[7], (D_MSG, D_MSG), dtype=jnp.float32) * s, 'b_v': jnp.zeros((D_MSG,), dtype=jnp.float32), 'W_e': jax.random.normal(ks[8], (D_MSG, D_MSG), dtype=jnp.float32) * s, 'W_skip': jax.random.normal(ks[9], (D_MSG, D_MSG), dtype=jnp.float32) * s, 'b_skip': jnp.zeros((D_MSG,), dtype=jnp.float32), 'W_beta': jax.random.normal(ks[10], (3 * D_MSG, 1), dtype=jnp.float32) * s, 'W_m2n': jax.random.normal(ks[11], (D_MSG, D_NODE), dtype=jnp.float32) * s}
        return inp
    _L2_gnn_all = _L2_gnn_setup()
    _L2_gnn_in = {k: v for k, v in _L2_gnn_all.items() if k in ('W_n2m', 'W_edge', 'W_q', 'b_q', 'W_k', 'b_k', 'W_v', 'b_v', 'W_e', 'W_skip', 'b_skip', 'W_beta', 'W_m2n')}
    del _L2_gnn_all

    def _L3_gnn_setup():
        import jax, jax.numpy as jnp
        import numpy as np
        N_NODES = 50000
        N_EDGES = 12500
        IN_DIM = 128
        HIDDEN = 128

        def _gcn_conv(x, W, b, src, dst, norm, n):
            h = x @ W
            msg = h[src] * norm[:, None]
            out = jax.ops.segment_sum(msg, dst, num_segments=n)
            return out + b
        key = jax.random.key(seed)
        ks = jax.random.split(key, 6)
        x = jax.random.normal(ks[0], (N_NODES, IN_DIM), dtype=jnp.float32)
        edge_index = jax.random.randint(ks[1], (2, N_EDGES), 0, N_NODES, dtype=jnp.int32)
        W1 = jax.random.normal(ks[2], (IN_DIM, HIDDEN), dtype=jnp.float32) * 0.05
        b1 = jnp.zeros((HIDDEN,), dtype=jnp.float32)
        W2 = jax.random.normal(ks[3], (HIDDEN, HIDDEN), dtype=jnp.float32) * 0.05
        b2 = jnp.zeros((HIDDEN,), dtype=jnp.float32)
        return {'x': x, 'edge_index': edge_index, 'W1': W1, 'b1': b1, 'W2': W2, 'b2': b2}
    _L3_gnn_all = _L3_gnn_setup()
    _L3_gnn_in = {k: v for k, v in _L3_gnn_all.items() if k in ('W1', 'b1', 'W2', 'b2')}
    del _L3_gnn_all
    return {'x': x, 'src': src, 'dst': dst, 'edge_attr_50': edge_attr_50, 'edge_weight': edge_weight, 'L0_gnn_W_pre': _L0_gnn_in['W_pre'], 'L0_gnn_b_pre': _L0_gnn_in['b_pre'], 'L0_gnn_W1': _L0_gnn_in['W1'], 'L0_gnn_b1': _L0_gnn_in['b1'], 'L0_gnn_W2': _L0_gnn_in['W2'], 'L0_gnn_b2': _L0_gnn_in['b2'], 'L0_gnn_gamma': _L0_gnn_in['gamma'], 'L0_gnn_beta': _L0_gnn_in['beta'], 'L1_gnn_W': _L1_gnn_in['W'], 'L1_gnn_b': _L1_gnn_in['b'], 'L1_gnn_gamma': _L1_gnn_in['gamma'], 'L1_gnn_beta': _L1_gnn_in['beta'], 'L2_gnn_W_n2m': _L2_gnn_in['W_n2m'], 'L2_gnn_W_edge': _L2_gnn_in['W_edge'], 'L2_gnn_W_q': _L2_gnn_in['W_q'], 'L2_gnn_b_q': _L2_gnn_in['b_q'], 'L2_gnn_W_k': _L2_gnn_in['W_k'], 'L2_gnn_b_k': _L2_gnn_in['b_k'], 'L2_gnn_W_v': _L2_gnn_in['W_v'], 'L2_gnn_b_v': _L2_gnn_in['b_v'], 'L2_gnn_W_e': _L2_gnn_in['W_e'], 'L2_gnn_W_skip': _L2_gnn_in['W_skip'], 'L2_gnn_b_skip': _L2_gnn_in['b_skip'], 'L2_gnn_W_beta': _L2_gnn_in['W_beta'], 'L2_gnn_W_m2n': _L2_gnn_in['W_m2n'], 'L3_gnn_W1': _L3_gnn_in['W1'], 'L3_gnn_b1': _L3_gnn_in['b1'], 'L3_gnn_W2': _L3_gnn_in['W2'], 'L3_gnn_b2': _L3_gnn_in['b2']}

def reference(x, src, dst, edge_attr_50, edge_weight, L0_gnn_W_pre, L0_gnn_b_pre, L0_gnn_W1, L0_gnn_b1, L0_gnn_W2, L0_gnn_b2, L0_gnn_gamma, L0_gnn_beta, L1_gnn_W, L1_gnn_b, L1_gnn_gamma, L1_gnn_beta, L2_gnn_W_n2m, L2_gnn_W_edge, L2_gnn_W_q, L2_gnn_b_q, L2_gnn_W_k, L2_gnn_b_k, L2_gnn_W_v, L2_gnn_b_v, L2_gnn_W_e, L2_gnn_W_skip, L2_gnn_b_skip, L2_gnn_W_beta, L2_gnn_W_m2n, L3_gnn_W1, L3_gnn_b1, L3_gnn_W2, L3_gnn_b2):
    import jax
    import jax.numpy as jnp

    def _L0_gnn_ref(h, src, dst, W_pre, b_pre, W1, b1, W2, b2, gamma, beta):
        import jax, jax.numpy as jnp
        import numpy as np
        N_NODES = 50000
        N_EDGES = 9375
        D = 128
        EPS = 1e-05

        def layer_norm(x, gamma, beta):
            mu = jnp.mean(x, axis=-1, keepdims=True)
            var = jnp.mean(jnp.square(x - mu), axis=-1, keepdims=True)
            return (x - mu) * jax.lax.rsqrt(var + EPS) * gamma + beta
        h = h @ W_pre + b_pre
        agg = jax.ops.segment_sum(h[src], dst, num_segments=N_NODES)
        h_new = jax.nn.relu(jax.nn.relu(agg @ W1 + b1) @ W2 + b2)
        return layer_norm(h + h_new, gamma, beta)

    def _L1_gnn_ref(x, edge_index, edge_weight, W, b, gamma, beta):
        import jax, jax.numpy as jnp
        import numpy as np
        N_NODES = 100000
        N_EDGES = 25000
        D_IN = 128
        D_OUT = 128
        BN_EPS = 1e-05
        n = x.shape[0]
        self_loops = jnp.arange(n, dtype=edge_index.dtype)
        row = jnp.concatenate([edge_index[0], self_loops])
        col = jnp.concatenate([edge_index[1], self_loops])
        ew = jnp.concatenate([edge_weight, jnp.ones((n,), x.dtype)])
        deg = jax.ops.segment_sum(jnp.ones_like(ew), row, num_segments=n)
        dinv = jnp.where(deg > 0, jax.lax.rsqrt(deg), 0.0)
        norm = dinv[row] * dinv[col] * ew
        h = x @ W + b
        msgs = norm[:, None] * h[row]
        out = jax.ops.segment_sum(msgs, col, num_segments=n)
        mean = jnp.mean(out, axis=0)
        var = jnp.mean(jnp.square(out - mean), axis=0)
        out = (out - mean) * jax.lax.rsqrt(var + BN_EPS) * gamma + beta
        return jax.nn.relu(out)

    def _L2_gnn_ref(x, edge_attr, edge_index, batch, W_n2m, W_edge, W_q, b_q, W_k, b_k, W_v, b_v, W_e, W_skip, b_skip, W_beta, W_m2n):
        import jax, jax.numpy as jnp
        import numpy as np
        N = 50000
        E = 12500
        D_NODE = 128
        D_MSG = 64
        R = 50
        H = 4
        C = D_MSG // H

        def _segment_softmax(alpha, seg, num_segments):
            amax = jax.ops.segment_max(alpha, seg, num_segments=num_segments)
            amax = jnp.where(jnp.isfinite(amax), amax, 0.0)
            ex = jnp.exp(alpha - amax[seg])
            den = jax.ops.segment_sum(ex, seg, num_segments=num_segments)
            return ex / den[seg]
        src, dst = (edge_index[0], edge_index[1])
        n = x.shape[0]
        xm = x @ W_n2m
        e = edge_attr @ W_edge
        q = (xm @ W_q + b_q).reshape(n, H, C)
        k = (xm @ W_k + b_k).reshape(n, H, C)
        v = (xm @ W_v + b_v).reshape(n, H, C)
        ee = (e @ W_e).reshape(-1, H, C)
        k_e = k[src] + ee
        alpha = jnp.sum(q[dst] * k_e, axis=-1) / jnp.sqrt(jnp.float32(C))
        alpha = _segment_softmax(alpha, dst, n)
        msg = (v[src] + ee) * alpha[..., None]
        out = jax.ops.segment_sum(msg, dst, num_segments=n).reshape(n, H * C)
        x_r = xm @ W_skip + b_skip
        beta = jax.nn.sigmoid(jnp.concatenate([out, x_r, out - x_r], axis=-1) @ W_beta)
        out = beta * x_r + (1.0 - beta) * out
        return out @ W_m2n

    def _L3_gnn_ref(x, edge_index, W1, b1, W2, b2):
        import jax, jax.numpy as jnp
        import numpy as np
        N_NODES = 50000
        N_EDGES = 12500
        IN_DIM = 128
        HIDDEN = 128

        def _gcn_conv(x, W, b, src, dst, norm, n):
            h = x @ W
            msg = h[src] * norm[:, None]
            out = jax.ops.segment_sum(msg, dst, num_segments=n)
            return out + b
        n = x.shape[0]
        loops = jnp.arange(n, dtype=edge_index.dtype)
        src = jnp.concatenate([edge_index[0], loops])
        dst = jnp.concatenate([edge_index[1], loops])
        deg = jax.ops.segment_sum(jnp.ones(src.shape, dtype=x.dtype), dst, num_segments=n)
        dinv = jax.lax.rsqrt(deg)
        norm = dinv[src] * dinv[dst]
        h = jax.nn.relu(_gcn_conv(x, W1, b1, src, dst, norm, n))
        return _gcn_conv(h, W2, b2, src, dst, norm, n)
    edge_index = jnp.stack([src, dst])
    batch0 = jnp.zeros((50000,), jnp.int32)
    x = _layernorm(x + _L0_gnn_ref(x, src, dst, L0_gnn_W_pre, L0_gnn_b_pre, L0_gnn_W1, L0_gnn_b1, L0_gnn_W2, L0_gnn_b2, L0_gnn_gamma, L0_gnn_beta), axis=-1)
    x = _layernorm(x + _L1_gnn_ref(x, edge_index, edge_weight, L1_gnn_W, L1_gnn_b, L1_gnn_gamma, L1_gnn_beta), axis=-1)
    x = _layernorm(x + _L2_gnn_ref(x, edge_attr_50, edge_index, batch0, L2_gnn_W_n2m, L2_gnn_W_edge, L2_gnn_W_q, L2_gnn_b_q, L2_gnn_W_k, L2_gnn_b_k, L2_gnn_W_v, L2_gnn_b_v, L2_gnn_W_e, L2_gnn_W_skip, L2_gnn_b_skip, L2_gnn_W_beta, L2_gnn_W_m2n), axis=-1)
    x = _layernorm(x + _L3_gnn_ref(x, edge_index, L3_gnn_W1, L3_gnn_b1, L3_gnn_W2, L3_gnn_b2), axis=-1)
    return x

_drawn_inputs = setup_inputs


def setup_inputs(seed=0):
    import zlib

    import numpy as np

    out = dict(_drawn_inputs(seed))
    spreads = {'L0_gnn_gamma': (1.0, 0.2),
     'L0_gnn_beta': (0.0, 0.1),
     'L1_gnn_gamma': (1.0, 0.2),
     'L1_gnn_beta': (0.0, 0.1),
     'L2_gnn_b_q': (0.0, 0.8),
     'L2_gnn_b_k': (0.0, 2.0),
     'L2_gnn_b_v': (0.0, 2.0),
     'L2_gnn_b_skip': (0.0, 0.336),
     'L3_gnn_b1': (0.0, 0.1),
     'L3_gnn_b2': (0.0, 0.1)}
    factors = {'edge_attr_50': 8.0,
     'L0_gnn_b1': 3.749,
     'L1_gnn_b': 8.0,
     'L2_gnn_W_edge': 7.478,
     'L2_gnn_W_q': 8.0,
     'L2_gnn_W_k': 8.0,
     'L2_gnn_W_e': 6.292,
     'L2_gnn_W_beta': 8.0,
     'L2_gnn_W_v': 5.483}
    for name, (base, spread) in spreads.items():
        noise = np.random.default_rng([zlib.crc32(name.encode()), seed]).standard_normal(out[name].shape)
        drawn = base * np.exp(spread * noise) if base else spread * noise
        out[name] = jnp.asarray(drawn.astype(out[name].dtype))
    for name, factor in factors.items():
        out[name] = (out[name] * factor).astype(out[name].dtype)
    return out
```

```python
from contextlib import ExitStack

import concourse.bass as bass
from concourse import mybir
from concourse.alu_op_type import AluOpType as ALU

F32, BF16, I32 = mybir.dt.float32, mybir.dt.bfloat16, mybir.dt.int32
ACT = mybir.ActivationFunctionType

P = 128
N, E, D = 50000, 25000, 128
R, M, H = 50, 64, 4
C = M // H
EPS = 1e-5
G = 8
NB = -(-N // (P * G))
NPAD = NB * P * G
COLS = NB * G
LAST = N - (NB - 1) * P * G
LASTP = LAST // G
assert LAST % G == 0 and G == 8 and NPAD > N
ET = -(-E // P)
T = 4
EB = ET // T
EPAD = ET * P
assert ET % T == 0
W = T * P
EROW = 256
ER = EPAD // EROW
AHEAD = 2
FAR = float(1 << 17)
BIG = 1e30


class Batch:

    def __init__(self, i, unroll, c):
        self.i, self.unroll, self.c, self.n = i, unroll, c, i * unroll + c

    def slot(self, m):
        return self.c % m

    def turn(self, m):
        return self.i * (self.unroll // m) + self.c // m

    def is_last(self, n):
        return isinstance(self.n, int) and self.n == n - 1


def pipeline(eng, n, unroll, depth, body):
    head = unroll * (-(-(depth + 2) // unroll))
    rounds = (n - head) // unroll

    def peeled(s):
        return lambda k: Batch(0, unroll, s - k) if 0 <= s - k < n else None

    for s in range(head):
        body(peeled(s))
    with eng.Fori(0, rounds) as i:
        for u in range(unroll):
            body(lambda k, u=u: Batch(i, unroll, head + u - k))
    for s in range(head + unroll * rounds, n + depth):
        body(peeled(s))


def after(eng, sem, b, lag=0, per=1, n=None):
    value = per * (b.n + 1 - lag)
    if isinstance(value, int):
        if value <= 0:
            return
        value = value if n is None else min(value, per * n)
    eng.wait_ge(sem, value)


def landed(eng, sems, b, per):
    eng.wait_ge(sems[b.slot(len(sems))], per * (b.turn(len(sems)) + 1))


def freed(eng, sems, b, per):
    value = per * b.turn(len(sems))
    if not (isinstance(value, int) and value == 0):
        eng.wait_ge(sems[b.slot(len(sems))], value)


def all_landed(eng, sems, n, per):
    for s in range(len(sems)):
        eng.wait_ge(sems[s], per * ((n + len(sems) - 1 - s) // len(sems)))


class Steps:

    def __init__(self, eng, sem, per):
        self.eng, self.sem, self.per = eng, sem, per

    def start(self, batch):
        self.batch, self.k = batch, 0

    def made(self, instruction):
        instruction.then_inc(self.sem, 1)
        self.k += 1
        self.eng.wait_ge(self.sem, self.batch * self.per + self.k)

    def end(self):
        assert self.k == self.per, (self.k, self.per)


def pass_semaphores(nc, ctx, prefix):
    made = []

    def sem(name):
        made.append(nc.alloc_semaphore(prefix + name))
        return made[-1]

    def clear():
        nc.clear_and_free_semaphores(made)
        nc.all_engine_barrier()

    ctx.callback(clear)
    return sem


def carry(eng, sem):
    eng.sem_inc(sem, 1)


def over_tiles(row, tiles=G):
    return row.unsqueeze(1).broadcast_to([P, tiles, row.shape[-1]])


def over_width(cols, width=D):
    return cols.unsqueeze(2).broadcast_to([P, cols.shape[-1], width])


def table_rows(table, batch, width=D):
    return table[bass.ds(batch * (P * G), P * G), :].rearrange("(p k) d -> p (k d)", p=P)


def flat(tile):
    return tile.rearrange("p k d -> p (k d)")


def node_stats(dve, steps, z, stats, sums, diff):
    for t in range(G):
        last = dve.bn_stats(stats[:, t, :], z[:, t, :])
    steps.made(last)
    dve.tensor_tensor(sums, stats[:, :, 1:3], stats[:, :, 4:6], ALU.add)
    steps.made(dve.tensor_tensor(diff, stats[:, :, 1], stats[:, :, 4], ALU.subtract))
    steps.made(dve.scalar_tensor_tensor(diff, diff, 0.25, diff, ALU.mult, ALU.mult))
    return dve.scalar_tensor_tensor(sums[:, :, 1], sums[:, :, 1], 1.0 / D, diff, ALU.mult, ALU.add)


def prepare(nc, k, a):
    with ExitStack() as ctx:
        sb = lambda name, shape, dt=F32: ctx.enter_context(nc.sbuf_tensor(name, shape, dt))
        ps = lambda name, shape: ctx.enter_context(nc.psum_tensor(name, shape, F32))
        sem = pass_semaphores(nc, ctx, "")
        idx_loaded, w_loaded, zero_made, ident_made = sem("idx_loaded"), sem("w_loaded"), sem("zero_made"), sem("ident_made")
        rows_made, turned, cols_made = sem("rows_made"), sem("turned"), sem("cols_made")
        keep_stored, keep_loaded, dve_steps = sem("keep_stored"), sem("keep_loaded"), sem("dve_steps")
        pool_steps, mul_ready, mul_done, const_made = sem("pool_steps"), sem("mul_ready"), sem("mul_done"), sem("const_made")
        wide_loaded = sem("wide_loaded")

        src_i = sb("src_i", [ER, EROW], I32)
        dst_i = sb("dst_i", [ER, EROW + 2], I32)
        part = sb("part", [ER, EROW], I32)
        part2 = sb("part2", [ER, EROW], I32)
        dst_f = sb("dst_f", [ER, EROW + 2])
        rows = sb("rows", [ER, 7, EROW])
        keep_r = sb("keep_r", [ER, EROW], BF16)
        ind = sb("ind", [P, COLS], I32)
        wn2m, wedge = sb("wn2m", [P, M]), sb("wedge", [R, M])
        wqkv = sb("wqkv", [M, 3, M])
        we, wskip = sb("we", [M, M]), sb("wskip", [M, M])
        wbeta = sb("wbeta", [M, 3])
        bskip_c = sb("bskip_c", [M, 1])
        n2m_t, edge_t, skip_t = sb("n2m_t", [M, P]), sb("edge_t", [M, R]), sb("skip_t", [M, M])
        rhs_v = sb("rhs_v", [M, 2 * M])
        rhs_e = sb("rhs_e", [M, 2 * M])
        rhs_r = sb("rhs_r", [M, M + 1])
        wdiff = sb("wdiff", [M, 1])
        wsum = sb("wsum", [M, 1])
        rb1 = sb("rb1", [P, 1])
        bias_hi, bias_mid = sb("bias_hi", [P, P], BF16), sb("bias_mid", [P, P], BF16)
        bias_a, bias_b = sb("bias_a", [P, P]), sb("bias_b", [P, P])
        lhs = sb("lhs", [P, 3, P])
        bank = [ps(f"turn_{i}", [P, 512]) for i in range(2)]
        mm = [ps(f"product_{i}", [P, 512]) for i in range(5)]
        block = ctx.enter_context(nc.Block())

        @block.sync
        def _(sp):
            ext = a["dst_ext"]
            sp.dma_start(dst_i[:, 1:EROW + 1], ext[1:EPAD + 1].rearrange("(r c) -> r c", c=EROW)).then_inc(idx_loaded, 16)
            sp.dma_start(dst_i[:, 0:1], ext[0:EPAD].rearrange("(r c) -> r c", c=EROW)[:, 0:1],
                         allow_slow_non_contiguous=True).then_inc(idx_loaded, 16)
            sp.dma_start(dst_i[:, EROW + 1:EROW + 2], ext[2:EPAD + 2].rearrange("(r c) -> r c", c=EROW)[:, EROW - 1:EROW],
                         allow_slow_non_contiguous=True).then_inc(idx_loaded, 16)
            sp.dma_start(src_i[:], a["src"].rearrange("(r c) -> r c", c=EROW)).then_inc(idx_loaded, 16)
            sp.dma_start(rows[:, 3, :], a["edge_weight"].rearrange("(r c) -> r c", c=EROW)).then_inc(idx_loaded, 16)
            sp.wait_ge(zero_made, 1)
            for s in range(0, NB, 7):
                sp.dma_start(k["agg"][s * P * G:(s + 7) * P * G, :].rearrange("(b p k) d -> p b (k d)", p=P, k=G),
                             k["zero"][:].unsqueeze(1).broadcast_to([P, 7, G * D])).then_inc(k["agg_zeroed"], 16)
            sp.wait_ge(rows_made, 1)
            sp.dma_start(k["keep_dram"].rearrange("(r c) -> r c", c=EROW), keep_r[:]).then_inc(keep_stored, 16)
            sp.wait_ge(keep_stored, 16)
            sp.dma_start(k["keep"][:], k["keep_dram"].partition_broadcast(P)).then_inc(keep_loaded, 16)
            sp.wait_ge(keep_loaded, 16)
            for s in range(0, NB, 7):
                sp.dma_start(k["agg_m"][s * P * G:(s + 7) * P * G, :].rearrange("(b p k) d -> p b (k d)", p=P, k=G),
                             k["zero"][:, 0:G * M].unsqueeze(1).broadcast_to([P, 7, G * M])).then_inc(k["agg_m_zeroed"], 16)

        weights = [(k["w_pre"], a["L0_gnn_W_pre"]), (k["w1"], a["L0_gnn_W1"]), (k["w2"], a["L0_gnn_W2"]), (k["w_l1"], a["L1_gnn_W"]),
                   (k["w_m2n"][0:M, :], a["L2_gnn_W_m2n"]), (k["w_m2n"][M:2 * M, :], a["L2_gnn_W_m2n"]), (k["w1_l3"], a["L3_gnn_W1"]), (k["w2_l3"], a["L3_gnn_W2"]),
                   (wn2m, a["L2_gnn_W_n2m"]), (wedge, a["L2_gnn_W_edge"]), (we, a["L2_gnn_W_e"]), (wskip, a["L2_gnn_W_skip"]),
                   (wqkv[:, 0, :], a["L2_gnn_W_q"]), (wqkv[:, 1, :], a["L2_gnn_W_v"]), (wqkv[:, 2, :], a["L2_gnn_W_k"]),
                   (wbeta, a["L2_gnn_W_beta"].rearrange("(j m) o -> m (j o)", m=M))]
        columns = [(k["b_pre_c"], a["L0_gnn_b_pre"]), (k["b1_c"], a["L0_gnn_b1"]), (k["gamma1_c"], a["L1_gnn_gamma"]),
                   (k["beta1_c"], a["L1_gnn_beta"]), (bskip_c, a["L2_gnn_b_skip"])]
        wide = [(k["b2_r"], a["L0_gnn_b2"]), (k["gamma0_r"], a["L0_gnn_gamma"]), (k["beta0_r"], a["L0_gnn_beta"]), (k["b_pre_r"], a["L0_gnn_b_pre"]),
                (k["b_l1_r"], a["L1_gnn_b"]), (k["b1_l3_r"], a["L3_gnn_b1"]), (k["b2_l3_r"], a["L3_gnn_b2"])]
        n_weights = len(weights) + len(columns) + 1 + 2

        @block.scalar
        def _(act):
            with nc.allow_non_contiguous_dma(reason="vectors of a few hundred bytes, once"):
                for tile, source in weights:
                    act.dma_start(tile if isinstance(tile, bass.AP) else tile[:], source).then_inc(w_loaded, 16)
                for tile, source in columns:
                    act.dma_start(tile[:], source.unsqueeze(1)).then_inc(w_loaded, 16)
                act.wait_ge(const_made, 1)
                act.dma_start(k["b_q"][M:2 * M, :], a["L2_gnn_b_q"].unsqueeze(1)).then_inc(w_loaded, 16)
                act.dma_start(k["w_ev"][R:R + 1, 0:M], a["L2_gnn_b_v"].unsqueeze(0)).then_inc(w_loaded, 16)
                act.dma_start(k["w_ev"][R:R + 1, M:2 * M], a["L2_gnn_b_k"].unsqueeze(0)).then_inc(w_loaded, 16)
                for tile, source in wide:
                    act.dma_start(tile[:], source.partition_broadcast(P)).then_inc(wide_loaded, 16)
            act.wait_ge(w_loaded, 16 * n_weights)
            act.wait_ge(wide_loaded, 16 * len(wide))

        @block.gpsimd
        def _(pool):
            pool.memset(k["zero"][:], 0.0).then_inc(zero_made, 1)
            pool.memset(k["ident"][:], 0.0).then_inc(pool_steps, 1)
            pool.wait_ge(pool_steps, 1)
            pool.affine_select(out=k["ident"][:], in_=k["ident"][:], compare_op=ALU.not_equal, fill=1.0, base=0,
                               pattern=[[-1, P]], channel_multiplier=1).then_inc(ident_made, 1)
            pool.iota(ind[:], pattern=[[1, COLS]], base=0, channel_multiplier=0).then_inc(ident_made, 1)
            pool.memset(k["head_sum"][:], 1.0).then_inc(pool_steps, 1)
            pool.wait_ge(pool_steps, 2)
            pool.affine_select(out=k["head_sum"][:], in_=k["head_sum"][:], compare_op=ALU.is_ge, fill=0.0, base=-M,
                               pattern=[[-C, H]], channel_multiplier=1).then_inc(pool_steps, 1)
            pool.wait_ge(pool_steps, 3)
            pool.affine_select(out=k["head_sum"][:], in_=k["head_sum"][:], compare_op=ALU.is_ge, fill=0.0, base=M + C - 1,
                               pattern=[[C, H]], channel_multiplier=-1).then_inc(ident_made, 1)
            pool.memset(k["head_spread"][:], 1.0).then_inc(pool_steps, 1)
            pool.wait_ge(pool_steps, 4)
            pool.affine_select(out=k["head_spread"][:], in_=k["head_spread"][:], compare_op=ALU.is_ge, fill=0.0, base=0,
                               pattern=[[1, M]], channel_multiplier=-C).then_inc(pool_steps, 1)
            pool.wait_ge(pool_steps, 5)
            pool.affine_select(out=k["head_spread"][:], in_=k["head_spread"][:], compare_op=ALU.is_ge, fill=0.0, base=C - 1,
                               pattern=[[-1, M]], channel_multiplier=C).then_inc(ident_made, 1)
            pool.memset(k["valid"][:], 1.0).then_inc(pool_steps, 1)
            pool.wait_ge(pool_steps, 6)
            pool.affine_select(out=k["valid"][:, COLS - G:COLS], in_=k["valid"][:, COLS - G:COLS], compare_op=ALU.is_ge, fill=0.0,
                               base=LAST - 1, pattern=[[-1, G]], channel_multiplier=-G).then_inc(ident_made, 1)

        def bias_parts(dve, steps, out, row):
            w = row.shape[-1]
            steps.made(dve.tensor_copy(bias_hi[:, 0:w], row))
            steps.made(dve.tensor_tensor(bias_a[:, 0:w], row, bias_hi[:, 0:w], ALU.subtract))
            steps.made(dve.tensor_copy(bias_mid[:, 0:w], bias_a[:, 0:w]))
            steps.made(dve.tensor_tensor(bias_a[:, 0:w], bias_a[:, 0:w], bias_mid[:, 0:w], ALU.subtract))
            steps.made(dve.tensor_scalar(bias_b[:, 0:w], bias_hi[:, 0:w], k["ident"][:, 0:1], None, ALU.mult))
            steps.made(dve.scalar_tensor_tensor(bias_b[:, 0:w], bias_mid[:, 0:w], k["ident"][:, 1:2], bias_b[:, 0:w], ALU.mult, ALU.add))
            steps.made(dve.scalar_tensor_tensor(out, over_tiles(bias_a[:, 0:w], 4), k["ident"][:, 2:3], over_tiles(bias_b[:, 0:w], 4),
                                                ALU.mult, ALU.add))

        tables = [k["src_lo"], k["src_hi"], k["src_c"], k["weight_c"], k["dst_lo"], k["dst_hi"], k["last_c"]]

        @block.vector
        def _(dve):
            steps = Steps(dve, dve_steps, 0)
            steps.start(0)
            for tile in (k["b_q"], k["w_ev"], k["w_q"]):
                last = dve.memset(tile[:], 0.0)
            last.then_inc(const_made, 1)
            dve.memset(k["eps"][:], EPS)
            dve.memset(k["ones_b"][:], 1.0)
            dve.wait_ge(idx_loaded, 16 * 5)
            for at, ids in ((0, src_i[:]), (4, dst_i[:, 1:EROW + 1])):
                steps.made(dve.tensor_scalar(part[:], ids, 3, P - 1, ALU.logical_shift_right, ALU.bitwise_and))
                steps.made(dve.tensor_copy(rows[:, at, :], part[:]))
                steps.made(dve.tensor_scalar(part[:], ids, 10, 3, ALU.logical_shift_right, ALU.logical_shift_left))
                steps.made(dve.tensor_scalar(part2[:], ids, G - 1, None, ALU.bitwise_and))
                steps.made(dve.tensor_tensor(part[:], part[:], part2[:], ALU.bitwise_or))
                steps.made(dve.tensor_copy(rows[:, at + 1, :], part[:]))
            dve.tensor_scalar(rows[:, 2, :], src_i[:], float(N - 1), None, ALU.min)
            steps.made(dve.tensor_copy(dst_f[:], dst_i[:]))
            dve.tensor_tensor(keep_r[:], dst_f[:, 1:EROW + 1], dst_f[:, 0:EROW], ALU.is_equal).then_inc(rows_made, 1)
            steps.made(dve.tensor_tensor(rows[:, 6, :], dst_f[:, 1:EROW + 1], dst_f[:, 2:EROW + 2], ALU.is_equal))
            dve.scalar_tensor_tensor(rows[:, 6, :], rows[:, 6, :], FAR, dst_f[:, 1:EROW + 1], ALU.mult, ALU.add).then_inc(rows_made, 1)
            dve.wait_ge(ident_made, 5)
            dve.tensor_copy(k["count_iota"][:], ind[:])
            for n, table in enumerate(tables + [k["dst_c"]]):
                dve.wait_ge(turned, n + 1)
                both = bank[n % 2][:, 0:2 * ER].rearrange("p (h r) -> p r h", h=2)
                dve.tensor_copy(table[:].rearrange("p (r h) -> p r h", h=2), both).then_inc(cols_made, 1)
            dve.wait_ge(cols_made, 8)
            dve.tensor_copy(k["gather_i"][:], k["src_c"][:])
            dve.tensor_copy(k["scatter_i"][:], k["last_c"][:])
            dve.tensor_copy(k["dst_i"][:], k["dst_c"][:])
            dve.wait_ge(w_loaded, 16 * n_weights)
            dve.wait_ge(wide_loaded, 16 * len(wide))
            dve.tensor_tensor(wdiff[:], wbeta[:, 1:2], wbeta[:, 2:3], ALU.subtract)
            dve.tensor_tensor(wsum[:], wbeta[:, 0:1], wbeta[:, 2:3], ALU.add)
            dve.tensor_copy(rhs_v[:], wqkv[:, 1:3, :].rearrange("p a b -> p (a b)"))
            dve.tensor_copy(rhs_e[:, 0:M], we[:])
            dve.tensor_copy(rhs_e[:, M:2 * M], we[:])
            dve.tensor_copy(rhs_r[:, 0:M], wskip[:])
            steps.made(dve.tensor_scalar(rb1[:], k["b1_c"][:], 0.0, None, ALU.max))
            dve.tensor_copy(lhs[:, 0, :], rb1[:].broadcast_to([P, P]))
            dve.tensor_copy(lhs[0:M, 1, :], bskip_c[:].broadcast_to([M, P]))
            dve.tensor_copy(lhs[0:M, 2, :], wsum[:].broadcast_to([M, P])).then_inc(mul_ready, 1)
            dve.wait_ge(mul_done, 1)
            dve.tensor_copy(n2m_t[:], mm[0][0:M, 0:P])
            dve.tensor_copy(edge_t[:], mm[1][0:M, 0:R])
            dve.tensor_copy(skip_t[:], mm[2][0:M, 0:M]).then_inc(mul_ready, 1)
            dve.wait_ge(mul_done, 2)
            dve.tensor_copy(rhs_r[:, M:M + 1], mm[3][0:M, 0:1]).then_inc(mul_ready, 1)
            dve.wait_ge(mul_done, 3)
            dve.tensor_scalar(k["w_q"][:, M:2 * M], mm[0][:, 0:M], float(C) ** -0.5, None, ALU.mult)
            dve.tensor_copy(k["w_vk"][:], mm[1][:, 0:2 * M])
            dve.tensor_copy(k["w_ev"][0:R, :], mm[2][0:R, 0:2 * M])
            dve.tensor_copy(k["w_r"][:], mm[3][:, 0:M + 1])
            dve.tensor_copy(k["b_r"][:], mm[4][:, 0:M + 1])
            dve.tensor_copy(k["w_out"][:], mm[4][:, 128:128 + M])
            steps.made(dve.tensor_tensor(k["none0_r"][:], mm[4][:, 256:256 + D], k["b2_r"][:], ALU.add))
            steps.made(dve.tensor_scalar(k["none0_r"][:], k["none0_r"][:], 0.0, None, ALU.max))
            steps.made(dve.tensor_tensor(k["b_pre_r"][:], k["b_pre_r"][:], k["none0_r"][:], ALU.add))
            dve.tensor_scalar(k["b_q"][:], k["b_q"][:], float(C) ** -0.5, None, ALU.mult)
            for out, row in ((k["bias_h"], k["b_pre_r"][:]), (k["bias_l1"], k["b_l1_r"][:]), (k["bias_r"], k["b_r"][:])):
                bias_parts(dve, steps, out[:], row)

        @block.tensor
        def _(pe):
            pe.wait_ge(ident_made, 5)
            pe.wait_ge(rows_made, 2)
            sources = [rows[:, i, :] for i in range(7)] + [dst_f[:, 1:EROW + 1]]
            for n, source in enumerate(sources):
                if n >= 2:
                    pe.wait_ge(cols_made, n - 1)
                for h in range(2):
                    last = pe.transpose(bank[n % 2][:, h * ER:(h + 1) * ER], source[:, h * P:(h + 1) * P],
                                        k["ident"][0:ER, 0:ER])
                last.then_inc(turned, 1)
            pe.wait_ge(mul_ready, 1)
            pe.transpose(mm[0][0:M, 0:P], wn2m[:], k["ident"][:])
            pe.transpose(mm[1][0:M, 0:R], wedge[:], k["ident"][0:R, 0:R])
            pe.transpose(mm[2][0:M, 0:M], wskip[:], k["ident"][0:M, 0:M]).then_inc(mul_done, 1)
            pe.wait_ge(mul_ready, 2)
            pe.matmul(mm[3][0:M, 0:1], skip_t[:], wdiff[:], start=True, stop=True).then_inc(mul_done, 1)
            pe.wait_ge(mul_ready, 3)
            pe.matmul(mm[0][:, 0:M], n2m_t[:], wqkv[:, 0, :], start=True, stop=True)
            pe.matmul(mm[1][:, 0:2 * M], n2m_t[:], rhs_v[:], start=True, stop=True)
            pe.matmul(mm[2][0:R, 0:2 * M], edge_t[:], rhs_e[:], start=True, stop=True)
            pe.matmul(mm[3][:, 0:M + 1], n2m_t[:], rhs_r[:], start=True, stop=True)
            pe.matmul(mm[4][:, 0:M], lhs[0:M, 1, :], k["ident"][0:M, 0:M], start=True, stop=True)
            pe.matmul(mm[4][:, M:M + 1], lhs[0:M, 1, :], wdiff[:], start=True, stop=True)
            pe.matmul(mm[4][:, 128:128 + M], lhs[0:M, 2, :], k["ident"][0:M, 0:M], start=True, stop=True)
            pe.matmul(mm[4][:, 256:256 + D], lhs[:, 0, :], k["w2"][:], start=True, stop=True).then_inc(mul_done, 1)


def scatter_rows(pool, table, rows, indices, landed):
    for t in range(T):
        pool.indirect_dma_start(table, bass.IndirectOffsetOnAxis(indices[:, t:t + 1], 0), rows[:, t, :], None,
                                bounds_check=NPAD - 1, oob_is_err=False).then_inc(landed, 16)


def gather_rows(pool, rows, table, indices, landed):
    for t in range(T):
        pool.indirect_dma_start(rows[:, t, :], None, table,
                                bass.IndirectOffsetOnAxis(indices[:, t:t + 1], 0)).then_inc(landed, 16)


def edges_layer0(nc, k, a):
    with ExitStack() as ctx:
        sb = lambda name, shape, dt=F32: ctx.enter_context(nc.sbuf_tensor(name, shape, dt))
        ps = lambda name, shape: ctx.enter_context(nc.psum_tensor(name, shape, F32))
        sem = pass_semaphores(nc, ctx, "")
        index_ready, sindex_ready, turned, xt_ready, h_done, h_ready = map(sem, ("e0_index", "e0_sindex", "e0_turned", "e0_xt", "e0_h_done", "e0_h"))
        summed, r_done, r_ready, out_done, out_ready = map(sem, ("e0_summed", "e0_r_done", "e0_r", "e0_out_done", "e0_out"))
        hot_ready, hot_used, out_steps, degree_steps, counted, const = map(sem, ("e0_hot", "e0_hot_used", "e0_out_steps", "e0_degree_steps", "e0_counted", "e0_const"))
        deg_ready, deg_root = sem("e0_deg"), sem("e0_root")
        gathered = [sem(f"e0_gathered{i}") for i in range(2)]
        scattered = [sem(f"e0_scattered{i}") for i in range(2)]
        issued = sem("issued")
        gi, si = sb("gi", [P, 2, T], I32), sb("si", [P, 2, T], I32)
        rows = sb("rows0", [P, 2, T, D])
        xt, hs, agg, r1, out = (sb(x, [P, 2, W]) for x in ("xt", "hs", "aggs", "r1", "e0_rows_out"))
        lo = sb("lo", [P, 2, 2 * T, P], BF16)
        hi = sb("hi", [P, 2, 2 * T, COLS], BF16)
        zero_b = sb("zero_b", [P, COLS], BF16)
        deg = sb("deg", [P, 3, COLS])
        p_t, p_h, p_r, p_o = (ps(x, [P, W]) for x in ("p_t", "p_h", "p_r", "p_o"))
        p_count = [ps("p_count_src", [P, 512]), ps("p_count_dst", [P, 512])]
        block = ctx.enter_context(nc.Block())
        DEPTH = 4

        @block.gpsimd
        def _(pool):
            pool.memset(agg[:, 1, W - 1:W], 0.0).then_inc(const, 1)
            pool.memset(zero_b[:], 0.0).then_inc(const, 1)

            def step(at):
                if b := at(1):
                    s = b.slot(2)
                    after(pool, index_ready, b)
                    after(pool, turned, b, lag=2)
                    carry(pool, issued)
                    gather_rows(pool, rows[:, s], a["x"], gi[:, s], gathered[s])
                if b := at(4):
                    s = b.slot(2)
                    after(pool, sindex_ready, b)
                    after(pool, out_ready, b)
                    pool.wait_ge(k["agg_zeroed"], 16 * (NB // 7))
                    carry(pool, issued)
                    scatter_rows(pool, k["agg"], out[:, s].rearrange("p (t d) -> p t d", t=T), si[:, s], scattered[s])
            pipeline(pool, EB, 2, DEPTH, step)
            all_landed(pool, scattered, EB, 16 * T)

        @block.tensor
        def _(pe):
            pe.wait_ge(const, 2)
            for c in range(2):
                pe.matmul(p_count[c][:, 0:COLS], zero_b[:, 0:P], zero_b[:], start=True, stop=False)

            def step(at):
                if b := at(3):
                    s = b.slot(2)
                    after(pe, summed, b)
                    after(pe, r_ready, b, lag=1)
                    pe.matmul(p_r[:], k["w1"][:], agg[:, s, :], start=True, stop=True).then_inc(r_done, 1)
                if b := at(2):
                    s = b.slot(2)
                    landed(pe, gathered, b, 16 * T)
                    after(pe, xt_ready, b, lag=1)
                    for t in range(T):
                        last = pe.transpose(p_t[:, t * P:(t + 1) * P], rows[:, s, t, :], k["ident"][:])
                    last.then_inc(turned, 1)
                if b := at(3):
                    s = b.slot(2)
                    after(pe, r_ready, b)
                    after(pe, out_ready, b, lag=1)
                    for t in range(T):
                        last = pe.matmul(p_o[:, t * P:(t + 1) * P], r1[:, s, t * P:(t + 1) * P], k["w2"][:], start=True, stop=True)
                    last.then_inc(out_done, 1)
                if b := at(2):
                    s = b.slot(2)
                    after(pe, xt_ready, b)
                    after(pe, h_ready, b, lag=1)
                    pe.matmul(p_h[:], k["w_pre"][:], xt[:, s, :], start=True, stop=True).then_inc(h_done, 1)
                if b := at(1):
                    s = b.slot(2)
                    after(pe, hot_ready, b)
                    for c in range(2):
                        for t in range(T):
                            last = pe.matmul(p_count[c][:, 0:COLS], lo[:, s, c * T + t, :], hi[:, s, c * T + t, :],
                                             start=False, stop=False)
                    last.then_inc(hot_used, 1)
            pipeline(pe, EB, 2, DEPTH, step)
            for c in range(2):
                last = pe.matmul(p_count[c][:, 0:COLS], zero_b[:, 0:P], zero_b[:], start=False, stop=True)
            last.then_inc(counted, 1)

        @block.scalar
        def _(act):
            def step(at):
                if b := at(2):
                    s = b.slot(2)
                    after(act, turned, b)
                    after(act, h_done, b, lag=2)
                    act.activation(xt[:, s, :], p_t[:], ACT.Copy).then_inc(xt_ready, 1)
                if b := at(3):
                    s = b.slot(2)
                    after(act, r_done, b)
                    after(act, out_done, b, lag=2)
                    act.activation(r1[:, s, :], p_r[:], ACT.Relu, bias=k["b1_c"][:]).then_inc(r_ready, 1)
                if b := at(2):
                    s = b.slot(2)
                    after(act, h_done, b)
                    after(act, summed, b, lag=2)
                    act.activation(hs[:, s, :], p_h[:], ACT.Identity, bias=k["b_pre_c"][:]).then_inc(h_ready, 1)
            pipeline(act, EB, 2, DEPTH, step)
            act.wait_ge(deg_ready, 1)
            act.activation(k["dinv_src"][:], deg[:, 0, :], ACT.Sqrt)
            act.activation(k["dinv_dst"][:], deg[:, 1, :], ACT.Sqrt).then_inc(deg_root, 1)

        @block.vector
        def _(dve):
            out_steps_ = Steps(dve, out_steps, 1)
            dve.wait_ge(const, 1)

            def step(at):
                if b := at(0):
                    s = b.slot(2)
                    freed(dve, gathered, b, 16 * T)
                    dve.tensor_copy(gi[:, s, :], k["gather_i"][:, bass.ds(b.n * T, T)]).then_inc(index_ready, 1)
                if b := at(3):
                    s = b.slot(2)
                    freed(dve, scattered, b, 16 * T)
                    dve.tensor_copy(si[:, s, :], k["scatter_i"][:, bass.ds(b.n * T, T)]).then_inc(sindex_ready, 1)
                if b := at(2):
                    s = b.slot(2)
                    after(dve, h_ready, b)
                    after(dve, r_done, b, lag=2)
                    after(dve, summed, b, lag=1)
                    dve.tensor_tensor_scan(agg[:, s, :], k["keep"][:, bass.ds(b.n * W, W)], hs[:, s, :],
                                           agg[:, 1 - s, W - 1:W], ALU.mult, ALU.add).then_inc(summed, 1)
                if b := at(3):
                    s = b.slot(2)
                    after(dve, out_done, b)
                    freed(dve, scattered, b, 16 * T)
                    out_steps_.start(b.n)
                    tiles = lambda x: x.rearrange("p (t d) -> p t d", t=T)
                    out_steps_.made(dve.tensor_tensor(tiles(out[:, s, :]), tiles(p_o[:]), over_tiles(k["b2_r"][:], T), ALU.add))
                    dve.scalar_tensor_tensor(tiles(out[:, s, :]), tiles(out[:, s, :]), 0.0, over_tiles(k["none0_r"][:], T),
                                             ALU.max, ALU.subtract).then_inc(out_ready, 1)
                if b := at(0):
                    s = b.slot(2)
                    after(dve, hot_used, b, lag=2)
                    for c, (table_lo, table_hi) in enumerate(((k["src_lo"], k["src_hi"]), (k["dst_lo"], k["dst_hi"]))):
                        for t in range(T):
                            dve.tensor_scalar(lo[:, s, c * T + t, :], k["count_iota"][:, 0:P], table_lo[:, bass.ds(b.n * T + t, 1)], None, ALU.is_equal)
                            last = dve.tensor_scalar(hi[:, s, c * T + t, :], k["count_iota"][:], table_hi[:, bass.ds(b.n * T + t, 1)], None, ALU.is_equal)
                    last.then_inc(hot_ready, 1)
            pipeline(dve, EB, 2, DEPTH, step)
            dve.wait_ge(counted, 1)
            dve.tensor_scalar(deg[:, 0, :], p_count[0][:, 0:COLS], 1.0, None, ALU.add)
            dve.tensor_scalar(deg[:, 1, :], p_count[1][:, 0:COLS], 1.0, None, ALU.add).then_inc(deg_ready, 1)
            dve.wait_ge(deg_root, 1)
            dve.reciprocal(k["dinv_src"][:], k["dinv_src"][:]).then_inc(degree_steps, 1)
            dve.reciprocal(k["dinv_dst"][:], k["dinv_dst"][:]).then_inc(degree_steps, 1)
            dve.wait_ge(degree_steps, 2)
            dve.tensor_tensor(k["sum_w"][:], k["dinv_src"][:], k["valid"][:], ALU.mult).then_inc(degree_steps, 1)
            dve.wait_ge(degree_steps, 3)
            dve.tensor_tensor(k["square_w"][:], k["sum_w"][:], k["sum_w"][:], ALU.mult)


def edges_sum(nc, k, name, source, weighted):
    with ExitStack() as ctx:
        sb = lambda n, shape, dt=F32: ctx.enter_context(nc.sbuf_tensor(name + n, shape, dt))
        ps = lambda n, shape: ctx.enter_context(nc.psum_tensor(name + n, shape, F32))
        sem = pass_semaphores(nc, ctx, name)
        index_ready, sindex_ready, scaled, turned, summed, back, out_ready, const = map(
            sem, ("index", "sindex", "scaled", "turned", "summed", "back", "out_ready", "const"))
        gathered = [sem(f"gathered{i}") for i in range(2)]
        scattered = [sem(f"scattered{i}") for i in range(2)]
        issued = sem("issued")
        gi, si = sb("gi", [P, 2, T], I32), sb("si", [P, 2, T], I32)
        rows = sb("rows", [P, 2, T, D])
        agg, out = sb("sums", [P, 2, W]), sb("out", [P, 2, W])
        p_t, p_o = [ps(f"p_t{i}", [P, W]) for i in range(2)], [ps(f"p_o{i}", [P, W]) for i in range(2)]
        block = ctx.enter_context(nc.Block())
        DEPTH = 4

        @block.gpsimd
        def _(pool):
            pool.memset(agg[:, 1, W - 1:W], 0.0).then_inc(const, 1)

            def step(at):
                if b := at(1):
                    s = b.slot(2)
                    after(pool, index_ready, b)
                    after(pool, turned, b, lag=2)
                    carry(pool, issued)
                    gather_rows(pool, rows[:, s], source, gi[:, s], gathered[s])
                if b := at(4):
                    s = b.slot(2)
                    after(pool, sindex_ready, b)
                    after(pool, out_ready, b)
                    carry(pool, issued)
                    scatter_rows(pool, k["agg"], out[:, s].rearrange("p (t d) -> p t d", t=T), si[:, s], scattered[s])
            pipeline(pool, EB, 2, DEPTH, step)
            all_landed(pool, scattered, EB, 16 * T)

        @block.tensor
        def _(pe):
            def step(at):
                if b := at(3):
                    s = b.slot(2)
                    after(pe, summed, b)
                    after(pe, out_ready, b, lag=2)
                    for t in range(T):
                        last = pe.transpose(p_o[s][:, t * P:(t + 1) * P], agg[:, s, t * P:(t + 1) * P], k["ident"][:])
                    last.then_inc(back, 1)
                if b := at(2):
                    s = b.slot(2)
                    if weighted:
                        after(pe, scaled, b)
                    else:
                        landed(pe, gathered, b, 16 * T)
                    after(pe, summed, b, lag=2)
                    for t in range(T):
                        last = pe.transpose(p_t[s][:, t * P:(t + 1) * P], rows[:, s, t, :], k["ident"][:])
                    last.then_inc(turned, 1)
            pipeline(pe, EB, 2, DEPTH, step)

        @block.scalar
        def _(act):
            def step(at):
                if b := at(3):
                    s = b.slot(2)
                    after(act, back, b)
                    freed(act, scattered, b, 16 * T)
                    act.activation(out[:, s, :], p_o[s][:], ACT.Copy).then_inc(out_ready, 1)
            pipeline(act, EB, 2, DEPTH, step)

        @block.vector
        def _(dve):
            dve.wait_ge(const, 1)

            def step(at):
                if b := at(0):
                    s = b.slot(2)
                    freed(dve, gathered, b, 16 * T)
                    dve.tensor_copy(gi[:, s, :], k["gather_i"][:, bass.ds(b.n * T, T)]).then_inc(index_ready, 1)
                if b := at(3):
                    s = b.slot(2)
                    freed(dve, scattered, b, 16 * T)
                    dve.tensor_copy(si[:, s, :], k["scatter_i"][:, bass.ds(b.n * T, T)]).then_inc(sindex_ready, 1)
                if b := at(2):
                    s = b.slot(2)
                    if weighted:
                        landed(dve, gathered, b, 16 * T)
                        dve.tensor_tensor(rows[:, s], rows[:, s], over_width(k["weight_c"][:, bass.ds(b.n * T, T)]),
                                          ALU.mult).then_inc(scaled, 1)
                    after(dve, turned, b)
                    after(dve, back, b, lag=2)
                    after(dve, summed, b, lag=1)
                    dve.tensor_tensor_scan(agg[:, s, :], k["keep"][:, bass.ds(b.n * W, W)], p_t[s][:],
                                           agg[:, 1 - s, W - 1:W], ALU.mult, ALU.add).then_inc(summed, 1)
            pipeline(dve, EB, 2, DEPTH, step)


def edges_attention(nc, k, a):
    with ExitStack() as ctx:
        sb = lambda n, shape, dt=F32: ctx.enter_context(nc.sbuf_tensor("at_" + n, shape, dt))
        ps = lambda n, shape: ctx.enter_context(nc.psum_tensor("at_" + n, shape, F32))
        sem = pass_semaphores(nc, ctx, "at_")
        (index_ready, sindex_ready, src_turned, dst_turned, src_ready, dst_ready, vk_done, vk_ready, q_done, product_ready,
         alpha_done, exp_in, exp_ready, spread, weighted, summed, den_summed, back, out_ready, const, max_steps, out_steps) = map(
            sem, ("index", "sindex", "src_turned", "dst_turned", "src_ready", "dst_ready", "vk_done", "vk_ready", "q_done",
                  "product", "alpha", "exp_in", "exp_ready", "spread", "weighted", "summed", "den_summed", "back", "out_ready",
                  "const", "max_steps", "out_steps"))
        U = 4
        gathered = [sem(f"gathered{i}") for i in range(2)]
        attr_loaded = [sem(f"attr{i}") for i in range(U)]
        scattered = [sem(f"scattered{i}") for i in range(2)]
        issued = sem("issued")
        pe_issued = sem("pe_issued")
        gi, di, si = (sb(x, [P, 2, T], I32) for x in ("gi", "di", "si"))
        src_rows, dst_rows = sb("src_rows", [P, 2, T, D]), sb("dst_rows", [P, 2, T, D])
        src_t, dst_t = sb("src_t", [P, 2, W]), sb("dst_t", [P, 2, W])
        attr = sb("attr", [R + 1, U, W])
        vk = sb("vk", [P, U, W])
        product = sb("product", [P, 2, W])
        restart = sb("restart", [H, W])
        top = sb("top", [H, 2, W + 1])
        change = sb("change", [H, 2, 2, W])
        v_w = sb("v_w", [M, 2, W])
        acc, den = sb("acc", [M, 2, W]), sb("den", [H, 2, W])
        inv = sb("inv", [P, 2, T, H])
        out = sb("out", [P, 2, T, M])
        p_a, p_b, p_q, p_vk, p_alpha, p_p, p_d, p_o = (ps(x, [P, W]) for x in ("p_a", "p_b", "p_q", "p_vk", "p_alpha", "p_p", "p_d", "p_o"))
        block = ctx.enter_context(nc.Block())
        DEPTH = 6

        @block.sync
        def _(sp):
            sp.wait_ge(const, 1)

            def step(at):
                if b := at(1):
                    s = b.slot(2)
                    after(sp, vk_done, b, lag=U)
                    sp.dma_start(attr[0:R, b.slot(U), :], a["edge_attr_t"][:, bass.ds(b.n * W, W)]).then_inc(attr_loaded[b.slot(U)], 16)
            pipeline(sp, EB, U, DEPTH, step)

        @block.gpsimd
        def _(pool):
            pool.memset(attr[:], 1.0).then_inc(const, 1)
            pool.memset(top[:, 1, W:W + 1], 0.0).then_inc(const, 1)
            pool.memset(acc[:, 1, W - 1:W], 0.0).then_inc(const, 1)
            pool.memset(den[:, 1, W - 1:W], 0.0).then_inc(const, 1)

            def step(at):
                if b := at(1):
                    s = b.slot(2)
                    after(pool, index_ready, b)
                    after(pool, src_turned, b, lag=2)
                    after(pool, dst_turned, b, lag=2)
                    carry(pool, issued)
                    gather_rows(pool, src_rows[:, s], k["x2"], gi[:, s], gathered[s])
                    gather_rows(pool, dst_rows[:, s], k["x2"], di[:, s], gathered[s])
                if b := at(6):
                    s = b.slot(2)
                    after(pool, sindex_ready, b)
                    after(pool, out_ready, b)
                    pool.wait_ge(k["agg_m_zeroed"], 16 * (NB // 7))
                    carry(pool, issued)
                    scatter_rows(pool, k["agg_m"], out[:, s], si[:, s], scattered[s])
            pipeline(pool, EB, U, DEPTH, step)
            all_landed(pool, scattered, EB, 16 * T)

        @block.tensor
        def _(pe):
            def step(at):
                if b := at(5):
                    s = b.slot(2)
                    after(pe, summed, b)
                    after(pe, den_summed, b)
                    after(pe, out_ready, b, lag=1)
                    carry(pe, pe_issued)
                    for t in range(T):
                        pe.transpose(p_o[:, t * M:(t + 1) * M], acc[:, s, t * P:(t + 1) * P], k["ident"][0:M, 0:M])
                    for t in range(T):
                        last = pe.transpose(p_o[:, T * M + t * H:T * M + (t + 1) * H], den[:, s, t * P:(t + 1) * P], k["ident"][0:H, 0:H])
                    last.then_inc(back, 1)
                if b := at(3):
                    s = b.slot(2)
                    after(pe, product_ready, b)
                    after(pe, exp_in, b, lag=1)
                    pe.matmul(p_alpha[0:H, :], k["head_sum"][:], product[:, s, :], start=True, stop=True).then_inc(alpha_done, 1)
                if b := at(4):
                    s = b.slot(2)
                    after(pe, exp_ready, b)
                    after(pe, weighted, b, lag=1)
                    after(pe, summed, b, lag=1)
                    pe.matmul(p_p[0:M, :], k["head_spread"][:], change[:, s, 1, :], start=True, stop=True)
                    pe.matmul(p_d[0:M, :], k["head_spread"][:], change[:, s, 0, :], start=True, stop=True).then_inc(spread, 1)
                if b := at(2):
                    s = b.slot(2)
                    landed(pe, gathered, b, 2 * 16 * T)
                    after(pe, src_ready, b, lag=1)
                    for t in range(T):
                        last = pe.transpose(p_a[:, t * P:(t + 1) * P], src_rows[:, s, t, :], k["ident"][:])
                    last.then_inc(src_turned, 1)
                    after(pe, dst_ready, b, lag=1)
                    for t in range(T):
                        last = pe.transpose(p_b[:, t * P:(t + 1) * P], dst_rows[:, s, t, :], k["ident"][:])
                    last.then_inc(dst_turned, 1)
                    landed(pe, attr_loaded, b, 16)
                    after(pe, src_ready, b)
                    after(pe, vk_ready, b, lag=1)
                    pe.matmul(p_vk[:], k["w_vk"][:], src_t[:, s, :], start=True, stop=False)
                    pe.matmul(p_vk[:], k["w_ev"][:], attr[:, b.slot(U), :], start=False, stop=True).then_inc(vk_done, 1)
                    after(pe, dst_ready, b)
                    after(pe, product_ready, b, lag=1)
                    pe.matmul(p_q[:], k["w_q"][:], dst_t[:, s, :], start=True, stop=True).then_inc(q_done, 1)
            pipeline(pe, EB, U, DEPTH, step)

        @block.scalar
        def _(act):
            def step(at):
                if b := at(2):
                    s = b.slot(2)
                    after(act, src_turned, b)
                    after(act, vk_done, b, lag=2)
                    act.activation(src_t[:, s, :], p_a[:], ACT.Copy).then_inc(src_ready, 1)
                    after(act, dst_turned, b)
                    after(act, q_done, b, lag=2)
                    act.activation(dst_t[:, s, :], p_b[:], ACT.Copy).then_inc(dst_ready, 1)
                    after(act, vk_done, b)
                    after(act, weighted, b, lag=U)
                    act.activation(vk[:, b.slot(U), :], p_vk[:], ACT.Copy).then_inc(vk_ready, 1)
                if b := at(3):
                    s = b.slot(2)
                    after(act, exp_in, b)
                    act.activation(change[:, s], change[:, s], ACT.Exp).then_inc(exp_ready, 1)
            pipeline(act, EB, U, DEPTH, step)

        @block.vector
        def _(dve):
            dve.wait_ge(const, 4)
            highest, outs = Steps(dve, max_steps, 4), Steps(dve, out_steps, 1)

            def step(at):
                if b := at(0):
                    s = b.slot(2)
                    freed(dve, gathered, b, 2 * 16 * T)
                    dve.tensor_copy(gi[:, s, :], k["gather_i"][:, bass.ds(b.n * T, T)])
                    dve.tensor_copy(di[:, s, :], k["dst_i"][:, bass.ds(b.n * T, T)]).then_inc(index_ready, 1)
                if b := at(5):
                    s = b.slot(2)
                    freed(dve, scattered, b, 16 * T)
                    dve.tensor_copy(si[:, s, :], k["scatter_i"][:, bass.ds(b.n * T, T)]).then_inc(sindex_ready, 1)
                    after(dve, back, b)
                    outs.start(b.n)
                    outs.made(dve.reciprocal(inv[:, s], p_o[:, T * M:T * M + T * H].rearrange("p (t h) -> p t h", t=T)))
                    dve.tensor_tensor(out[:, s].rearrange("p t (h c) -> p (t h) c", h=H),
                                      p_o[:, 0:T * M].rearrange("p (g c) -> p g c", c=C),
                                      inv[:, s].rearrange("p t h -> p (t h)").unsqueeze(2).broadcast_to([P, T * H, C]),
                                      ALU.mult).then_inc(out_ready, 1)
                if b := at(3):
                    s = b.slot(2)
                    u = s
                    highest.start(b.n)
                    highest.made(dve.tensor_copy(top[:, u, 0:1], top[:, 1 - u, W:W + 1]))
                    highest.made(dve.tensor_scalar(restart[:], k["keep"][0:H, bass.ds(b.n * W, W)], 1.0, BIG, ALU.subtract, ALU.mult))
                    after(dve, alpha_done, b)
                    highest.made(dve.tensor_tensor_scan(top[:, u, 1:W + 1], restart[:], p_alpha[0:H, :], top[:, u, 0:1], ALU.add, ALU.max))
                    after(dve, spread, b, lag=2)
                    after(dve, den_summed, b, lag=2)
                    highest.made(dve.tensor_tensor(change[:, u, 0, :], top[:, u, 0:W], restart[:], ALU.add))
                    dve.tensor_tensor(change[:, u, 0, :], change[:, u, 0, :], top[:, u, 1:W + 1], ALU.subtract)
                    dve.tensor_tensor(change[:, u, 1, :], p_alpha[0:H, :], top[:, u, 1:W + 1], ALU.subtract).then_inc(exp_in, 1)
                    highest.end()
                if b := at(4):
                    s = b.slot(2)
                    after(dve, spread, b)
                    after(dve, back, b, lag=2)
                    dve.tensor_tensor(v_w[:, s, :], p_p[0:M, :], vk[0:M, b.slot(U), :], ALU.mult).then_inc(weighted, 1)
                    after(dve, den_summed, b, lag=1)
                    dve.tensor_tensor_scan(den[:, s, :], change[:, s, 0, :], change[:, s, 1, :],
                                           den[:, 1 - s, W - 1:W], ALU.mult, ALU.add).then_inc(den_summed, 1)
                    after(dve, weighted, b)
                    after(dve, summed, b, lag=1)
                    dve.tensor_tensor_scan(acc[:, s, :], p_d[0:M, :], v_w[:, s, :],
                                           acc[:, 1 - s, W - 1:W], ALU.mult, ALU.add).then_inc(summed, 1)
                if b := at(2):
                    s = b.slot(2)
                    after(dve, q_done, b)
                    after(dve, vk_ready, b)
                    after(dve, alpha_done, b, lag=2)
                    dve.scalar_tensor_tensor(product[:, s, :], p_q[:], k["b_q"][:], vk[:, b.slot(U), :], ALU.add, ALU.mult).then_inc(product_ready, 1)
            pipeline(dve, EB, U, DEPTH, step)


class NodeInput:

    def __init__(self, sem, n_tables, slots, reads_x=False):
        self.sems = [sem(f"loaded{i}") for i in range(slots)]
        self.per, self.reads_x = 16 * n_tables, reads_x

    def landed(self, eng, b):
        s, turn = b.slot(len(self.sems)), b.turn(len(self.sems))
        more = 16 if self.reads_x and b.is_last(NB) else 0
        eng.wait_ge(self.sems[s], self.per * (turn + 1) + more)

    def load(self, sp, tile, table, b, width=D):
        sem = self.sems[b.slot(len(self.sems))]
        if table.shape[0] == NPAD or not b.is_last(NB):
            sp.dma_start(flat(tile), table_rows(table, b.n, width)).then_inc(sem, 16)
            return
        rest = table[(NB - 1) * P * G:N, :].rearrange("(p k) d -> p (k d)", k=G)
        sp.dma_start(flat(tile[0:96]), rest[0:96]).then_inc(sem, 16)
        sp.dma_start(flat(tile[96:LASTP]), rest[96:LASTP]).then_inc(sem, 16)


def nodes_layer0(nc, k, a):
    with ExitStack() as ctx:
        sb = lambda n, shape, dt=F32: ctx.enter_context(nc.sbuf_tensor("n0_" + n, shape, dt))
        ps = lambda n, shape: ctx.enter_context(nc.psum_tensor("n0_" + n, shape, F32))
        sem = pass_semaphores(nc, ctx, "n0_")
        x_turned, xt_ready, h_done, var1, root1, scale1, norm1, beta_done, gamma_done, res_ready = map(
            sem, ("x_turned", "xt_ready", "h_done", "var1", "root1", "scale1", "norm1", "beta_done", "gamma_done", "res_ready"))
        var2, root2, scale2, x1_ready, x1_turned, x1t_ready, y_done, hs_ready, steps1, steps2, norm_steps1, norm_steps2 = map(
            sem, ("var2", "root2", "scale2", "x1_ready", "x1_turned", "x1t_ready", "y_done", "hs_ready", "steps1", "steps2", "norm_steps1", "norm_steps2"))
        U = 4
        source = NodeInput(sem, 2, U, reads_x=True)
        x1_stored, hs_stored = ([sem(f"{n}{i}") for i in range(2)] for n in ("x1_stored", "hs_stored"))
        x, agg, z = (sb(n, [P, U, G, D]) for n in ("x", "agg", "z"))
        xt, x1, x1t, hs = (sb(n, [P, 2, G, D]) for n in ("xt", "x1", "x1t", "hs"))
        stats1, stats2 = sb("stats1", [P, G, 6]), sb("stats2", [P, G, 6])
        diff1, diff2 = sb("diff1", [P, G]), sb("diff2", [P, G])
        mv1, mv2 = sb("mv1", [P, 2, G, 2]), sb("mv2", [P, 2, G, 2])
        r1, r2, nm1, nm2 = (sb(n, [P, 2, G]) for n in ("r1", "r2", "nm1", "nm2"))
        p_x, p_h, p_x1, p_y = (ps(n, [P, G, D]) for n in ("p_x", "p_h", "p_x1", "p_y"))
        block = ctx.enter_context(nc.Block())
        DEPTH = 6

        @block.sync
        def _(sp):
            def step(at):
                if b := at(0):
                    u = b.slot(U)
                    after(sp, res_ready, b, lag=U)
                    after(sp, h_done, b, lag=U)
                    source.load(sp, x[:, u], a["x"], b)
                    source.load(sp, agg[:, u], k["agg"], b)
                if b := at(6 + AHEAD):
                    after(sp, hs_ready, b)
                    sp.dma_start(table_rows(k["hs1"], b.n), flat(hs[:, b.slot(2)])).then_inc(hs_stored[b.slot(2)], 16)
                if b := at(4 + AHEAD):
                    after(sp, x1_ready, b)
                    sp.dma_start(table_rows(k["x1"], b.n), flat(x1[:, b.slot(2)])).then_inc(x1_stored[b.slot(2)], 16)
            pipeline(sp, NB, U, DEPTH + AHEAD, step)
            all_landed(sp, x1_stored, NB, 16)
            all_landed(sp, hs_stored, NB, 16)

        @block.gpsimd
        def _(pool):
            def step(at):
                if b := at(2):
                    u = b.slot(U)
                    after(pool, x_turned, b)
                    pool.tensor_tensor(x[:, u], x[:, u], over_tiles(k["beta0_r"][:]), ALU.add).then_inc(beta_done, 1)
                    after(pool, norm1, b)
                    pool.tensor_tensor(z[:, u], z[:, u], over_tiles(k["gamma0_r"][:]), ALU.mult).then_inc(gamma_done, 1)
                    after(pool, beta_done, b)
                    after(pool, gamma_done, b)
                    pool.tensor_tensor(z[:, u], z[:, u], x[:, u], ALU.add).then_inc(res_ready, 1)
            pipeline(pool, NB, U, DEPTH, step)

        @block.tensor
        def _(pe):
            def step(at):
                if b := at(6):
                    after(pe, x1t_ready, b)
                    after(pe, hs_ready, b, lag=1)
                    for t in range(G):
                        last = pe.matmul(p_y[:, t, :], x1t[:, b.slot(2), t, :], k["w_l1"][:], start=t % 4 == 0, stop=False,
                                         skip_group_check=True)
                    for c in range(2):
                        last = pe.matmul(p_y[:, 4 * c:4 * c + 4, :], k["ones_b"][:], k["bias_l1"][:], start=False, stop=True,
                                         skip_group_check=True)
                    last.then_inc(y_done, 1)
                if b := at(5):
                    after(pe, x1_ready, b)
                    after(pe, x1t_ready, b, lag=1)
                    for t in range(G):
                        last = pe.transpose(p_x1[:, t, :], x1[:, b.slot(2), t, :], k["ident"][:])
                    last.then_inc(x1_turned, 1)
                if b := at(0):
                    source.landed(pe, b)
                    after(pe, xt_ready, b, lag=1)
                    for t in range(G):
                        last = pe.transpose(p_x[:, t, :], x[:, b.slot(U), t, :], k["ident"][:])
                    last.then_inc(x_turned, 1)
                if b := at(1):
                    after(pe, xt_ready, b)
                    after(pe, norm1, b, lag=1)
                    for t in range(G):
                        pe.matmul(p_h[:, t, :], xt[:, b.slot(2), t, :], k["w_pre"][:], start=t % 4 == 0, stop=False,
                                  skip_group_check=True)
                    for c in range(2):
                        pe.matmul(p_h[:, 4 * c:4 * c + 4, :], k["ident"][:], agg[:, b.slot(U), 4 * c:4 * c + 4, :], start=False, stop=False,
                                  skip_group_check=True)
                        last = pe.matmul(p_h[:, 4 * c:4 * c + 4, :], k["ones_b"][:], k["bias_h"][:], start=False, stop=True,
                                         skip_group_check=True)
                    last.then_inc(h_done, 1)
            pipeline(pe, NB, U, DEPTH, step)

        @block.scalar
        def _(act):
            def step(at):
                if b := at(2):
                    s = b.slot(2)
                    after(act, scale1, b)
                    after(act, x1_ready, b, lag=U)
                    for t in range(G):
                        last = act.activation(z[:, b.slot(U), t, :], p_h[:, t, :], ACT.Identity, scale=r1[:, s, t:t + 1], bias=nm1[:, s, t:t + 1])
                    last.then_inc(norm1, 1)
                if b := at(5):
                    after(act, x1_turned, b)
                    after(act, y_done, b, lag=2)
                    act.activation(x1t[:, b.slot(2)], p_x1[:], ACT.Copy).then_inc(x1t_ready, 1)
                if b := at(0):
                    after(act, x_turned, b)
                    after(act, h_done, b, lag=2)
                    act.activation(xt[:, b.slot(2)], p_x[:], ACT.Copy).then_inc(xt_ready, 1)
                if b := at(4):
                    s = b.slot(2)
                    after(act, scale2, b)
                    freed(act, x1_stored, b, 16)
                    after(act, x1_turned, b, lag=2)
                    for t in range(G):
                        last = act.activation(x1[:, s, t, :], z[:, b.slot(U), t, :], ACT.Identity, scale=r2[:, s, t:t + 1], bias=nm2[:, s, t:t + 1])
                    last.then_inc(x1_ready, 1)
                if b := at(3):
                    s = b.slot(2)
                    after(act, var2, b)
                    act.activation(r2[:, s], mv2[:, s, :, 1], ACT.Sqrt, bias=k["eps"][:]).then_inc(root2, 1)
                if b := at(1):
                    s = b.slot(2)
                    after(act, var1, b)
                    act.activation(r1[:, s], mv1[:, s, :, 1], ACT.Sqrt, bias=k["eps"][:]).then_inc(root1, 1)
            pipeline(act, NB, U, DEPTH, step)

        @block.vector
        def _(dve):
            first, second = Steps(dve, steps1, 3), Steps(dve, steps2, 3)
            norm_first, norm_second = Steps(dve, norm_steps1, 1), Steps(dve, norm_steps2, 1)

            def step(at):
                if b := at(2):
                    s = b.slot(2)
                    after(dve, root1, b)
                    norm_first.start(b.n)
                    norm_first.made(dve.reciprocal(r1[:, s], r1[:, s]))
                    dve.scalar_tensor_tensor(nm1[:, s], mv1[:, s, :, 0], -0.5, r1[:, s], ALU.mult, ALU.mult).then_inc(scale1, 1)
                if b := at(4):
                    s = b.slot(2)
                    after(dve, root2, b)
                    norm_second.start(b.n)
                    norm_second.made(dve.reciprocal(r2[:, s], r2[:, s]))
                    dve.scalar_tensor_tensor(nm2[:, s], mv2[:, s, :, 0], -0.5, r2[:, s], ALU.mult, ALU.mult).then_inc(scale2, 1)
                if b := at(6):
                    after(dve, y_done, b)
                    freed(dve, hs_stored, b, 16)
                    dve.tensor_tensor(hs[:, b.slot(2)], p_y[:], over_width(k["dinv_src"][:, bass.ds(b.n * G, G)]), ALU.mult).then_inc(hs_ready, 1)
                if b := at(3):
                    after(dve, res_ready, b)
                    second.start(b.n)
                    node_stats(dve, second, z[:, b.slot(U)], stats2, mv2[:, b.slot(2)], diff2[:]).then_inc(var2, 1)
                    second.end()
                if b := at(1):
                    after(dve, h_done, b)
                    first.start(b.n)
                    node_stats(dve, first, p_h, stats1, mv1[:, b.slot(2)], diff1[:]).then_inc(var1, 1)
                    first.end()
            pipeline(dve, NB, U, DEPTH, step)


def nodes_batch_stats(nc, k, a):
    with ExitStack() as ctx:
        sb = lambda n, shape, dt=F32: ctx.enter_context(nc.sbuf_tensor("bs_" + n, shape, dt))
        ps = lambda n, shape: ctx.enter_context(nc.psum_tensor("bs_" + n, shape, F32))
        sem = pass_semaphores(nc, ctx, "bs_")
        sum_ready, square_ready, used, const, totals, steps_, root, rows_ready, rows_done = map(
            sem, ("sum", "square", "used", "const", "totals", "steps", "root", "rows_ready", "rows_done"))
        U = 4
        source = NodeInput(sem, 2, U)
        h, agg, sq = sb("h", [P, U, G, D]), sb("agg", [P, U, G, D]), sb("sq", [P, 2, G, D])
        zero = sb("zero", [P, P])
        mean, ex2, var, inv, scale, shift = (sb(n, [P, 1]) for n in ("mean", "ex2", "var", "inv", "scale", "shift"))
        spread = sb("spread", [P, 2, P])
        p_sum, p_sq, p_rows = ps("p_sum", [P, 512]), ps("p_sq", [P, 512]), ps("p_rows", [P, 512])
        block = ctx.enter_context(nc.Block())
        DEPTH = 1

        @block.sync
        def _(sp):
            def step(at):
                if b := at(0):
                    u = b.slot(U)
                    after(sp, used, b, lag=U)
                    source.load(sp, h[:, u], k["hs1"], b)
                    source.load(sp, agg[:, u], k["agg"], b)
            pipeline(sp, NB, U, DEPTH + AHEAD, step)

        @block.gpsimd
        def _(pool):
            pool.memset(zero[:], 0.0).then_inc(const, 1)

        @block.tensor
        def _(pe):
            pe.wait_ge(const, 1)
            for p in (p_sum, p_sq):
                pe.matmul(p[:, 0:1], zero[:], zero[:, 0:1], start=True, stop=False)

            def step(at):
                if b := at(1):
                    after(pe, sum_ready, b)
                    for t in range(G):
                        pe.matmul(p_sum[:, 0:1], h[:, b.slot(U), t, :], k["sum_w"][:, bass.ds(b.n * G + t, 1)], start=False, stop=False)
                    after(pe, square_ready, b)
                    for t in range(G):
                        last = pe.matmul(p_sq[:, 0:1], sq[:, b.slot(2), t, :], k["square_w"][:, bass.ds(b.n * G + t, 1)], start=False, stop=False)
                    last.then_inc(used, 1)
            pipeline(pe, NB, U, DEPTH, step)
            for p in (p_sum, p_sq):
                last = pe.matmul(p[:, 0:1], zero[:], zero[:, 0:1], start=False, stop=True)
            last.then_inc(totals, 1)
            pe.wait_ge(rows_ready, 1)
            for i in range(2):
                last = pe.matmul(p_rows[:, i * D:(i + 1) * D], spread[:, i, :], k["ident"][:], start=True, stop=True)
            last.then_inc(rows_done, 1)

        @block.scalar
        def _(act):
            def step(at):
                if b := at(0):
                    after(act, sum_ready, b)
                    after(act, used, b, lag=2)
                    act.activation(sq[:, b.slot(2)], h[:, b.slot(U)], ACT.Square).then_inc(square_ready, 1)
            pipeline(act, NB, U, DEPTH, step)
            act.wait_ge(steps_, 4)
            act.activation(inv[:], var[:], ACT.Sqrt, bias=k["eps"][:]).then_inc(root, 1)

        @block.vector
        def _(dve):
            def step(at):
                if b := at(0):
                    u = b.slot(U)
                    source.landed(dve, b)
                    dve.tensor_tensor(h[:, u], h[:, u], agg[:, u], ALU.add).then_inc(sum_ready, 1)
            pipeline(dve, NB, U, DEPTH, step)
            dve.wait_ge(totals, 1)
            steps = Steps(dve, steps_, 8)
            steps.start(0)
            steps.made(dve.tensor_scalar(mean[:], p_sum[:, 0:1], 1.0 / N, None, ALU.mult))
            steps.made(dve.tensor_scalar(ex2[:], p_sq[:, 0:1], 1.0 / N, None, ALU.mult))
            steps.made(dve.tensor_tensor(var[:], mean[:], mean[:], ALU.mult))
            steps.made(dve.tensor_tensor(var[:], ex2[:], var[:], ALU.subtract))
            dve.wait_ge(root, 1)
            steps.made(dve.reciprocal(inv[:], inv[:]))
            steps.made(dve.tensor_tensor(scale[:], inv[:], k["gamma1_c"][:], ALU.mult))
            steps.made(dve.tensor_tensor(shift[:], mean[:], scale[:], ALU.mult))
            steps.made(dve.tensor_tensor(shift[:], k["beta1_c"][:], shift[:], ALU.subtract))
            steps.end()
            dve.tensor_copy(spread[:, 0, :], scale[:].broadcast_to([P, P]))
            dve.tensor_copy(spread[:, 1, :], shift[:].broadcast_to([P, P])).then_inc(rows_ready, 1)
            dve.wait_ge(rows_done, 1)
            dve.tensor_copy(k["bn_scale_r"][:], p_rows[:, 0:D])
            dve.tensor_copy(k["bn_shift_r"][:], p_rows[:, D:2 * D])


def nodes_layer1(nc, k, a):
    with ExitStack() as ctx:
        sb = lambda n, shape, dt=F32: ctx.enter_context(nc.sbuf_tensor("n1_" + n, shape, dt))
        sem = pass_semaphores(nc, ctx, "n1_")
        sum_ready, scaled, shifted, z_ready, var, root, scale_ready, x2_ready, steps_ = map(
            sem, ("sum", "scaled", "shifted", "z", "var", "root", "scale", "x2", "steps"))
        U = 4
        source = NodeInput(sem, 3, U)
        x2_stored = [sem(f"x2_stored{i}") for i in range(2)]
        x, h, agg = (sb(n, [P, U, G, D]) for n in ("x", "h", "agg"))
        x2 = sb("x2", [P, 2, G, D])
        diff = sb("diff", [P, G])
        stats, mv, r, nm = sb("stats", [P, G, 6]), sb("mv", [P, 2, G, 2]), sb("r", [P, 2, G]), sb("nm", [P, 2, G])
        block = ctx.enter_context(nc.Block())
        DEPTH = 2

        @block.sync
        def _(sp):
            def step(at):
                if b := at(0):
                    u = b.slot(U)
                    after(sp, x2_ready, b, lag=U)
                    source.load(sp, x[:, u], k["x1"], b)
                    source.load(sp, h[:, u], k["hs1"], b)
                    source.load(sp, agg[:, u], k["agg"], b)
                if b := at(2 + AHEAD):
                    after(sp, x2_ready, b)
                    sp.dma_start(table_rows(k["x2"], b.n), flat(x2[:, b.slot(2)])).then_inc(x2_stored[b.slot(2)], 16)
            pipeline(sp, NB, U, DEPTH + AHEAD, step)
            all_landed(sp, x2_stored, NB, 16)

        @block.gpsimd
        def _(pool):
            def step(at):
                if b := at(1):
                    u = b.slot(U)
                    after(pool, scaled, b)
                    pool.tensor_tensor(h[:, u], h[:, u], over_tiles(k["bn_shift_r"][:]), ALU.add).then_inc(shifted, 1)
                if b := at(0):
                    u = b.slot(U)
                    source.landed(pool, b)
                    pool.tensor_tensor(h[:, u], h[:, u], agg[:, u], ALU.add).then_inc(sum_ready, 1)
            pipeline(pool, NB, U, DEPTH, step)

        @block.scalar
        def _(act):
            def step(at):
                if b := at(2):
                    s = b.slot(2)
                    after(act, var, b)
                    act.activation(r[:, s], mv[:, s, :, 1], ACT.Sqrt, bias=k["eps"][:]).then_inc(root, 1)
                    after(act, scale_ready, b)
                    freed(act, x2_stored, b, 16)
                    for t in range(G):
                        last = act.activation(x2[:, s, t, :], h[:, b.slot(U), t, :], ACT.Identity, scale=r[:, s, t:t + 1], bias=nm[:, s, t:t + 1])
                    last.then_inc(x2_ready, 1)
            pipeline(act, NB, U, DEPTH, step)

        @block.vector
        def _(dve):
            steps = Steps(dve, steps_, 4)

            def step(at):
                if b := at(2):
                    s, u = b.slot(2), b.slot(U)
                    steps.start(b.n)
                    after(dve, shifted, b)
                    dve.scalar_tensor_tensor(h[:, u], h[:, u], 0.0, x[:, u], ALU.max, ALU.add).then_inc(z_ready, 1)
                    after(dve, z_ready, b)
                    node_stats(dve, steps, h[:, u], stats, mv[:, s], diff[:]).then_inc(var, 1)
                if b := at(1):
                    u = b.slot(U)
                    after(dve, sum_ready, b)
                    for t in range(G):
                        last = dve.scalar_tensor_tensor(h[:, u, t, :], h[:, u, t, :], k["dinv_src"][:, bass.ds(b.n * G + t, 1)], k["bn_scale_r"][:],
                                                        ALU.mult, ALU.mult)
                    last.then_inc(scaled, 1)
                if b := at(2):
                    s = b.slot(2)
                    after(dve, root, b)
                    steps.made(dve.reciprocal(r[:, s], r[:, s]))
                    dve.scalar_tensor_tensor(nm[:, s], mv[:, s, :, 0], -0.5, r[:, s], ALU.mult, ALU.mult).then_inc(scale_ready, 1)
                    steps.end()
            pipeline(dve, NB, U, DEPTH, step)


def nodes_layer2(nc, k, a):
    with ExitStack() as ctx:
        sb = lambda n, shape, dt=F32: ctx.enter_context(nc.sbuf_tensor("n2_" + n, shape, dt))
        ps = lambda n, shape: ctx.enter_context(nc.psum_tensor("n2_" + n, shape, F32))
        sem = pass_semaphores(nc, ctx, "n2_")
        x_turned, xt_ready, r_done, gated, gate_in, beta_ready, diff_ready, mix_ready = map(
            sem, ("x_turned", "xt_ready", "r_done", "gated", "gate_in", "beta", "diff", "mix"))
        mix_turned, mixt_ready, m_done, z_ready, var, root, scale_ready, x3_ready = map(
            sem, ("mix_turned", "mixt", "m_done", "z", "var", "root", "scale", "x3"))
        x3_turned, x3t_ready, y_done, hs_ready, gate_steps, mix_steps, steps_, pool_steps = map(
            sem, ("x3_turned", "x3t", "y_done", "hs", "gate_steps", "mix_steps", "steps", "pool_steps"))
        U = 6
        source = NodeInput(sem, 2, U)
        x3_stored, hs_stored = ([sem(f"{n}{i}") for i in range(2)] for n in ("x3_stored", "hs_stored"))
        x, msg = sb("x", [P, U, G, D]), sb("msg", [P, U, G, M])
        xt, z, x3, x3t, hs = (sb(n, [P, 2, G, D]) for n in ("xt", "z", "x3", "x3t", "hs"))
        prod, mix = sb("prod", [P, 2, G, M]), sb("mix", [P, 2, G, M])
        mixt = sb("mixt", [P, 2, G // 2, P])
        gate = sb("gate", [P, 2, G])
        diff = sb("diff", [P, G])
        stats, mv, r, nm = sb("stats", [P, G, 6]), sb("mv", [P, 2, G, 2]), sb("r", [P, 2, G]), sb("nm", [P, 2, G])
        half = sb("half", [P, G])
        issued = sem("issued")
        p_x, p_r, p_y = (ps(n, [P, G, D]) for n in ("p_x", "p_r", "p_y"))
        p_mix = ps("p_mix", [P, G // 2, P])
        block = ctx.enter_context(nc.Block())
        DEPTH = 6

        @block.sync
        def _(sp):
            def step(at):
                if b := at(0):
                    u = b.slot(U)
                    after(sp, z_ready, b, lag=U)
                    source.load(sp, x[:, u], k["x2"], b)
                    source.load(sp, msg[:, u], k["agg_m"], b, M)
                if b := at(6 + AHEAD):
                    after(sp, hs_ready, b)
                    sp.dma_start(table_rows(k["hs3"], b.n), flat(hs[:, b.slot(2)])).then_inc(hs_stored[b.slot(2)], 16)
                if b := at(4 + AHEAD):
                    after(sp, x3_ready, b)
                    sp.dma_start(table_rows(k["x3"], b.n), flat(x3[:, b.slot(2)])).then_inc(x3_stored[b.slot(2)], 16)
            pipeline(sp, NB, U, DEPTH + AHEAD, step)
            all_landed(sp, x3_stored, NB, 16)
            all_landed(sp, hs_stored, NB, 16)

        @block.gpsimd
        def _(pool):
            pool.memset(half[:], -0.5).then_inc(pool_steps, 1)
            pool.wait_ge(pool_steps, 1)

            def step(at):
                if b := at(4):
                    s = b.slot(2)
                    after(pool, var, b)
                    carry(pool, issued)
                    pool.tensor_scalar(r[:, s], mv[:, s, :, 1], EPS, None, ALU.add).then_inc(pool_steps, 1)
                    pool.wait_ge(pool_steps, b.n + 2)
                    pool.tensor_tensor(r[:, s], r[:, s], half[:], ALU.pow).then_inc(root, 1)
                if b := at(2):
                    s, u = b.slot(2), b.slot(U)
                    after(pool, diff_ready, b)
                    pool.tensor_tensor(mix[:, s], mix[:, s], msg[:, u], ALU.add).then_inc(mix_ready, 1)
                if b := at(0):
                    s, u = b.slot(2), b.slot(U)
                    source.landed(pool, b)
                    after(pool, gate_in, b, lag=2)
                    pool.tensor_tensor(prod[:, s], msg[:, u], over_tiles(k["w_out"][:]), ALU.mult).then_inc(gated, 1)
            pipeline(pool, NB, U, DEPTH, step)

        @block.tensor
        def _(pe):
            def step(at):
                if b := at(3):
                    s = b.slot(2)
                    after(pe, mix_ready, b)
                    after(pe, mixt_ready, b, lag=1)
                    for t in range(G // 2):
                        last = pe.transpose(p_mix[:, t, :], mix[:, s, 2 * t:2 * t + 2, :].rearrange("p k d -> p (k d)"), k["ident"][:])
                    last.then_inc(mix_turned, 1)
                if b := at(0):
                    source.landed(pe, b)
                    after(pe, x3t_ready, b, lag=6)
                    after(pe, xt_ready, b, lag=1)
                    for t in range(G):
                        last = pe.transpose(p_x[:, t, :], x[:, b.slot(U), t, :], k["ident"][:])
                    last.then_inc(x_turned, 1)
                if b := at(3):
                    after(pe, mixt_ready, b)
                    after(pe, hs_ready, b, lag=4)
                    after(pe, z_ready, b, lag=1)
                    for t in range(G):
                        part = slice(M * (t % 2), M * (t % 2 + 1))
                        last = pe.matmul(p_y[:, 4 * (t % 2) + t // 2, :], mixt[part, b.slot(2), t // 2, :], k["w_m2n"][part, :], start=True, stop=True)
                    last.then_inc(m_done, 1)
                if b := at(1):
                    after(pe, xt_ready, b)
                    after(pe, diff_ready, b, lag=1)
                    after(pe, gate_in, b, lag=1)
                    for t in range(G):
                        pe.matmul(p_r[:, t, 0:M + 1], xt[:, b.slot(2), t, :], k["w_r"][:], start=t % 4 == 0, stop=False,
                                  skip_group_check=True)
                    for c in range(2):
                        last = pe.matmul(p_r[:, 4 * c:4 * c + 4, 0:M + 1], k["ones_b"][:], k["bias_r"][:], start=False, stop=True,
                                         skip_group_check=True)
                    last.then_inc(r_done, 1)
                if b := at(5):
                    after(pe, x3_ready, b)
                    after(pe, xt_ready, b, lag=-5, n=NB)
                    after(pe, x3t_ready, b, lag=1)
                    for t in range(G):
                        last = pe.transpose(p_x[:, t, :], x3[:, b.slot(2), t, :], k["ident"][:])
                    last.then_inc(x3_turned, 1)
                if b := at(6):
                    after(pe, x3t_ready, b)
                    after(pe, z_ready, b, lag=-3, n=NB)
                    after(pe, hs_ready, b, lag=1)
                    for t in range(G):
                        last = pe.matmul(p_y[:, t, :], x3t[:, b.slot(2), t, :], k["w1_l3"][:], start=True, stop=True)
                    last.then_inc(y_done, 1)
            pipeline(pe, NB, U, DEPTH, step)

        @block.scalar
        def _(act):
            def step(at):
                if b := at(2):
                    s = b.slot(2)
                    after(act, gate_in, b)
                    act.activation(gate[:, s], gate[:, s], ACT.Sigmoid).then_inc(beta_ready, 1)
                if b := at(3):
                    after(act, mix_turned, b)
                    after(act, m_done, b, lag=2)
                    act.activation(mixt[:, b.slot(2)], p_mix[:], ACT.Copy).then_inc(mixt_ready, 1)
                if b := at(0):
                    after(act, x_turned, b)
                    after(act, r_done, b, lag=2)
                    act.activation(xt[:, b.slot(2)], p_x[:], ACT.Copy).then_inc(xt_ready, 1)
                if b := at(4):
                    s = b.slot(2)
                    after(act, scale_ready, b)
                    freed(act, x3_stored, b, 16)
                    after(act, x3_turned, b, lag=2)
                    for t in range(G):
                        last = act.activation(x3[:, s, t, :], z[:, s, t, :], ACT.Identity, scale=r[:, s, t:t + 1], bias=nm[:, s, t:t + 1])
                    last.then_inc(x3_ready, 1)
                if b := at(5):
                    after(act, x3_turned, b)
                    after(act, y_done, b, lag=2)
                    act.activation(x3t[:, b.slot(2)], p_x[:], ACT.Copy).then_inc(x3t_ready, 1)
            pipeline(act, NB, U, DEPTH, step)

        @block.vector
        def _(dve):
            gates, mixes, steps = Steps(dve, gate_steps, 1), Steps(dve, mix_steps, 1), Steps(dve, steps_, 3)

            def step(at):
                if b := at(2):
                    s, u = b.slot(2), b.slot(U)
                    mixes.start(b.n)
                    after(dve, r_done, b)
                    after(dve, mix_turned, b, lag=2)
                    mixes.made(dve.tensor_tensor(mix[:, s], p_r[:, :, 0:M], msg[:, u], ALU.subtract))
                    after(dve, beta_ready, b)
                    dve.tensor_tensor(mix[:, s], mix[:, s], over_width(gate[:, s], M), ALU.mult).then_inc(diff_ready, 1)
                    mixes.end()
                if b := at(4):
                    s = b.slot(2)
                    after(dve, root, b)
                    dve.scalar_tensor_tensor(nm[:, s], mv[:, s, :, 0], -0.5, r[:, s], ALU.mult, ALU.mult).then_inc(scale_ready, 1)
                if b := at(3):
                    s, u = b.slot(2), b.slot(U)
                    after(dve, m_done, b)
                    after(dve, x3_ready, b, lag=2)
                    dve.tensor_tensor(z[:, s].rearrange("p (q h) d -> p q h d", h=2), p_y[:].rearrange("p (h q) d -> p q h d", h=2),
                                      x[:, u].rearrange("p (q h) d -> p q h d", h=2), ALU.add).then_inc(z_ready, 1)
                    after(dve, z_ready, b)
                    steps.start(b.n)
                    node_stats(dve, steps, z[:, s], stats, mv[:, s], diff[:]).then_inc(var, 1)
                    steps.end()
                if b := at(1):
                    s = b.slot(2)
                    gates.start(b.n)
                    after(dve, gated, b)
                    after(dve, diff_ready, b, lag=2)
                    gates.made(dve.tensor_reduce(gate[:, s], prod[:, s], mybir.AxisListType.X, ALU.add))
                    gates.end()
                    after(dve, r_done, b)
                    dve.tensor_tensor(gate[:, s], gate[:, s], p_r[:, :, M], ALU.add).then_inc(gate_in, 1)
                if b := at(6):
                    after(dve, y_done, b)
                    freed(dve, hs_stored, b, 16)
                    dve.tensor_tensor(hs[:, b.slot(2)], p_y[:], over_width(k["dinv_dst"][:, bass.ds(b.n * G, G)]), ALU.mult).then_inc(hs_ready, 1)
            pipeline(dve, NB, U, DEPTH, step)


def nodes_layer3_middle(nc, k, a):
    with ExitStack() as ctx:
        sb = lambda n, shape, dt=F32: ctx.enter_context(nc.sbuf_tensor("n3_" + n, shape, dt))
        ps = lambda n, shape: ctx.enter_context(nc.psum_tensor("n3_" + n, shape, F32))
        sem = pass_semaphores(nc, ctx, "n3_")
        sum_ready, scaled, g_ready, turned, gt_ready, y_done, y_ready = map(sem, ("sum", "scaled", "g", "turned", "gt", "y_done", "y"))
        U = 4
        source = NodeInput(sem, 2, U)
        stored = [sem(f"stored{i}") for i in range(2)]
        h, agg = sb("h", [P, U, G, D]), sb("agg", [P, U, G, D])
        gt, y = sb("gt", [P, 2, G, D]), sb("y", [P, 2, G, D])
        p_t, p_y = [ps(f"p_t{i}", [P, G, D]) for i in range(2)], [ps(f"p_y{i}", [P, G, D]) for i in range(2)]
        block = ctx.enter_context(nc.Block())
        DEPTH = 3

        @block.sync
        def _(sp):
            def step(at):
                if b := at(0):
                    u = b.slot(U)
                    after(sp, turned, b, lag=U)
                    source.load(sp, h[:, u], k["hs3"], b)
                    source.load(sp, agg[:, u], k["agg"], b)
                if b := at(3 + AHEAD):
                    after(sp, y_ready, b)
                    sp.dma_start(table_rows(k["hs4"], b.n), flat(y[:, b.slot(2)])).then_inc(stored[b.slot(2)], 16)
            pipeline(sp, NB, U, DEPTH + AHEAD, step)
            all_landed(sp, stored, NB, 16)

        @block.gpsimd
        def _(pool):
            def step(at):
                if b := at(0):
                    u = b.slot(U)
                    source.landed(pool, b)
                    pool.tensor_tensor(h[:, u], h[:, u], agg[:, u], ALU.add).then_inc(sum_ready, 1)
            pipeline(pool, NB, U, DEPTH, step)

        @block.tensor
        def _(pe):
            def step(at):
                if b := at(3):
                    s = b.slot(2)
                    after(pe, gt_ready, b)
                    after(pe, y_ready, b, lag=2)
                    for t in range(G):
                        last = pe.matmul(p_y[s][:, t, :], gt[:, s, t, :], k["w2_l3"][:], start=True, stop=True)
                    last.then_inc(y_done, 1)
                if b := at(2):
                    s = b.slot(2)
                    after(pe, g_ready, b)
                    after(pe, gt_ready, b, lag=2)
                    for t in range(G):
                        last = pe.transpose(p_t[s][:, t, :], h[:, b.slot(U), t, :], k["ident"][:])
                    last.then_inc(turned, 1)
            pipeline(pe, NB, U, DEPTH, step)

        @block.scalar
        def _(act):
            def step(at):
                if b := at(3):
                    s = b.slot(2)
                    after(act, y_done, b)
                    freed(act, stored, b, 16)
                    act.activation(y[:, s], p_y[s][:], ACT.Copy).then_inc(y_ready, 1)
                if b := at(2):
                    s = b.slot(2)
                    after(act, turned, b)
                    after(act, y_done, b, lag=2)
                    act.activation(gt[:, s], p_t[s][:], ACT.Copy).then_inc(gt_ready, 1)
            pipeline(act, NB, U, DEPTH, step)

        @block.vector
        def _(dve):
            def step(at):
                if b := at(1):
                    u = b.slot(U)
                    after(dve, sum_ready, b)
                    for t in range(G):
                        last = dve.scalar_tensor_tensor(h[:, u, t, :], h[:, u, t, :], k["dinv_dst"][:, bass.ds(b.n * G + t, 1)], k["b1_l3_r"][:],
                                                        ALU.mult, ALU.add)
                    last.then_inc(scaled, 1)
                    after(dve, scaled, b)
                    dve.scalar_tensor_tensor(h[:, u], h[:, u], 0.0, over_width(k["dinv_dst"][:, bass.ds(b.n * G, G)]), ALU.max, ALU.mult).then_inc(g_ready, 1)
            pipeline(dve, NB, U, DEPTH, step)


def nodes_layer3_out(nc, k, a):
    with ExitStack() as ctx:
        sb = lambda n, shape, dt=F32: ctx.enter_context(nc.sbuf_tensor("n4_" + n, shape, dt))
        sem = pass_semaphores(nc, ctx, "n4_")
        sum_ready, scaled, z_ready, var, root, scale_ready, out_ready, steps_ = map(
            sem, ("sum", "scaled", "z", "var", "root", "scale", "out", "steps"))
        U = 4
        source = NodeInput(sem, 3, U)
        stored = [sem(f"stored{i}") for i in range(2)]
        x, h, agg = (sb(n, [P, U, G, D]) for n in ("x", "h", "agg"))
        out = sb("out", [P, 2, G, D])
        diff = sb("diff", [P, G])
        stats, mv, r, nm = sb("stats", [P, G, 6]), sb("mv", [P, 2, G, 2]), sb("r", [P, 2, G]), sb("nm", [P, 2, G])
        block = ctx.enter_context(nc.Block())
        DEPTH = 2

        @block.sync
        def _(sp):
            def step(at):
                if b := at(0):
                    u = b.slot(U)
                    after(sp, out_ready, b, lag=U)
                    source.load(sp, x[:, u], k["x3"], b)
                    source.load(sp, h[:, u], k["hs4"], b)
                    source.load(sp, agg[:, u], k["agg"], b)
                if b := at(2 + AHEAD):
                    s = b.slot(2)
                    after(sp, out_ready, b)
                    if b.is_last(NB):
                        rest = a["out"][(NB - 1) * P * G:N, :].rearrange("(p k) d -> p (k d)", k=G)
                        sp.dma_start(rest[0:96], flat(out[0:96, s])).then_inc(stored[s], 16)
                        sp.dma_start(rest[96:LASTP], flat(out[96:LASTP, s])).then_inc(stored[s], 16)
                    else:
                        sp.dma_start(table_rows(a["out"], b.n), flat(out[:, s])).then_inc(stored[s], 16)
            pipeline(sp, NB, U, DEPTH + AHEAD, step)
            for s in range(2):
                sp.wait_ge(stored[s], 16 * ((NB + 1 - s) // 2 + ((NB - 1) % 2 == s)))

        @block.gpsimd
        def _(pool):
            def step(at):
                if b := at(0):
                    u = b.slot(U)
                    source.landed(pool, b)
                    pool.tensor_tensor(h[:, u], h[:, u], agg[:, u], ALU.add).then_inc(sum_ready, 1)
            pipeline(pool, NB, U, DEPTH, step)

        @block.scalar
        def _(act):
            def step(at):
                if b := at(2):
                    s = b.slot(2)
                    after(act, var, b)
                    act.activation(r[:, s], mv[:, s, :, 1], ACT.Sqrt, bias=k["eps"][:]).then_inc(root, 1)
                    after(act, scale_ready, b)
                    freed(act, stored, b, 16)
                    for t in range(G):
                        last = act.activation(out[:, s, t, :], h[:, b.slot(U), t, :], ACT.Identity, scale=r[:, s, t:t + 1], bias=nm[:, s, t:t + 1])
                    last.then_inc(out_ready, 1)
            pipeline(act, NB, U, DEPTH, step)

        @block.vector
        def _(dve):
            steps = Steps(dve, steps_, 5)

            def step(at):
                if b := at(2):
                    s, u = b.slot(2), b.slot(U)
                    steps.start(b.n)
                    after(dve, scaled, b)
                    steps.made(dve.tensor_tensor(h[:, u], h[:, u], x[:, u], ALU.add))
                    node_stats(dve, steps, h[:, u], stats, mv[:, s], diff[:]).then_inc(var, 1)
                if b := at(1):
                    u = b.slot(U)
                    after(dve, sum_ready, b)
                    for t in range(G):
                        last = dve.scalar_tensor_tensor(h[:, u, t, :], h[:, u, t, :], k["dinv_dst"][:, bass.ds(b.n * G + t, 1)], k["b2_l3_r"][:],
                                                        ALU.mult, ALU.add)
                    last.then_inc(scaled, 1)
                if b := at(2):
                    s = b.slot(2)
                    after(dve, root, b)
                    steps.made(dve.reciprocal(r[:, s], r[:, s]))
                    dve.scalar_tensor_tensor(nm[:, s], mv[:, s, :, 0], -0.5, r[:, s], ALU.mult, ALU.mult).then_inc(scale_ready, 1)
                    steps.end()
            pipeline(dve, NB, U, DEPTH, step)


def build(nc, a):
    with ExitStack() as ctx:
        made = {}
        for name, shape, dt in (
                ("ident", [P, P], F32), ("zero", [P, G * D], F32), ("eps", [P, 1], F32), ("keep", [P, EPAD], BF16), ("count_iota", [P, COLS], F32),
                ("valid", [P, COLS], F32), ("dinv_src", [P, COLS], F32), ("dinv_dst", [P, COLS], F32),
                ("sum_w", [P, COLS], F32), ("square_w", [P, COLS], F32),
                ("src_lo", [P, ET], F32), ("src_hi", [P, ET], F32), ("src_c", [P, ET], F32), ("weight_c", [P, ET], F32),
                ("dst_lo", [P, ET], F32), ("dst_hi", [P, ET], F32), ("last_c", [P, ET], F32), ("dst_c", [P, ET], F32),
                ("gather_i", [P, ET], I32), ("scatter_i", [P, ET], I32), ("dst_i", [P, ET], I32),
                ("w_pre", [P, D], F32), ("w1", [P, D], F32), ("w2", [P, D], F32), ("w_l1", [P, D], F32),
                ("w_m2n", [P, D], F32), ("w1_l3", [P, D], F32), ("w2_l3", [P, D], F32),
                ("w_q", [P, 2 * M], F32), ("w_vk", [P, 2 * M], F32), ("w_ev", [R + 1, 2 * M], F32), ("w_r", [P, M + 1], F32),
                ("b_q", [P, 1], F32), ("b_r", [P, M + 1], F32), ("w_out", [P, M], F32),
                ("head_sum", [P, H], F32), ("head_spread", [H, M], F32),
                ("b_pre_c", [P, 1], F32), ("b1_c", [P, 1], F32), ("gamma1_c", [P, 1], F32), ("beta1_c", [P, 1], F32),
                ("b2_r", [P, D], F32), ("none0_r", [P, D], F32), ("gamma0_r", [P, D], F32), ("beta0_r", [P, D], F32),
                ("b_pre_r", [P, D], F32), ("b_l1_r", [P, D], F32), ("b1_l3_r", [P, D], F32), ("b2_l3_r", [P, D], F32),
                ("ones_b", [P, P], BF16), ("bias_h", [P, 4, D], BF16), ("bias_l1", [P, 4, D], BF16), ("bias_r", [P, 4, M + 1], BF16),
                ("bn_scale_r", [P, D], F32), ("bn_shift_r", [P, D], F32)):
            made[name] = ctx.enter_context(nc.sbuf_tensor("k_" + name, shape, dt))
        for name, width in (("agg", D), ("agg_m", M), ("x1", D), ("hs1", D), ("x2", D), ("x3", D), ("hs3", D), ("hs4", D)):
            made[name] = nc.dram_tensor("t_" + name, [NPAD, width], F32).ap()
        k = made
        k["keep_dram"] = nc.dram_tensor("t_keep", [EPAD], BF16).ap()
        k["agg_zeroed"] = ctx.enter_context(nc.semaphore("agg_zeroed"))
        k["agg_m_zeroed"] = ctx.enter_context(nc.semaphore("agg_m_zeroed"))
        todo = [
            lambda: prepare(nc, k, a),
            lambda: edges_layer0(nc, k, a),
            lambda: nodes_layer0(nc, k, a),
            lambda: edges_sum(nc, k, "e1_", k["hs1"], True),
            lambda: nodes_batch_stats(nc, k, a),
            lambda: nodes_layer1(nc, k, a),
            lambda: edges_attention(nc, k, a),
            lambda: nodes_layer2(nc, k, a),
            lambda: edges_sum(nc, k, "e3_", k["hs3"], False),
            lambda: nodes_layer3_middle(nc, k, a),
            lambda: edges_sum(nc, k, "e4_", k["hs4"], False),
            lambda: nodes_layer3_out(nc, k, a),
        ]
        for run in todo:
            run()


def kernel(**inputs):
    import numpy as np
    import concourse.bacc as bacc
    from concourse.bass_utils import run_bass_kernel_spmd

    pad = EPAD - E
    dst = np.concatenate([np.asarray(inputs["dst"]), np.full(pad, NPAD - 1, np.int32)])
    arrays = {
        "x": inputs["x"],
        "src": np.concatenate([np.asarray(inputs["src"]), np.full(pad, NPAD - 1, np.int32)]),
        "dst_ext": np.concatenate([np.full(1, -1, np.int32), dst, np.full(1, -1, np.int32)]),
        "edge_weight": np.pad(np.asarray(inputs["edge_weight"]), (0, pad)),
        "edge_attr_t": np.pad(np.asarray(inputs["edge_attr_50"]).T, ((0, 0), (0, pad))),
    }
    arrays.update({n: v for n, v in inputs.items() if n.startswith("L")})
    arrays = {n: np.ascontiguousarray(v) for n, v in arrays.items()}
    nc = bacc.Bacc("TRN2", target_bir_lowering=False, num_devices=1)
    a = {n: nc.dram_tensor("in_" + n, v.shape, mybir.dt.from_np(v.dtype), kind="ExternalInput").ap()
                           for n, v in arrays.items()}
    a["out"] = nc.dram_tensor("out", (N, D), F32, kind="ExternalOutput").ap()
    build(nc, a)
    r = run_bass_kernel_spmd(nc, [{"in_" + n: v for n, v in arrays.items()}], core_ids=[0])
    return r.results[0]["out"]
```

```python
from contextlib import ExitStack

import concourse.bass as bass
from concourse import mybir
from concourse.alu_op_type import AluOpType as ALU

F32, BF16, I32 = mybir.dt.float32, mybir.dt.bfloat16, mybir.dt.int32
ACT = mybir.ActivationFunctionType

P = 128
N, E, D = 50000, 25000, 128
R, M, H = 50, 64, 4
C = M // H
EPS = 1e-5
G = 8
NB = -(-N // (P * G))
NPAD = NB * P * G
COLS = NB * G
LAST = N - (NB - 1) * P * G
LASTP = LAST // G
assert LAST % G == 0 and G == 8 and NPAD > N
ET = -(-E // P)
T = 4
EB = ET // T
EPAD = ET * P
assert ET % T == 0 and EB == NB
W = T * P
EROW = 256
ACC = NPAD + -(-EPAD // (P * G)) * P * G
ER = EPAD // EROW
ZEROED_EARLY = NB // 2
AHEAD = 2
FAR = float(1 << 17)
BIG = 1e30


class Batch:

    def __init__(self, i, unroll, c):
        self.i, self.unroll, self.c, self.n = i, unroll, c, i * unroll + c

    def slot(self, m):
        return self.c % m

    def turn(self, m):
        return self.i * (self.unroll // m) + self.c // m

    def is_last(self, n):
        return isinstance(self.n, int) and self.n == n - 1


def pipeline(eng, n, unroll, depth, body):
    head = unroll * (-(-(depth + 2) // unroll))
    rounds = (n - head) // unroll

    def peeled(s):
        return lambda k: Batch(0, unroll, s - k) if 0 <= s - k < n else None

    for s in range(head):
        body(peeled(s))
    with eng.Fori(0, rounds) as i:
        for u in range(unroll):
            body(lambda k, u=u: Batch(i, unroll, head + u - k))
    for s in range(head + unroll * rounds, n + depth):
        body(peeled(s))


def after(eng, sem, b, lag=0, per=1, n=None):
    value = per * (b.n + 1 - lag)
    if isinstance(value, int):
        if value <= 0:
            return
        value = value if n is None else min(value, per * n)
    eng.wait_ge(sem, value)


def landed(eng, sems, b, per):
    eng.wait_ge(sems[b.slot(len(sems))], per * (b.turn(len(sems)) + 1))


def freed(eng, sems, b, per):
    value = per * b.turn(len(sems))
    if not (isinstance(value, int) and value == 0):
        eng.wait_ge(sems[b.slot(len(sems))], value)


def all_landed(eng, sems, n, per):
    for s in range(len(sems)):
        eng.wait_ge(sems[s], per * ((n + len(sems) - 1 - s) // len(sems)))


class Steps:

    def __init__(self, eng, sem, per):
        self.eng, self.sem, self.per = eng, sem, per

    def start(self, batch):
        self.batch, self.k = batch, 0

    def made(self, instruction):
        instruction.then_inc(self.sem, 1)
        self.k += 1
        self.eng.wait_ge(self.sem, self.batch * self.per + self.k)

    def end(self):
        assert self.k == self.per, (self.k, self.per)


def pass_semaphores(nc, ctx, prefix):
    made = []

    def sem(name):
        made.append(nc.alloc_semaphore(prefix + name))
        return made[-1]

    def clear():
        nc.clear_and_free_semaphores(made)
        nc.all_engine_barrier()

    ctx.callback(clear)
    return sem


def carry(eng, sem):
    eng.sem_inc(sem, 1)


def over_tiles(row, tiles=G):
    return row.unsqueeze(1).broadcast_to([P, tiles, row.shape[-1]])


def over_width(cols, width=D):
    return cols.unsqueeze(2).broadcast_to([P, cols.shape[-1], width])


def table_rows(table, batch, width=D):
    return table[bass.ds(batch * (P * G), P * G), :].rearrange("(p k) d -> p (k d)", p=P)


def flat(tile):
    return tile.rearrange("p k d -> p (k d)")


def zero_rows(sp, k, table, batches, sems, first=0):
    few = len(sems)
    for b in batches:
        n = b - first
        if n >= few:
            sp.wait_ge(sems[n % few], 16 * (n // few))
        sp.dma_start(table_rows(table, b), k["zero"][:, 0:G * table.shape[-1]]).then_inc(sems[n % few], 16)


def node_stats(dve, steps, z, stats, sums, diff):
    for t in range(G):
        last = dve.bn_stats(stats[:, t, :], z[:, t, :])
    steps.made(last)
    dve.tensor_tensor(sums, stats[:, :, 1:3], stats[:, :, 4:6], ALU.add)
    steps.made(dve.tensor_tensor(diff, stats[:, :, 1], stats[:, :, 4], ALU.subtract))
    steps.made(dve.scalar_tensor_tensor(diff, diff, 0.25, diff, ALU.mult, ALU.mult))
    return dve.scalar_tensor_tensor(sums[:, :, 1], sums[:, :, 1], 1.0 / D, diff, ALU.mult, ALU.add)


class NodeInput:

    def __init__(self, sem, n_tables, slots, reads_x=False):
        self.sems = [sem(f"loaded{i}") for i in range(slots)]
        self.per, self.reads_x = 16 * n_tables, reads_x

    def landed(self, eng, b):
        s, turn = b.slot(len(self.sems)), b.turn(len(self.sems))
        more = 16 if self.reads_x and b.is_last(NB) else 0
        eng.wait_ge(self.sems[s], self.per * (turn + 1) + more)

    def load(self, sp, tile, table, b, width=D):
        sem = self.sems[b.slot(len(self.sems))]
        if table.shape[0] >= NPAD or not b.is_last(NB):
            sp.dma_start(flat(tile), table_rows(table, b.n, width)).then_inc(sem, 16)
            return
        rest = table[(NB - 1) * P * G:N, :].rearrange("(p k) d -> p (k d)", k=G)
        sp.dma_start(flat(tile[0:96]), rest[0:96]).then_inc(sem, 16)
        sp.dma_start(flat(tile[96:LASTP]), rest[96:LASTP]).then_inc(sem, 16)


def prepare(nc, k, a):
    with ExitStack() as ctx:
        sb = lambda name, shape, dt=F32: ctx.enter_context(nc.sbuf_tensor(name, shape, dt))
        ps = lambda name, shape: ctx.enter_context(nc.psum_tensor(name, shape, F32))
        sem = pass_semaphores(nc, ctx, "")
        idx_loaded, w_loaded, zero_made, ident_made = sem("idx_loaded"), sem("w_loaded"), sem("zero_made"), sem("ident_made")
        rows_made, turned, cols_made = sem("rows_made"), sem("turned"), sem("cols_made")
        keep_stored, keep_loaded, dve_steps = sem("keep_stored"), sem("keep_loaded"), sem("dve_steps")
        pool_steps, mul_ready, mul_done, const_made = sem("pool_steps"), sem("mul_ready"), sem("mul_done"), sem("const_made")
        wide_loaded = sem("wide_loaded")

        src_i = sb("src_i", [ER, EROW], I32)
        dst_i = sb("dst_i", [ER, EROW + 2], I32)
        part = sb("part", [ER, EROW], I32)
        part2 = sb("part2", [ER, EROW], I32)
        dst_f = sb("dst_f", [ER, EROW + 2])
        rows = sb("rows", [ER, 7, EROW])
        keep_r = sb("keep_r", [ER, EROW], BF16)
        ind = sb("ind", [P, COLS], I32)
        own, own_f = sb("own", [P, ET], I32), sb("own_f", [P, ET])
        wn2m, wedge = sb("wn2m", [P, M]), sb("wedge", [R, M])
        wqkv = sb("wqkv", [M, 3, M])
        we, wskip = sb("we", [M, M]), sb("wskip", [M, M])
        wbeta = sb("wbeta", [M, 3])
        bskip_c = sb("bskip_c", [M, 1])
        n2m_t, edge_t, skip_t = sb("n2m_t", [M, P]), sb("edge_t", [M, R]), sb("skip_t", [M, M])
        rhs_v = sb("rhs_v", [M, 2 * M])
        rhs_e = sb("rhs_e", [M, 2 * M])
        rhs_r = sb("rhs_r", [M, M + 1])
        wdiff = sb("wdiff", [M, 1])
        wsum = sb("wsum", [M, 1])
        rb1 = sb("rb1", [P, 1])
        bias_hi, bias_mid = sb("bias_hi", [P, P], BF16), sb("bias_mid", [P, P], BF16)
        bias_a, bias_b = sb("bias_a", [P, P]), sb("bias_b", [P, P])
        lhs = sb("lhs", [P, 3, P])
        bank = [ps(f"turn_{i}", [P, 512]) for i in range(2)]
        mm = [ps(f"product_{i}", [P, 512]) for i in range(5)]
        block = ctx.enter_context(nc.Block())

        @block.sync
        def _(sp):
            ext = a["dst_ext"]
            sp.dma_start(dst_i[:, 1:EROW + 1], ext[1:EPAD + 1].rearrange("(r c) -> r c", c=EROW)).then_inc(idx_loaded, 16)
            sp.dma_start(dst_i[:, 0:1], ext[0:EPAD].rearrange("(r c) -> r c", c=EROW)[:, 0:1],
                         allow_slow_non_contiguous=True).then_inc(idx_loaded, 16)
            sp.dma_start(dst_i[:, EROW + 1:EROW + 2], ext[2:EPAD + 2].rearrange("(r c) -> r c", c=EROW)[:, EROW - 1:EROW],
                         allow_slow_non_contiguous=True).then_inc(idx_loaded, 16)
            sp.dma_start(src_i[:], a["src"].rearrange("(r c) -> r c", c=EROW)).then_inc(idx_loaded, 16)
            sp.dma_start(rows[:, 3, :], a["edge_weight"].rearrange("(r c) -> r c", c=EROW)).then_inc(idx_loaded, 16)
            sp.wait_ge(zero_made, 1)
            zero_rows(sp, k, k["agg"], range(ZEROED_EARLY), k["agg_zeroed"])
            sp.wait_ge(idx_loaded, 16 * 5)

        weights = [(k["w_pre"], a["L0_gnn_W_pre"]), (k["w1"], a["L0_gnn_W1"]), (k["w2"], a["L0_gnn_W2"]), (k["w_l1"], a["L1_gnn_W"]),
                   (k["w_m2n"][0:M, :], a["L2_gnn_W_m2n"]), (k["w_m2n"][M:2 * M, :], a["L2_gnn_W_m2n"]), (k["w1_l3"], a["L3_gnn_W1"]), (k["w2_l3"], a["L3_gnn_W2"]),
                   (wn2m, a["L2_gnn_W_n2m"]), (wedge, a["L2_gnn_W_edge"]), (we, a["L2_gnn_W_e"]), (wskip, a["L2_gnn_W_skip"]),
                   (wqkv[:, 0, :], a["L2_gnn_W_q"]), (wqkv[:, 1, :], a["L2_gnn_W_v"]), (wqkv[:, 2, :], a["L2_gnn_W_k"]),
                   (wbeta, a["L2_gnn_W_beta"].rearrange("(j m) o -> m (j o)", m=M))]
        columns = [(k["b_pre_c"], a["L0_gnn_b_pre"]), (k["b1_c"], a["L0_gnn_b1"]), (bskip_c, a["L2_gnn_b_skip"])]
        wide = [(k["b2_r"], a["L0_gnn_b2"]), (k["gamma0_r"], a["L0_gnn_gamma"]), (k["beta0_r"], a["L0_gnn_beta"]), (k["b_pre_r"], a["L0_gnn_b_pre"]),
                (k["b_l1_r"], a["L1_gnn_b"]), (k["gamma1_r"], a["L1_gnn_gamma"]), (k["beta1_r"], a["L1_gnn_beta"]), (k["b1_l3_r"], a["L3_gnn_b1"]), (k["b2_l3_r"], a["L3_gnn_b2"])]
        n_weights = len(weights) + len(columns) + 1 + 2

        @block.scalar
        def _(act):
            with nc.allow_non_contiguous_dma(reason="vectors of a few hundred bytes, once"):
                for tile, source in weights:
                    act.dma_start(tile if isinstance(tile, bass.AP) else tile[:], source).then_inc(w_loaded, 16)
                for tile, source in columns:
                    act.dma_start(tile[:], source.unsqueeze(1)).then_inc(w_loaded, 16)
                act.wait_ge(const_made, 1)
                act.dma_start(k["b_q"][M:2 * M, :], a["L2_gnn_b_q"].unsqueeze(1)).then_inc(w_loaded, 16)
                act.dma_start(k["w_ev"][R:R + 1, 0:M], a["L2_gnn_b_v"].unsqueeze(0)).then_inc(w_loaded, 16)
                act.dma_start(k["w_ev"][R:R + 1, M:2 * M], a["L2_gnn_b_k"].unsqueeze(0)).then_inc(w_loaded, 16)
                for tile, source in wide:
                    act.dma_start(tile[:], source.partition_broadcast(P)).then_inc(wide_loaded, 16)
            act.wait_ge(rows_made, 1)
            act.dma_start(k["keep_dram"].rearrange("(r c) -> r c", c=EROW), keep_r[:]).then_inc(keep_stored, 16)
            act.wait_ge(keep_stored, 16)
            act.dma_start(k["keep"][:], k["keep_dram"].partition_broadcast(P)).then_inc(keep_loaded, 16)
            act.wait_ge(keep_loaded, 16)
            act.wait_ge(w_loaded, 16 * n_weights)
            act.wait_ge(wide_loaded, 16 * len(wide))

        @block.gpsimd
        def _(pool):
            pool.memset(k["zero"][:], 0.0).then_inc(zero_made, 1)
            pool.memset(k["ident"][:], 0.0).then_inc(pool_steps, 1)
            pool.wait_ge(pool_steps, 1)
            pool.affine_select(out=k["ident"][:], in_=k["ident"][:], compare_op=ALU.not_equal, fill=1.0, base=0,
                               pattern=[[-1, P]], channel_multiplier=1).then_inc(ident_made, 1)
            pool.iota(own[:], pattern=[[P, ET]], base=NPAD, channel_multiplier=1)
            pool.iota(ind[:], pattern=[[1, COLS]], base=0, channel_multiplier=0).then_inc(ident_made, 1)
            pool.memset(k["head_sum"][:], 1.0).then_inc(pool_steps, 1)
            pool.wait_ge(pool_steps, 2)
            pool.affine_select(out=k["head_sum"][:], in_=k["head_sum"][:], compare_op=ALU.is_ge, fill=0.0, base=-M,
                               pattern=[[-C, H]], channel_multiplier=1).then_inc(pool_steps, 1)
            pool.wait_ge(pool_steps, 3)
            pool.affine_select(out=k["head_sum"][:], in_=k["head_sum"][:], compare_op=ALU.is_ge, fill=0.0, base=M + C - 1,
                               pattern=[[C, H]], channel_multiplier=-1).then_inc(ident_made, 1)
            pool.memset(k["head_spread"][:], 1.0).then_inc(pool_steps, 1)
            pool.wait_ge(pool_steps, 4)
            pool.affine_select(out=k["head_spread"][:], in_=k["head_spread"][:], compare_op=ALU.is_ge, fill=0.0, base=0,
                               pattern=[[1, M]], channel_multiplier=-C).then_inc(pool_steps, 1)
            pool.wait_ge(pool_steps, 5)
            pool.affine_select(out=k["head_spread"][:], in_=k["head_spread"][:], compare_op=ALU.is_ge, fill=0.0, base=C - 1,
                               pattern=[[-1, M]], channel_multiplier=C).then_inc(ident_made, 1)
            pool.memset(k["valid"][:], 1.0).then_inc(pool_steps, 1)
            pool.wait_ge(pool_steps, 6)
            pool.affine_select(out=k["valid"][:, COLS - G:COLS], in_=k["valid"][:, COLS - G:COLS], compare_op=ALU.is_ge, fill=0.0,
                               base=LAST - 1, pattern=[[-1, G]], channel_multiplier=-G).then_inc(ident_made, 1)

        def bias_parts(dve, steps, out, row):
            w = row.shape[-1]
            steps.made(dve.tensor_copy(bias_hi[:, 0:w], row))
            steps.made(dve.tensor_tensor(bias_a[:, 0:w], row, bias_hi[:, 0:w], ALU.subtract))
            steps.made(dve.tensor_copy(bias_mid[:, 0:w], bias_a[:, 0:w]))
            steps.made(dve.tensor_tensor(bias_a[:, 0:w], bias_a[:, 0:w], bias_mid[:, 0:w], ALU.subtract))
            steps.made(dve.tensor_scalar(bias_b[:, 0:w], bias_hi[:, 0:w], k["ident"][:, 0:1], None, ALU.mult))
            steps.made(dve.scalar_tensor_tensor(bias_b[:, 0:w], bias_mid[:, 0:w], k["ident"][:, 1:2], bias_b[:, 0:w], ALU.mult, ALU.add))
            steps.made(dve.scalar_tensor_tensor(out, over_tiles(bias_a[:, 0:w], 4), k["ident"][:, 2:3], over_tiles(bias_b[:, 0:w], 4),
                                                ALU.mult, ALU.add))

        tables = [k["src_lo"], k["src_hi"], k["src_c"], k["weight_c"], k["dst_lo"], k["dst_hi"], k["last_c"]]

        @block.vector
        def _(dve):
            steps = Steps(dve, dve_steps, 0)
            steps.start(0)
            for tile in (k["b_q"], k["w_ev"], k["w_q"]):
                last = dve.memset(tile[:], 0.0)
            last.then_inc(const_made, 1)
            dve.memset(k["eps"][:], EPS)
            dve.memset(k["ones_b"][:], 1.0)
            dve.wait_ge(idx_loaded, 16 * 5)
            for at, ids in ((0, src_i[:]), (4, dst_i[:, 1:EROW + 1])):
                steps.made(dve.tensor_scalar(part[:], ids, 3, P - 1, ALU.logical_shift_right, ALU.bitwise_and))
                steps.made(dve.tensor_copy(rows[:, at, :], part[:]))
                steps.made(dve.tensor_scalar(part[:], ids, 10, 3, ALU.logical_shift_right, ALU.logical_shift_left))
                steps.made(dve.tensor_scalar(part2[:], ids, G - 1, None, ALU.bitwise_and))
                steps.made(dve.tensor_tensor(part[:], part[:], part2[:], ALU.bitwise_or))
                steps.made(dve.tensor_copy(rows[:, at + 1, :], part[:]))
            dve.tensor_scalar(rows[:, 2, :], src_i[:], float(N - 1), None, ALU.min)
            steps.made(dve.tensor_copy(dst_f[:], dst_i[:]))
            dve.tensor_tensor(keep_r[:], dst_f[:, 1:EROW + 1], dst_f[:, 0:EROW], ALU.is_equal).then_inc(rows_made, 1)
            steps.made(dve.tensor_tensor(rows[:, 6, :], dst_f[:, 1:EROW + 1], dst_f[:, 2:EROW + 2], ALU.is_equal))
            dve.scalar_tensor_tensor(rows[:, 6, :], rows[:, 6, :], FAR, dst_f[:, 1:EROW + 1], ALU.mult, ALU.add).then_inc(rows_made, 1)
            dve.wait_ge(ident_made, 5)
            dve.tensor_copy(k["count_iota"][:], ind[:])
            steps.made(dve.tensor_copy(own_f[:], own[:]))
            for n, table in enumerate(tables + [k["dst_c"]]):
                dve.wait_ge(turned, n + 1)
                both = bank[n % 2][:, 0:2 * ER].rearrange("p (h r) -> p r h", h=2)
                dve.tensor_copy(table[:].rearrange("p (r h) -> p r h", h=2), both).then_inc(cols_made, 1)
            dve.wait_ge(cols_made, 8)
            dve.tensor_copy(k["gather_i"][:], k["src_c"][:])
            dve.tensor_copy(k["scatter_i"][:], k["last_c"][:])
            steps.made(dve.tensor_tensor(own_f[:], own_f[:], k["last_c"][:], ALU.min))
            dve.tensor_copy(k["accumulate_i"][:], own_f[:])
            dve.tensor_copy(k["dst_i"][:], k["dst_c"][:])
            dve.wait_ge(w_loaded, 16 * n_weights)
            dve.wait_ge(wide_loaded, 16 * len(wide))
            dve.tensor_tensor(wdiff[:], wbeta[:, 1:2], wbeta[:, 2:3], ALU.subtract)
            dve.tensor_tensor(wsum[:], wbeta[:, 0:1], wbeta[:, 2:3], ALU.add)
            dve.tensor_copy(rhs_v[:], wqkv[:, 1:3, :].rearrange("p a b -> p (a b)"))
            dve.tensor_copy(rhs_e[:, 0:M], we[:])
            dve.tensor_copy(rhs_e[:, M:2 * M], we[:])
            dve.tensor_copy(rhs_r[:, 0:M], wskip[:])
            steps.made(dve.tensor_scalar(rb1[:], k["b1_c"][:], 0.0, None, ALU.max))
            dve.tensor_copy(lhs[:, 0, :], rb1[:].broadcast_to([P, P]))
            dve.tensor_copy(lhs[0:M, 1, :], bskip_c[:].broadcast_to([M, P]))
            dve.tensor_copy(lhs[0:M, 2, :], wsum[:].broadcast_to([M, P])).then_inc(mul_ready, 1)
            dve.wait_ge(mul_done, 1)
            dve.tensor_copy(n2m_t[:], mm[0][0:M, 0:P])
            dve.tensor_copy(edge_t[:], mm[1][0:M, 0:R])
            dve.tensor_copy(skip_t[:], mm[2][0:M, 0:M]).then_inc(mul_ready, 1)
            dve.wait_ge(mul_done, 2)
            dve.tensor_copy(rhs_r[:, M:M + 1], mm[3][0:M, 0:1]).then_inc(mul_ready, 1)
            dve.wait_ge(mul_done, 3)
            dve.tensor_scalar(k["w_q"][:, M:2 * M], mm[0][:, 0:M], float(C) ** -0.5, None, ALU.mult)
            dve.tensor_copy(k["w_vk"][:], mm[1][:, 0:2 * M])
            dve.tensor_copy(k["w_ev"][0:R, :], mm[2][0:R, 0:2 * M])
            dve.tensor_copy(k["w_r"][:], mm[3][:, 0:M + 1])
            dve.tensor_copy(k["b_r"][:], mm[4][:, 0:M + 1])
            dve.tensor_copy(k["w_out"][:], mm[4][:, 128:128 + M])
            steps.made(dve.tensor_tensor(k["none0_r"][:], mm[4][:, 256:256 + D], k["b2_r"][:], ALU.add))
            steps.made(dve.tensor_scalar(k["none0_r"][:], k["none0_r"][:], 0.0, None, ALU.max))
            steps.made(dve.tensor_tensor(k["b_pre_r"][:], k["b_pre_r"][:], k["none0_r"][:], ALU.add))
            dve.tensor_scalar(k["b_q"][:], k["b_q"][:], float(C) ** -0.5, None, ALU.mult)
            for out, row in ((k["bias_h"], k["b_pre_r"][:]), (k["bias_l1"], k["b_l1_r"][:]), (k["bias_r"], k["b_r"][:])):
                bias_parts(dve, steps, out[:], row)

        @block.tensor
        def _(pe):
            pe.wait_ge(ident_made, 5)
            pe.wait_ge(rows_made, 2)
            sources = [rows[:, i, :] for i in range(7)] + [dst_f[:, 1:EROW + 1]]
            for n, source in enumerate(sources):
                if n >= 2:
                    pe.wait_ge(cols_made, n - 1)
                for h in range(2):
                    last = pe.transpose(bank[n % 2][:, h * ER:(h + 1) * ER], source[:, h * P:(h + 1) * P],
                                        k["ident"][0:ER, 0:ER])
                last.then_inc(turned, 1)
            pe.wait_ge(mul_ready, 1)
            pe.transpose(mm[0][0:M, 0:P], wn2m[:], k["ident"][:])
            pe.transpose(mm[1][0:M, 0:R], wedge[:], k["ident"][0:R, 0:R])
            pe.transpose(mm[2][0:M, 0:M], wskip[:], k["ident"][0:M, 0:M]).then_inc(mul_done, 1)
            pe.wait_ge(mul_ready, 2)
            pe.matmul(mm[3][0:M, 0:1], skip_t[:], wdiff[:], start=True, stop=True).then_inc(mul_done, 1)
            pe.wait_ge(mul_ready, 3)
            pe.matmul(mm[0][:, 0:M], n2m_t[:], wqkv[:, 0, :], start=True, stop=True)
            pe.matmul(mm[1][:, 0:2 * M], n2m_t[:], rhs_v[:], start=True, stop=True)
            pe.matmul(mm[2][0:R, 0:2 * M], edge_t[:], rhs_e[:], start=True, stop=True)
            pe.matmul(mm[3][:, 0:M + 1], n2m_t[:], rhs_r[:], start=True, stop=True)
            pe.matmul(mm[4][:, 0:M], lhs[0:M, 1, :], k["ident"][0:M, 0:M], start=True, stop=True)
            pe.matmul(mm[4][:, M:M + 1], lhs[0:M, 1, :], wdiff[:], start=True, stop=True)
            pe.matmul(mm[4][:, 128:128 + M], lhs[0:M, 2, :], k["ident"][0:M, 0:M], start=True, stop=True)
            pe.matmul(mm[4][:, 256:256 + D], lhs[:, 0, :], k["w2"][:], start=True, stop=True).then_inc(mul_done, 1)


def scatter_rows(pool, table, rows, indices, landed):
    for t in range(T):
        pool.indirect_dma_start(table, bass.IndirectOffsetOnAxis(indices[:, t:t + 1], 0), rows[:, t, :], None,
                                bounds_check=NPAD - 1, oob_is_err=False).then_inc(landed, 16)


def accumulate_rows(pool, table, rows, indices, landed):
    for t in range(T):
        pool.indirect_dma_start(table, bass.IndirectOffsetOnAxis(indices[:, t:t + 1], 0), rows[:, t, :], None,
                                compute_op=ALU.add).then_inc(landed, 16)


def gather_rows(pool, rows, table, indices, landed):
    for t in range(T):
        pool.indirect_dma_start(rows[:, t, :], None, table,
                                bass.IndirectOffsetOnAxis(indices[:, t:t + 1], 0)).then_inc(landed, 16)


def edges_layer0(nc, k, a):
    with ExitStack() as ctx:
        sb = lambda name, shape, dt=F32: ctx.enter_context(nc.sbuf_tensor(name, shape, dt))
        ps = lambda name, shape: ctx.enter_context(nc.psum_tensor(name, shape, F32))
        sem = pass_semaphores(nc, ctx, "")
        index_ready, sindex_ready, turned, xt_ready, h_done, h_ready = map(sem, ("e0_index", "e0_sindex", "e0_turned", "e0_xt", "e0_h_done", "e0_h"))
        summed, r_done, r_ready, out_done, out_ready = map(sem, ("e0_summed", "e0_r_done", "e0_r", "e0_out_done", "e0_out"))
        hot_ready, hot_used, out_steps, degree_steps, counted, const = map(sem, ("e0_hot", "e0_hot_used", "e0_out_steps", "e0_degree_steps", "e0_counted", "e0_const"))
        deg_ready, deg_root = sem("e0_deg"), sem("e0_root")
        gathered = [sem(f"e0_gathered{i}") for i in range(2)]
        scattered = [sem(f"e0_scattered{i}") for i in range(2)]
        agg_m_zeroed = [sem(f"agg_m_zeroed{i}") for i in range(2)]
        own_zeroed = [sem(f"own_zeroed{i}") for i in range(2)]
        issued = sem("issued")
        gi, si = sb("gi", [P, 2, T], I32), sb("si", [P, 2, T], I32)
        rows = sb("rows0", [P, 2, T, D])
        xt, hs, agg, r1, out = (sb(x, [P, 2, W]) for x in ("xt", "hs", "aggs", "r1", "e0_rows_out"))
        lo = sb("lo", [P, 2, 2 * T, P], BF16)
        hi = sb("hi", [P, 2, 2 * T, COLS], BF16)
        zero_b = sb("zero_b", [P, COLS], BF16)
        deg = sb("deg", [P, 3, COLS])
        p_t, p_h, p_r, p_o = (ps(x, [P, W]) for x in ("p_t", "p_h", "p_r", "p_o"))
        p_count = [ps("p_count_src", [P, 512]), ps("p_count_dst", [P, 512])]
        block = ctx.enter_context(nc.Block())
        DEPTH = 4

        @block.sync
        def _(sp):
            zero_rows(sp, k, k["agg"], range(ZEROED_EARLY, NB), k["agg_zeroed"])
            zero_rows(sp, k, k["agg_m"], range(NB), agg_m_zeroed)
            all_landed(sp, agg_m_zeroed, NB, 16)
            zero_rows(sp, k, k["acc"], range(NB, ACC // (P * G)), own_zeroed, first=NB)
            all_landed(sp, own_zeroed, ACC // (P * G) - NB, 16)

        @block.gpsimd
        def _(pool):
            pool.memset(agg[:, 1, W - 1:W], 0.0).then_inc(const, 1)
            pool.memset(zero_b[:], 0.0).then_inc(const, 1)

            def step(at):
                if b := at(1):
                    s = b.slot(2)
                    after(pool, index_ready, b)
                    after(pool, turned, b, lag=2)
                    carry(pool, issued)
                    gather_rows(pool, rows[:, s], a["x"], gi[:, s], gathered[s])
                if b := at(4):
                    s = b.slot(2)
                    after(pool, sindex_ready, b)
                    after(pool, out_ready, b)
                    all_landed(pool, k["agg_zeroed"], NB, 16)
                    carry(pool, issued)
                    scatter_rows(pool, k["agg"], out[:, s].rearrange("p (t d) -> p t d", t=T), si[:, s], scattered[s])
            pipeline(pool, EB, 2, DEPTH, step)
            all_landed(pool, scattered, EB, 16 * T)

        @block.tensor
        def _(pe):
            pe.wait_ge(const, 2)
            for c in range(2):
                pe.matmul(p_count[c][:, 0:COLS], zero_b[:, 0:P], zero_b[:], start=True, stop=False)

            def step(at):
                if b := at(3):
                    s = b.slot(2)
                    after(pe, summed, b)
                    after(pe, r_ready, b, lag=1)
                    pe.matmul(p_r[:], k["w1"][:], agg[:, s, :], start=True, stop=True).then_inc(r_done, 1)
                if b := at(2):
                    s = b.slot(2)
                    landed(pe, gathered, b, 16 * T)
                    after(pe, xt_ready, b, lag=1)
                    for t in range(T):
                        last = pe.transpose(p_t[:, t * P:(t + 1) * P], rows[:, s, t, :], k["ident"][:])
                    last.then_inc(turned, 1)
                if b := at(3):
                    s = b.slot(2)
                    after(pe, r_ready, b)
                    after(pe, out_ready, b, lag=1)
                    for t in range(T):
                        last = pe.matmul(p_o[:, t * P:(t + 1) * P], r1[:, s, t * P:(t + 1) * P], k["w2"][:], start=True, stop=True)
                    last.then_inc(out_done, 1)
                if b := at(2):
                    s = b.slot(2)
                    after(pe, xt_ready, b)
                    after(pe, h_ready, b, lag=1)
                    pe.matmul(p_h[:], k["w_pre"][:], xt[:, s, :], start=True, stop=True).then_inc(h_done, 1)
                if b := at(1):
                    s = b.slot(2)
                    after(pe, hot_ready, b)
                    for c in range(2):
                        for t in range(T):
                            last = pe.matmul(p_count[c][:, 0:COLS], lo[:, s, c * T + t, :], hi[:, s, c * T + t, :],
                                             start=False, stop=False)
                    last.then_inc(hot_used, 1)
            pipeline(pe, EB, 2, DEPTH, step)
            for c in range(2):
                last = pe.matmul(p_count[c][:, 0:COLS], zero_b[:, 0:P], zero_b[:], start=False, stop=True)
            last.then_inc(counted, 1)

        @block.scalar
        def _(act):
            def step(at):
                if b := at(2):
                    s = b.slot(2)
                    after(act, turned, b)
                    after(act, h_done, b, lag=2)
                    act.activation(xt[:, s, :], p_t[:], ACT.Copy).then_inc(xt_ready, 1)
                if b := at(3):
                    s = b.slot(2)
                    after(act, r_done, b)
                    after(act, out_done, b, lag=2)
                    act.activation(r1[:, s, :], p_r[:], ACT.Relu, bias=k["b1_c"][:]).then_inc(r_ready, 1)
                if b := at(2):
                    s = b.slot(2)
                    after(act, h_done, b)
                    after(act, summed, b, lag=2)
                    act.activation(hs[:, s, :], p_h[:], ACT.Identity, bias=k["b_pre_c"][:]).then_inc(h_ready, 1)
            pipeline(act, EB, 2, DEPTH, step)
            act.wait_ge(deg_ready, 1)
            act.activation(k["dinv_src"][:], deg[:, 0, :], ACT.Sqrt)
            act.activation(k["dinv_dst"][:], deg[:, 1, :], ACT.Sqrt).then_inc(deg_root, 1)

        @block.vector
        def _(dve):
            out_steps_ = Steps(dve, out_steps, 1)
            dve.wait_ge(const, 1)

            def step(at):
                if b := at(0):
                    s = b.slot(2)
                    freed(dve, gathered, b, 16 * T)
                    dve.tensor_copy(gi[:, s, :], k["gather_i"][:, bass.ds(b.n * T, T)]).then_inc(index_ready, 1)
                if b := at(3):
                    s = b.slot(2)
                    freed(dve, scattered, b, 16 * T)
                    dve.tensor_copy(si[:, s, :], k["scatter_i"][:, bass.ds(b.n * T, T)]).then_inc(sindex_ready, 1)
                if b := at(2):
                    s = b.slot(2)
                    after(dve, h_ready, b)
                    after(dve, r_done, b, lag=2)
                    after(dve, summed, b, lag=1)
                    dve.tensor_tensor_scan(agg[:, s, :], k["keep"][:, bass.ds(b.n * W, W)], hs[:, s, :],
                                           agg[:, 1 - s, W - 1:W], ALU.mult, ALU.add).then_inc(summed, 1)
                if b := at(3):
                    s = b.slot(2)
                    after(dve, out_done, b)
                    freed(dve, scattered, b, 16 * T)
                    out_steps_.start(b.n)
                    tiles = lambda x: x.rearrange("p (t d) -> p t d", t=T)
                    out_steps_.made(dve.tensor_tensor(tiles(out[:, s, :]), tiles(p_o[:]), over_tiles(k["b2_r"][:], T), ALU.add))
                    dve.scalar_tensor_tensor(tiles(out[:, s, :]), tiles(out[:, s, :]), 0.0, over_tiles(k["none0_r"][:], T),
                                             ALU.max, ALU.subtract).then_inc(out_ready, 1)
                if b := at(0):
                    s = b.slot(2)
                    after(dve, hot_used, b, lag=2)
                    for c, (table_lo, table_hi) in enumerate(((k["src_lo"], k["src_hi"]), (k["dst_lo"], k["dst_hi"]))):
                        for t in range(T):
                            dve.tensor_scalar(lo[:, s, c * T + t, :], k["count_iota"][:, 0:P], table_lo[:, bass.ds(b.n * T + t, 1)], None, ALU.is_equal)
                            last = dve.tensor_scalar(hi[:, s, c * T + t, :], k["count_iota"][:], table_hi[:, bass.ds(b.n * T + t, 1)], None, ALU.is_equal)
                    last.then_inc(hot_ready, 1)
            pipeline(dve, EB, 2, DEPTH, step)
            dve.wait_ge(counted, 1)
            dve.tensor_scalar(deg[:, 0, :], p_count[0][:, 0:COLS], 1.0, None, ALU.add)
            dve.tensor_scalar(deg[:, 1, :], p_count[1][:, 0:COLS], 1.0, None, ALU.add).then_inc(deg_ready, 1)
            dve.wait_ge(deg_root, 1)
            dve.reciprocal(k["dinv_src"][:], k["dinv_src"][:]).then_inc(degree_steps, 1)
            dve.reciprocal(k["dinv_dst"][:], k["dinv_dst"][:]).then_inc(degree_steps, 1)
            dve.wait_ge(degree_steps, 2)
            dve.tensor_tensor(k["sum_w"][:], k["dinv_src"][:], k["valid"][:], ALU.mult).then_inc(degree_steps, 1)


def edges_sum(nc, k, name, source, weighted, onto_source=False, with_residual=False):
    with ExitStack() as ctx:
        sb = lambda n, shape, dt=F32: ctx.enter_context(nc.sbuf_tensor(name + n, shape, dt))
        ps = lambda n, shape: ctx.enter_context(nc.psum_tensor(name + n, shape, F32))
        sem = pass_semaphores(nc, ctx, name)
        index_ready, sindex_ready, scaled, turned, summed, back, out_ready, const = map(
            sem, ("index", "sindex", "scaled", "turned", "summed", "back", "out_ready", "const"))
        gathered = [sem(f"gathered{i}") for i in range(2)]
        scattered = [sem(f"scattered{i}") for i in range(2)]
        issued = sem("issued")
        gi, si = sb("gi", [P, 2, T], I32), sb("si", [P, 2, T], I32)
        rows = sb("rows", [P, 2, T, D])
        agg, out = sb("sums", [P, 2, W]), sb("out", [P, 2, W])
        p_t, p_o = [ps(f"p_t{i}", [P, W]) for i in range(2)], [ps(f"p_o{i}", [P, W]) for i in range(2)]
        rows_to = k["accumulate_i"] if onto_source else k["scatter_i"]
        if with_residual:
            nodes = NodeInput(sem, 2, 2)
            part_stored = [sem(f"part_stored{i}") for i in range(2)]
            scaled_part, part_ready = sem("scaled_part"), sem("part_ready")
            x, part = sb("x", [P, 2, G, D]), sb("part", [P, 2, G, D])
        block = ctx.enter_context(nc.Block())
        DEPTH = 4

        @block.sync
        def _(sp):
            def step(at):
                if b := at(0):
                    s = b.slot(2)
                    freed(sp, part_stored, b, 16)
                    nodes.load(sp, x[:, s], k["x3"], b)
                    nodes.load(sp, part[:, s], source, b)
                if b := at(1):
                    after(sp, part_ready, b)
                    sp.dma_start(table_rows(k["part"], b.n), flat(part[:, b.slot(2)])).then_inc(part_stored[b.slot(2)], 16)
            if with_residual:
                pipeline(sp, NB, 2, DEPTH, step)
                all_landed(sp, part_stored, NB, 16)

        @block.gpsimd
        def _(pool):
            pool.memset(agg[:, 1, W - 1:W], 0.0).then_inc(const, 1)

            def step(at):
                if b := at(1):
                    s = b.slot(2)
                    after(pool, index_ready, b)
                    after(pool, turned, b, lag=2)
                    carry(pool, issued)
                    gather_rows(pool, rows[:, s], source, gi[:, s], gathered[s])
                if b := at(4):
                    s = b.slot(2)
                    after(pool, sindex_ready, b)
                    after(pool, out_ready, b)
                    carry(pool, issued)
                    sums = out[:, s].rearrange("p (t d) -> p t d", t=T)
                    if onto_source:
                        accumulate_rows(pool, k["acc"], sums, si[:, s], scattered[s])
                    else:
                        scatter_rows(pool, k["agg"], sums, si[:, s], scattered[s])
            pipeline(pool, EB, 2, DEPTH, step)
            all_landed(pool, scattered, EB, 16 * T)

        @block.tensor
        def _(pe):
            def step(at):
                if b := at(3):
                    s = b.slot(2)
                    after(pe, summed, b)
                    after(pe, out_ready, b, lag=2)
                    for t in range(T):
                        last = pe.transpose(p_o[s][:, t * P:(t + 1) * P], agg[:, s, t * P:(t + 1) * P], k["ident"][:])
                    last.then_inc(back, 1)
                if b := at(2):
                    s = b.slot(2)
                    if weighted:
                        after(pe, scaled, b)
                    else:
                        landed(pe, gathered, b, 16 * T)
                    after(pe, summed, b, lag=2)
                    for t in range(T):
                        last = pe.transpose(p_t[s][:, t * P:(t + 1) * P], rows[:, s, t, :], k["ident"][:])
                    last.then_inc(turned, 1)
            pipeline(pe, EB, 2, DEPTH, step)

        @block.scalar
        def _(act):
            def step(at):
                if b := at(3):
                    s = b.slot(2)
                    after(act, back, b)
                    freed(act, scattered, b, 16 * T)
                    act.activation(out[:, s, :], p_o[s][:], ACT.Copy).then_inc(out_ready, 1)
            pipeline(act, EB, 2, DEPTH, step)

        @block.vector
        def _(dve):
            dve.wait_ge(const, 1)

            def step(at):
                if b := at(0):
                    s = b.slot(2)
                    freed(dve, gathered, b, 16 * T)
                    dve.tensor_copy(gi[:, s, :], k["gather_i"][:, bass.ds(b.n * T, T)]).then_inc(index_ready, 1)
                if b := at(3):
                    s = b.slot(2)
                    freed(dve, scattered, b, 16 * T)
                    dve.tensor_copy(si[:, s, :], rows_to[:, bass.ds(b.n * T, T)]).then_inc(sindex_ready, 1)
                if b := at(2):
                    s = b.slot(2)
                    if weighted:
                        landed(dve, gathered, b, 16 * T)
                        dve.tensor_tensor(rows[:, s], rows[:, s], over_width(k["weight_c"][:, bass.ds(b.n * T, T)]),
                                          ALU.mult).then_inc(scaled, 1)
                    after(dve, turned, b)
                    after(dve, back, b, lag=2)
                    after(dve, summed, b, lag=1)
                    dve.tensor_tensor_scan(agg[:, s, :], k["keep"][:, bass.ds(b.n * W, W)], p_t[s][:],
                                           agg[:, 1 - s, W - 1:W], ALU.mult, ALU.add).then_inc(summed, 1)
                if b := with_residual and at(1):
                    s = b.slot(2)
                    nodes.landed(dve, b)
                    for t in range(G):
                        last = dve.scalar_tensor_tensor(part[:, s, t, :], part[:, s, t, :], k["dinv_dst"][:, bass.ds(b.n * G + t, 1)], x[:, s, t, :],
                                                        ALU.mult, ALU.add)
                    last.then_inc(scaled_part, 1)
                    after(dve, scaled_part, b)
                    dve.tensor_tensor(part[:, s], part[:, s], over_tiles(k["b2_l3_r"][:]), ALU.add).then_inc(part_ready, 1)
            pipeline(dve, EB, 2, DEPTH, step)


def edges_attention(nc, k, a):
    with ExitStack() as ctx:
        sb = lambda n, shape, dt=F32: ctx.enter_context(nc.sbuf_tensor("at_" + n, shape, dt))
        ps = lambda n, shape: ctx.enter_context(nc.psum_tensor("at_" + n, shape, F32))
        sem = pass_semaphores(nc, ctx, "at_")
        (index_ready, sindex_ready, src_turned, dst_turned, src_ready, dst_ready, vk_done, vk_ready, q_done, product_ready,
         alpha_done, exp_in, exp_ready, spread, weighted, summed, den_summed, back, out_ready, const, max_steps, out_steps) = map(
            sem, ("index", "sindex", "src_turned", "dst_turned", "src_ready", "dst_ready", "vk_done", "vk_ready", "q_done",
                  "product", "alpha", "exp_in", "exp_ready", "spread", "weighted", "summed", "den_summed", "back", "out_ready",
                  "const", "max_steps", "out_steps"))
        U = 4
        gathered = [sem(f"gathered{i}") for i in range(2)]
        attr_loaded = [sem(f"attr{i}") for i in range(U)]
        scattered = [sem(f"scattered{i}") for i in range(2)]
        issued = sem("issued")
        pe_issued = sem("pe_issued")
        gi, di, si = (sb(x, [P, 2, T], I32) for x in ("gi", "di", "si"))
        src_rows, dst_rows = sb("src_rows", [P, 2, T, D]), sb("dst_rows", [P, 2, T, D])
        src_t, dst_t = sb("src_t", [P, 2, W]), sb("dst_t", [P, 2, W])
        attr = sb("attr", [R + 1, U, W])
        vk = sb("vk", [P, U, W])
        product = sb("product", [P, 2, W])
        restart = sb("restart", [H, W])
        top = sb("top", [H, 2, W + 1])
        change = sb("change", [H, 2, 2, W])
        v_w = sb("v_w", [M, 2, W])
        acc, den = sb("acc", [M, 2, W]), sb("den", [H, 2, W])
        inv = sb("inv", [P, 2, T, H])
        out = sb("out", [P, 2, T, M])
        p_a, p_b, p_q, p_vk, p_alpha, p_p, p_d, p_o = (ps(x, [P, W]) for x in ("p_a", "p_b", "p_q", "p_vk", "p_alpha", "p_p", "p_d", "p_o"))
        block = ctx.enter_context(nc.Block())
        DEPTH = 6

        @block.sync
        def _(sp):
            sp.wait_ge(const, 1)

            def step(at):
                if b := at(1):
                    s = b.slot(2)
                    after(sp, vk_done, b, lag=U)
                    sp.dma_start(attr[0:R, b.slot(U), :], a["edge_attr_t"][:, bass.ds(b.n * W, W)]).then_inc(attr_loaded[b.slot(U)], 16)
            pipeline(sp, EB, U, DEPTH, step)

        @block.gpsimd
        def _(pool):
            pool.memset(attr[:], 1.0).then_inc(const, 1)
            pool.memset(top[:, 1, W:W + 1], 0.0).then_inc(const, 1)
            pool.memset(acc[:, 1, W - 1:W], 0.0).then_inc(const, 1)
            pool.memset(den[:, 1, W - 1:W], 0.0).then_inc(const, 1)

            def step(at):
                if b := at(1):
                    s = b.slot(2)
                    after(pool, index_ready, b)
                    after(pool, src_turned, b, lag=2)
                    after(pool, dst_turned, b, lag=2)
                    carry(pool, issued)
                    gather_rows(pool, src_rows[:, s], k["x2"], gi[:, s], gathered[s])
                    gather_rows(pool, dst_rows[:, s], k["x2"], di[:, s], gathered[s])
                if b := at(6):
                    s = b.slot(2)
                    after(pool, sindex_ready, b)
                    after(pool, out_ready, b)
                    carry(pool, issued)
                    scatter_rows(pool, k["agg_m"], out[:, s], si[:, s], scattered[s])
            pipeline(pool, EB, U, DEPTH, step)
            all_landed(pool, scattered, EB, 16 * T)

        @block.tensor
        def _(pe):
            def step(at):
                if b := at(5):
                    s = b.slot(2)
                    after(pe, summed, b)
                    after(pe, den_summed, b)
                    after(pe, out_ready, b, lag=1)
                    carry(pe, pe_issued)
                    for t in range(T):
                        pe.transpose(p_o[:, t * M:(t + 1) * M], acc[:, s, t * P:(t + 1) * P], k["ident"][0:M, 0:M])
                    for t in range(T):
                        last = pe.transpose(p_o[:, T * M + t * H:T * M + (t + 1) * H], den[:, s, t * P:(t + 1) * P], k["ident"][0:H, 0:H])
                    last.then_inc(back, 1)
                if b := at(3):
                    s = b.slot(2)
                    after(pe, product_ready, b)
                    after(pe, exp_in, b, lag=1)
                    pe.matmul(p_alpha[0:H, :], k["head_sum"][:], product[:, s, :], start=True, stop=True).then_inc(alpha_done, 1)
                if b := at(4):
                    s = b.slot(2)
                    after(pe, exp_ready, b)
                    after(pe, weighted, b, lag=1)
                    after(pe, summed, b, lag=1)
                    pe.matmul(p_p[0:M, :], k["head_spread"][:], change[:, s, 1, :], start=True, stop=True)
                    pe.matmul(p_d[0:M, :], k["head_spread"][:], change[:, s, 0, :], start=True, stop=True).then_inc(spread, 1)
                if b := at(2):
                    s = b.slot(2)
                    landed(pe, gathered, b, 2 * 16 * T)
                    after(pe, src_ready, b, lag=1)
                    for t in range(T):
                        last = pe.transpose(p_a[:, t * P:(t + 1) * P], src_rows[:, s, t, :], k["ident"][:])
                    last.then_inc(src_turned, 1)
                    after(pe, dst_ready, b, lag=1)
                    for t in range(T):
                        last = pe.transpose(p_b[:, t * P:(t + 1) * P], dst_rows[:, s, t, :], k["ident"][:])
                    last.then_inc(dst_turned, 1)
                    landed(pe, attr_loaded, b, 16)
                    after(pe, src_ready, b)
                    after(pe, vk_ready, b, lag=1)
                    pe.matmul(p_vk[:], k["w_vk"][:], src_t[:, s, :], start=True, stop=False)
                    pe.matmul(p_vk[:], k["w_ev"][:], attr[:, b.slot(U), :], start=False, stop=True).then_inc(vk_done, 1)
                    after(pe, dst_ready, b)
                    after(pe, product_ready, b, lag=1)
                    pe.matmul(p_q[:], k["w_q"][:], dst_t[:, s, :], start=True, stop=True).then_inc(q_done, 1)
            pipeline(pe, EB, U, DEPTH, step)

        @block.scalar
        def _(act):
            def step(at):
                if b := at(2):
                    s = b.slot(2)
                    after(act, src_turned, b)
                    after(act, vk_done, b, lag=2)
                    act.activation(src_t[:, s, :], p_a[:], ACT.Copy).then_inc(src_ready, 1)
                    after(act, dst_turned, b)
                    after(act, q_done, b, lag=2)
                    act.activation(dst_t[:, s, :], p_b[:], ACT.Copy).then_inc(dst_ready, 1)
                    after(act, vk_done, b)
                    after(act, weighted, b, lag=U)
                    act.activation(vk[:, b.slot(U), :], p_vk[:], ACT.Copy).then_inc(vk_ready, 1)
                if b := at(3):
                    s = b.slot(2)
                    after(act, exp_in, b)
                    act.activation(change[:, s], change[:, s], ACT.Exp).then_inc(exp_ready, 1)
            pipeline(act, EB, U, DEPTH, step)

        @block.vector
        def _(dve):
            dve.wait_ge(const, 4)
            highest, outs = Steps(dve, max_steps, 4), Steps(dve, out_steps, 1)

            def step(at):
                if b := at(0):
                    s = b.slot(2)
                    freed(dve, gathered, b, 2 * 16 * T)
                    dve.tensor_copy(gi[:, s, :], k["gather_i"][:, bass.ds(b.n * T, T)])
                    dve.tensor_copy(di[:, s, :], k["dst_i"][:, bass.ds(b.n * T, T)]).then_inc(index_ready, 1)
                if b := at(5):
                    s = b.slot(2)
                    freed(dve, scattered, b, 16 * T)
                    dve.tensor_copy(si[:, s, :], k["scatter_i"][:, bass.ds(b.n * T, T)]).then_inc(sindex_ready, 1)
                    after(dve, back, b)
                    outs.start(b.n)
                    outs.made(dve.reciprocal(inv[:, s], p_o[:, T * M:T * M + T * H].rearrange("p (t h) -> p t h", t=T)))
                    dve.tensor_tensor(out[:, s].rearrange("p t (h c) -> p (t h) c", h=H),
                                      p_o[:, 0:T * M].rearrange("p (g c) -> p g c", c=C),
                                      inv[:, s].rearrange("p t h -> p (t h)").unsqueeze(2).broadcast_to([P, T * H, C]),
                                      ALU.mult).then_inc(out_ready, 1)
                if b := at(3):
                    s = b.slot(2)
                    highest.start(b.n)
                    highest.made(dve.tensor_copy(top[:, s, 0:1], top[:, 1 - s, W:W + 1]))
                    highest.made(dve.tensor_scalar(restart[:], k["keep"][0:H, bass.ds(b.n * W, W)], 1.0, BIG, ALU.subtract, ALU.mult))
                    after(dve, alpha_done, b)
                    highest.made(dve.tensor_tensor_scan(top[:, s, 1:W + 1], restart[:], p_alpha[0:H, :], top[:, s, 0:1], ALU.add, ALU.max))
                    after(dve, spread, b, lag=2)
                    after(dve, den_summed, b, lag=2)
                    highest.made(dve.tensor_tensor(change[:, s, 0, :], top[:, s, 0:W], restart[:], ALU.add))
                    dve.tensor_tensor(change[:, s, 0, :], change[:, s, 0, :], top[:, s, 1:W + 1], ALU.subtract)
                    dve.tensor_tensor(change[:, s, 1, :], p_alpha[0:H, :], top[:, s, 1:W + 1], ALU.subtract).then_inc(exp_in, 1)
                    highest.end()
                if b := at(4):
                    s = b.slot(2)
                    after(dve, spread, b)
                    after(dve, back, b, lag=2)
                    dve.tensor_tensor(v_w[:, s, :], p_p[0:M, :], vk[0:M, b.slot(U), :], ALU.mult).then_inc(weighted, 1)
                    after(dve, den_summed, b, lag=1)
                    dve.tensor_tensor_scan(den[:, s, :], change[:, s, 0, :], change[:, s, 1, :],
                                           den[:, 1 - s, W - 1:W], ALU.mult, ALU.add).then_inc(den_summed, 1)
                    after(dve, weighted, b)
                    after(dve, summed, b, lag=1)
                    dve.tensor_tensor_scan(acc[:, s, :], p_d[0:M, :], v_w[:, s, :],
                                           acc[:, 1 - s, W - 1:W], ALU.mult, ALU.add).then_inc(summed, 1)
                if b := at(2):
                    s = b.slot(2)
                    after(dve, q_done, b)
                    after(dve, vk_ready, b)
                    after(dve, alpha_done, b, lag=2)
                    dve.scalar_tensor_tensor(product[:, s, :], p_q[:], k["b_q"][:], vk[:, b.slot(U), :], ALU.add, ALU.mult).then_inc(product_ready, 1)
            pipeline(dve, EB, U, DEPTH, step)


def nodes_layer0(nc, k, a):
    with ExitStack() as ctx:
        sb = lambda n, shape, dt=F32: ctx.enter_context(nc.sbuf_tensor("n0_" + n, shape, dt))
        ps = lambda n, shape: ctx.enter_context(nc.psum_tensor("n0_" + n, shape, F32))
        sem = pass_semaphores(nc, ctx, "n0_")
        x_turned, xt_ready, h_done, var1, root1, scale1, norm1, beta_done, gamma_done, res_ready = map(
            sem, ("x_turned", "xt_ready", "h_done", "var1", "root1", "scale1", "norm1", "beta_done", "gamma_done", "res_ready"))
        var2, root2, scale2, x1_ready, x1_turned, x1t_ready, y_done, hs_ready, steps1, steps2, norm_steps1, norm_steps2 = map(
            sem, ("var2", "root2", "scale2", "x1_ready", "x1_turned", "x1t_ready", "y_done", "hs_ready", "steps1", "steps2", "norm_steps1", "norm_steps2"))
        U = 6
        source = NodeInput(sem, 2, U, reads_x=True)
        x1_stored, hs_stored = ([sem(f"{n}{i}") for i in range(2)] for n in ("x1_stored", "hs_stored"))
        x, agg, z = (sb(n, [P, U, G, D]) for n in ("x", "agg", "z"))
        xt, x1, x1t, hs = (sb(n, [P, 2, G, D]) for n in ("xt", "x1", "x1t", "hs"))
        stats1, stats2 = sb("stats1", [P, G, 6]), sb("stats2", [P, G, 6])
        diff1, diff2 = sb("diff1", [P, G]), sb("diff2", [P, G])
        mv1, mv2 = sb("mv1", [P, 2, G, 2]), sb("mv2", [P, 2, G, 2])
        r1, r2, nm1, nm2 = (sb(n, [P, 2, G]) for n in ("r1", "r2", "nm1", "nm2"))
        p_x, p_y = (ps(n, [P, G, D]) for n in ("p_x", "p_y"))
        p_h = [ps(f"p_h{i}", [P, G, D]) for i in range(2)]
        block = ctx.enter_context(nc.Block())
        DEPTH = 7

        @block.sync
        def _(sp):
            def step(at):
                if b := at(0):
                    u = b.slot(U)
                    after(sp, res_ready, b, lag=U)
                    after(sp, h_done, b, lag=U)
                    source.load(sp, x[:, u], a["x"], b)
                    source.load(sp, agg[:, u], k["agg"], b)
                if b := at(7 + AHEAD):
                    after(sp, hs_ready, b)
                    sp.dma_start(table_rows(k["hs1"], b.n), flat(hs[:, b.slot(2)])).then_inc(hs_stored[b.slot(2)], 16)
                    sp.dma_start(table_rows(k["acc"], b.n), flat(hs[:, b.slot(2)])).then_inc(hs_stored[b.slot(2)], 16)
                if b := at(5 + AHEAD):
                    after(sp, x1_ready, b)
                    sp.dma_start(table_rows(k["x1"], b.n), flat(x1[:, b.slot(2)])).then_inc(x1_stored[b.slot(2)], 16)
            pipeline(sp, NB, U, DEPTH + AHEAD, step)
            all_landed(sp, x1_stored, NB, 16)
            all_landed(sp, hs_stored, NB, 32)

        @block.gpsimd
        def _(pool):
            def step(at):
                if b := at(3):
                    u = b.slot(U)
                    after(pool, norm1, b)
                    pool.tensor_tensor(z[:, u], z[:, u], over_tiles(k["gamma0_r"][:]), ALU.mult).then_inc(gamma_done, 1)
                    after(pool, beta_done, b)
                    after(pool, gamma_done, b)
                    pool.tensor_tensor(z[:, u], z[:, u], x[:, u], ALU.add).then_inc(res_ready, 1)
                if b := at(2):
                    u = b.slot(U)
                    after(pool, x_turned, b)
                    pool.tensor_tensor(x[:, u], x[:, u], over_tiles(k["beta0_r"][:]), ALU.add).then_inc(beta_done, 1)
            pipeline(pool, NB, U, DEPTH, step)

        @block.tensor
        def _(pe):
            def step(at):
                if b := at(0):
                    source.landed(pe, b)
                    after(pe, xt_ready, b, lag=1)
                    after(pe, x1t_ready, b, lag=7)
                    for t in range(G):
                        last = pe.transpose(p_x[:, t, :], x[:, b.slot(U), t, :], k["ident"][:])
                    last.then_inc(x_turned, 1)
                if b := at(1):
                    s = b.slot(2)
                    after(pe, xt_ready, b)
                    after(pe, norm1, b, lag=2)
                    for t in range(G):
                        pe.matmul(p_h[s][:, t, :], xt[:, s, t, :], k["w_pre"][:], start=t % 4 == 0, stop=False,
                                  skip_group_check=True)
                    for c in range(2):
                        pe.matmul(p_h[s][:, 4 * c:4 * c + 4, :], k["ident"][:], agg[:, b.slot(U), 4 * c:4 * c + 4, :], start=False, stop=False,
                                  skip_group_check=True)
                        last = pe.matmul(p_h[s][:, 4 * c:4 * c + 4, :], k["ones_b"][:], k["bias_h"][:], start=False, stop=True,
                                         skip_group_check=True)
                    last.then_inc(h_done, 1)
                if b := at(6):
                    after(pe, x1_ready, b)
                    after(pe, xt_ready, b, lag=-6, n=NB)
                    after(pe, x1t_ready, b, lag=1)
                    for t in range(G):
                        last = pe.transpose(p_x[:, t, :], x1[:, b.slot(2), t, :], k["ident"][:])
                    last.then_inc(x1_turned, 1)
                if b := at(7):
                    after(pe, x1t_ready, b)
                    after(pe, hs_ready, b, lag=1)
                    for t in range(G):
                        last = pe.matmul(p_y[:, t, :], x1t[:, b.slot(2), t, :], k["w_l1"][:], start=t % 4 == 0, stop=False,
                                         skip_group_check=True)
                    for c in range(2):
                        last = pe.matmul(p_y[:, 4 * c:4 * c + 4, :], k["ones_b"][:], k["bias_l1"][:], start=False, stop=True,
                                         skip_group_check=True)
                    last.then_inc(y_done, 1)
            pipeline(pe, NB, U, DEPTH, step)

        @block.scalar
        def _(act):
            def step(at):
                if b := at(2):
                    s = b.slot(2)
                    after(act, var1, b)
                    act.activation(r1[:, s], mv1[:, s, :, 1], ACT.Sqrt, bias=k["eps"][:]).then_inc(root1, 1)
                if b := at(5):
                    s = b.slot(2)
                    after(act, var2, b)
                    act.activation(r2[:, s], mv2[:, s, :, 1], ACT.Sqrt, bias=k["eps"][:]).then_inc(root2, 1)
                if b := at(0):
                    after(act, x_turned, b)
                    after(act, h_done, b, lag=2)
                    act.activation(xt[:, b.slot(2)], p_x[:], ACT.Copy).then_inc(xt_ready, 1)
                if b := at(2):
                    s = b.slot(2)
                    after(act, scale1, b)
                    after(act, x1_ready, b, lag=U)
                    for t in range(G):
                        last = act.activation(z[:, b.slot(U), t, :], p_h[s][:, t, :], ACT.Identity, scale=r1[:, s, t:t + 1], bias=nm1[:, s, t:t + 1])
                    last.then_inc(norm1, 1)
                if b := at(6):
                    after(act, x1_turned, b)
                    after(act, y_done, b, lag=2)
                    act.activation(x1t[:, b.slot(2)], p_x[:], ACT.Copy).then_inc(x1t_ready, 1)
                if b := at(5):
                    s = b.slot(2)
                    after(act, scale2, b)
                    freed(act, x1_stored, b, 16)
                    after(act, x1_turned, b, lag=2)
                    for t in range(G):
                        last = act.activation(x1[:, s, t, :], z[:, b.slot(U), t, :], ACT.Identity, scale=r2[:, s, t:t + 1], bias=nm2[:, s, t:t + 1])
                    last.then_inc(x1_ready, 1)
            pipeline(act, NB, U, DEPTH, step)

        @block.vector
        def _(dve):
            first, second = Steps(dve, steps1, 3), Steps(dve, steps2, 3)
            norm_first, norm_second = Steps(dve, norm_steps1, 1), Steps(dve, norm_steps2, 1)

            def step(at):
                if b := at(2):
                    s = b.slot(2)
                    after(dve, root1, b)
                    norm_first.start(b.n)
                    norm_first.made(dve.reciprocal(r1[:, s], r1[:, s]))
                    norm_first.end()
                    dve.scalar_tensor_tensor(nm1[:, s], mv1[:, s, :, 0], -0.5, r1[:, s], ALU.mult, ALU.mult).then_inc(scale1, 1)
                if b := at(5):
                    s = b.slot(2)
                    after(dve, root2, b)
                    norm_second.start(b.n)
                    norm_second.made(dve.reciprocal(r2[:, s], r2[:, s]))
                    norm_second.end()
                    dve.scalar_tensor_tensor(nm2[:, s], mv2[:, s, :, 0], -0.5, r2[:, s], ALU.mult, ALU.mult).then_inc(scale2, 1)
                if b := at(4):
                    after(dve, res_ready, b)
                    second.start(b.n)
                    node_stats(dve, second, z[:, b.slot(U)], stats2, mv2[:, b.slot(2)], diff2[:]).then_inc(var2, 1)
                    second.end()
                if b := at(1):
                    s = b.slot(2)
                    after(dve, h_done, b)
                    first.start(b.n)
                    node_stats(dve, first, p_h[s], stats1, mv1[:, s], diff1[:]).then_inc(var1, 1)
                    first.end()
                if b := at(7):
                    after(dve, y_done, b)
                    freed(dve, hs_stored, b, 32)
                    dve.tensor_tensor(hs[:, b.slot(2)], p_y[:], over_width(k["dinv_src"][:, bass.ds(b.n * G, G)]), ALU.mult).then_inc(hs_ready, 1)
            pipeline(dve, NB, U, DEPTH, step)


def nodes_batch_stats(nc, k, a):
    with ExitStack() as ctx:
        sb = lambda n, shape, dt=F32: ctx.enter_context(nc.sbuf_tensor("bs_" + n, shape, dt))
        ps = lambda n, shape: ctx.enter_context(nc.psum_tensor("bs_" + n, shape, F32))
        sem = pass_semaphores(nc, ctx, "bs_")
        out_ready, square_ready, used, const, totals, steps_, root = map(
            sem, ("out", "square", "used", "const", "totals", "steps", "root"))
        added = [sem("added_dve"), sem("added_pool")]
        U = 4
        source = NodeInput(sem, 1, U)
        h, sq = sb("h", [P, U, G, D]), sb("sq", [P, U, G, D])
        sq_sum = sb("sq_sum", [P, 2, G, D])
        ones, zero = sb("ones", [P, P]), sb("zero", [P, 512])
        mean, var = sb("mean", [P, D]), sb("var", [P, D])
        p_sum, p_sq = ps("p_sum", [P, 4, D]), ps("p_sq", [P, 4, D])
        block = ctx.enter_context(nc.Block())

        def follows(eng, sem, b):
            if not (isinstance(b.n, int) and b.n < 2):
                eng.wait_ge(sem, b.turn(2))
        DEPTH = 2

        @block.sync
        def _(sp):
            def step(at):
                if b := at(0):
                    u = b.slot(U)
                    after(sp, used, b, lag=U)
                    after(sp, square_ready, b, lag=U)
                    source.load(sp, h[:, u], k["acc"], b)
            pipeline(sp, NB, U, DEPTH, step)

        @block.gpsimd
        def _(pool):
            pool.memset(ones[:], 1.0)
            pool.memset(zero[:], 0.0).then_inc(const, 1)
            pool.memset(sq_sum[:], 0.0).then_inc(const, 1)
            pool.wait_ge(const, 2)

            def step(at):
                if (b := at(1)) and b.slot(2) == 1:
                    after(pool, square_ready, b)
                    follows(pool, added[1], b)
                    pool.tensor_tensor(sq_sum[:, 1], sq_sum[:, 1], sq[:, b.slot(U)], ALU.add).then_inc(added[1], 1)
            pipeline(pool, NB, U, DEPTH, step)

        @block.tensor
        def _(pe):
            pe.wait_ge(const, 1)
            for p in (p_sum, p_sq):
                pe.matmul(p[:], ones[:], zero[:], start=True, stop=False, skip_group_check=True)

            def step(at):
                if b := at(2):
                    after(pe, out_ready, b)
                    for c in range(2):
                        last = pe.matmul(p_sum[:], ones[:], h[:, b.slot(U), 4 * c:4 * c + 4, :], start=False, stop=False, skip_group_check=True)
                    last.then_inc(used, 1)
            pipeline(pe, NB, U, DEPTH, step)
            for i in range(2):
                pe.wait_ge(added[i], (NB + 1 - i) // 2)
                for c in range(2):
                    pe.matmul(p_sq[:], ones[:], sq_sum[:, i, 4 * c:4 * c + 4, :], start=False, stop=False, skip_group_check=True)
            for p in (p_sum, p_sq):
                last = pe.matmul(p[:], ones[:], zero[:], start=False, stop=True, skip_group_check=True)
            last.then_inc(totals, 1)

        @block.scalar
        def _(act):
            def step(at):
                if b := at(1):
                    after(act, out_ready, b)
                    if not (isinstance(b.n, int) and b.n < U):
                        act.wait_ge(added[b.slot(2)], b.turn(2) + 1 - U // 2)
                    act.activation(sq[:, b.slot(U)], h[:, b.slot(U)], ACT.Square).then_inc(square_ready, 1)
            pipeline(act, NB, U, DEPTH, step)
            act.wait_ge(steps_, 6)
            act.activation(var[:], var[:], ACT.Sqrt, bias=k["eps"][:]).then_inc(root, 1)

        @block.vector
        def _(dve):
            def step(at):
                if b := at(0):
                    u = b.slot(U)
                    source.landed(dve, b)
                    dve.tensor_tensor(h[:, u], h[:, u], over_width(k["sum_w"][:, bass.ds(b.n * G, G)]), ALU.mult).then_inc(out_ready, 1)
                if (b := at(1)) and b.slot(2) == 0:
                    after(dve, square_ready, b)
                    follows(dve, added[0], b)
                    dve.tensor_tensor(sq_sum[:, 0], sq_sum[:, 0], sq[:, b.slot(U)], ALU.add).then_inc(added[0], 1)
            dve.wait_ge(const, 2)
            pipeline(dve, NB, U, DEPTH, step)
            dve.wait_ge(totals, 1)
            steps = Steps(dve, steps_, 10)
            steps.start(0)
            by_feature = lambda p: p[:].rearrange("p k d -> p d k")
            steps.made(dve.tensor_reduce(mean[:], by_feature(p_sum), mybir.AxisListType.X, ALU.add))
            steps.made(dve.tensor_reduce(var[:], by_feature(p_sq), mybir.AxisListType.X, ALU.add))
            steps.made(dve.tensor_scalar(mean[:], mean[:], 1.0 / N, None, ALU.mult))
            steps.made(dve.tensor_scalar(var[:], var[:], 1.0 / N, None, ALU.mult))
            steps.made(dve.tensor_tensor(k["bn_shift_r"][:], mean[:], mean[:], ALU.mult))
            steps.made(dve.tensor_tensor(var[:], var[:], k["bn_shift_r"][:], ALU.subtract))
            dve.wait_ge(root, 1)
            steps.made(dve.reciprocal(var[:], var[:]))
            steps.made(dve.tensor_tensor(k["bn_scale_r"][:], var[:], k["gamma1_r"][:], ALU.mult))
            steps.made(dve.tensor_tensor(mean[:], mean[:], k["bn_scale_r"][:], ALU.mult))
            steps.made(dve.tensor_tensor(k["bn_shift_r"][:], k["beta1_r"][:], mean[:], ALU.subtract))
            steps.end()


def nodes_layer1(nc, k, a):
    with ExitStack() as ctx:
        sb = lambda n, shape, dt=F32: ctx.enter_context(nc.sbuf_tensor("n1_" + n, shape, dt))
        sem = pass_semaphores(nc, ctx, "n1_")
        out_ready, scaled, shifted, z_ready, var, root, scale_ready, x2_ready, steps_, norm_steps = map(
            sem, ("out", "scaled", "shifted", "z", "var", "root", "scale", "x2", "steps", "norm_steps"))
        U = 6
        source = NodeInput(sem, 2, U)
        x2_stored = [sem(f"x2_stored{i}") for i in range(2)]
        x, h = (sb(n, [P, U, G, D]) for n in ("x", "h"))
        z, x2 = sb("z", [P, 2, G, D]), sb("x2", [P, 2, G, D])
        diff = sb("diff", [P, G])
        stats, mv, r, nm = sb("stats", [P, G, 6]), sb("mv", [P, 2, G, 2]), sb("r", [P, 2, G]), sb("nm", [P, 2, G])
        block = ctx.enter_context(nc.Block())
        DEPTH = 3

        @block.sync
        def _(sp):
            def step(at):
                if b := at(0):
                    u = b.slot(U)
                    after(sp, z_ready, b, lag=U)
                    source.load(sp, x[:, u], k["x1"], b)
                    source.load(sp, h[:, u], k["acc"], b)
                if b := at(3 + AHEAD):
                    after(sp, x2_ready, b)
                    sp.dma_start(table_rows(k["x2"], b.n), flat(x2[:, b.slot(2)])).then_inc(x2_stored[b.slot(2)], 16)
            pipeline(sp, NB, U, DEPTH + AHEAD, step)
            all_landed(sp, x2_stored, NB, 16)

        @block.gpsimd
        def _(pool):
            def step(at):
                if b := at(1):
                    u = b.slot(U)
                    after(pool, out_ready, b)
                    pool.tensor_tensor(h[:, u], h[:, u], over_tiles(k["bn_scale_r"][:]), ALU.mult).then_inc(scaled, 1)
                    after(pool, scaled, b)
                    pool.tensor_tensor(h[:, u], h[:, u], over_tiles(k["bn_shift_r"][:]), ALU.add).then_inc(shifted, 1)
            pipeline(pool, NB, U, DEPTH, step)

        @block.scalar
        def _(act):
            def step(at):
                if b := at(3):
                    s = b.slot(2)
                    after(act, var, b)
                    act.activation(r[:, s], mv[:, s, :, 1], ACT.Sqrt, bias=k["eps"][:]).then_inc(root, 1)
                    after(act, scale_ready, b)
                    freed(act, x2_stored, b, 16)
                    for t in range(G):
                        last = act.activation(x2[:, s, t, :], z[:, s, t, :], ACT.Identity, scale=r[:, s, t:t + 1], bias=nm[:, s, t:t + 1])
                    last.then_inc(x2_ready, 1)
            pipeline(act, NB, U, DEPTH, step)

        @block.vector
        def _(dve):
            steps, norm = Steps(dve, steps_, 3), Steps(dve, norm_steps, 1)

            def step(at):
                if b := at(0):
                    u = b.slot(U)
                    source.landed(dve, b)
                    dve.tensor_tensor(h[:, u], h[:, u], over_width(k["dinv_src"][:, bass.ds(b.n * G, G)]), ALU.mult).then_inc(out_ready, 1)
                if b := at(3):
                    s = b.slot(2)
                    norm.start(b.n)
                    after(dve, root, b)
                    norm.made(dve.reciprocal(r[:, s], r[:, s]))
                    norm.end()
                    dve.scalar_tensor_tensor(nm[:, s], mv[:, s, :, 0], -0.5, r[:, s], ALU.mult, ALU.mult).then_inc(scale_ready, 1)
                if b := at(2):
                    s, u = b.slot(2), b.slot(U)
                    after(dve, shifted, b)
                    after(dve, x2_ready, b, lag=2)
                    dve.scalar_tensor_tensor(z[:, s], h[:, u], 0.0, x[:, u], ALU.max, ALU.add).then_inc(z_ready, 1)
                    after(dve, z_ready, b)
                    steps.start(b.n)
                    node_stats(dve, steps, z[:, s], stats, mv[:, s], diff[:]).then_inc(var, 1)
                    steps.end()
            pipeline(dve, NB, U, DEPTH, step)


def nodes_layer2(nc, k, a):
    with ExitStack() as ctx:
        sb = lambda n, shape, dt=F32: ctx.enter_context(nc.sbuf_tensor("n2_" + n, shape, dt))
        ps = lambda n, shape: ctx.enter_context(nc.psum_tensor("n2_" + n, shape, F32))
        sem = pass_semaphores(nc, ctx, "n2_")
        x_turned, xt_ready, r_done, gated, gate_in, beta_ready, diff_ready, mix_ready = map(
            sem, ("x_turned", "xt_ready", "r_done", "gated", "gate_in", "beta", "diff", "mix"))
        mix_turned, mixt_ready, m_done, z_ready, var, root, scale_ready, x3_ready = map(
            sem, ("mix_turned", "mixt", "m_done", "z", "var", "root", "scale", "x3"))
        x3_turned, x3t_ready, y_done, hs_ready, gate_steps, mix_steps, steps_, pool_steps = map(
            sem, ("x3_turned", "x3t", "y_done", "hs", "gate_steps", "mix_steps", "steps", "pool_steps"))
        U = 6
        source = NodeInput(sem, 2, U)
        x3_stored, hs_stored = ([sem(f"{n}{i}") for i in range(2)] for n in ("x3_stored", "hs_stored"))
        x, msg = sb("x", [P, U, G, D]), sb("msg", [P, U, G, M])
        xt, z, x3, x3t, hs = (sb(n, [P, 2, G, D]) for n in ("xt", "z", "x3", "x3t", "hs"))
        prod, mix = sb("prod", [P, 2, G, M]), sb("mix", [P, 2, G, M])
        mixt = sb("mixt", [P, 2, G // 2, P])
        gate = sb("gate", [P, 2, G])
        diff = sb("diff", [P, G])
        stats, mv, r, nm = sb("stats", [P, G, 6]), sb("mv", [P, 2, G, 2]), sb("r", [P, 2, G]), sb("nm", [P, 2, G])
        half = sb("half", [P, G])
        issued = sem("issued")
        p_x, p_r, p_y = (ps(n, [P, G, D]) for n in ("p_x", "p_r", "p_y"))
        p_mix = ps("p_mix", [P, G // 2, P])
        block = ctx.enter_context(nc.Block())
        DEPTH = 6

        @block.sync
        def _(sp):
            def step(at):
                if b := at(0):
                    u = b.slot(U)
                    after(sp, z_ready, b, lag=U)
                    source.load(sp, x[:, u], k["x2"], b)
                    source.load(sp, msg[:, u], k["agg_m"], b, M)
                if b := at(6 + AHEAD):
                    after(sp, hs_ready, b)
                    sp.dma_start(table_rows(k["hs3"], b.n), flat(hs[:, b.slot(2)])).then_inc(hs_stored[b.slot(2)], 16)
                    sp.dma_start(table_rows(k["acc"], b.n), flat(hs[:, b.slot(2)])).then_inc(hs_stored[b.slot(2)], 16)
                if b := at(4 + AHEAD):
                    after(sp, x3_ready, b)
                    sp.dma_start(table_rows(k["x3"], b.n), flat(x3[:, b.slot(2)])).then_inc(x3_stored[b.slot(2)], 16)
            pipeline(sp, NB, U, DEPTH + AHEAD, step)
            all_landed(sp, x3_stored, NB, 16)
            all_landed(sp, hs_stored, NB, 32)

        @block.gpsimd
        def _(pool):
            pool.memset(half[:], -0.5).then_inc(pool_steps, 1)
            pool.wait_ge(pool_steps, 1)

            def step(at):
                if b := at(4):
                    s = b.slot(2)
                    after(pool, var, b)
                    carry(pool, issued)
                    pool.tensor_scalar(r[:, s], mv[:, s, :, 1], EPS, None, ALU.add).then_inc(pool_steps, 1)
                    pool.wait_ge(pool_steps, b.n + 2)
                    pool.tensor_tensor(r[:, s], r[:, s], half[:], ALU.pow).then_inc(root, 1)
                if b := at(2):
                    s, u = b.slot(2), b.slot(U)
                    after(pool, diff_ready, b)
                    pool.tensor_tensor(mix[:, s], mix[:, s], msg[:, u], ALU.add).then_inc(mix_ready, 1)
                if b := at(0):
                    s, u = b.slot(2), b.slot(U)
                    source.landed(pool, b)
                    after(pool, gate_in, b, lag=2)
                    pool.tensor_tensor(prod[:, s], msg[:, u], over_tiles(k["w_out"][:]), ALU.mult).then_inc(gated, 1)
            pipeline(pool, NB, U, DEPTH, step)

        @block.tensor
        def _(pe):
            def step(at):
                if b := at(3):
                    s = b.slot(2)
                    after(pe, mix_ready, b)
                    after(pe, mixt_ready, b, lag=1)
                    for t in range(G // 2):
                        last = pe.transpose(p_mix[:, t, :], mix[:, s, 2 * t:2 * t + 2, :].rearrange("p k d -> p (k d)"), k["ident"][:])
                    last.then_inc(mix_turned, 1)
                if b := at(0):
                    source.landed(pe, b)
                    after(pe, x3t_ready, b, lag=6)
                    after(pe, xt_ready, b, lag=1)
                    for t in range(G):
                        last = pe.transpose(p_x[:, t, :], x[:, b.slot(U), t, :], k["ident"][:])
                    last.then_inc(x_turned, 1)
                if b := at(3):
                    after(pe, mixt_ready, b)
                    after(pe, hs_ready, b, lag=4)
                    after(pe, z_ready, b, lag=1)
                    for t in range(G):
                        part = slice(M * (t % 2), M * (t % 2 + 1))
                        last = pe.matmul(p_y[:, 4 * (t % 2) + t // 2, :], mixt[part, b.slot(2), t // 2, :], k["w_m2n"][part, :], start=True, stop=True)
                    last.then_inc(m_done, 1)
                if b := at(1):
                    after(pe, xt_ready, b)
                    after(pe, diff_ready, b, lag=1)
                    after(pe, gate_in, b, lag=1)
                    for t in range(G):
                        pe.matmul(p_r[:, t, 0:M + 1], xt[:, b.slot(2), t, :], k["w_r"][:], start=t % 4 == 0, stop=False,
                                  skip_group_check=True)
                    for c in range(2):
                        last = pe.matmul(p_r[:, 4 * c:4 * c + 4, 0:M + 1], k["ones_b"][:], k["bias_r"][:], start=False, stop=True,
                                         skip_group_check=True)
                    last.then_inc(r_done, 1)
                if b := at(5):
                    after(pe, x3_ready, b)
                    after(pe, xt_ready, b, lag=-5, n=NB)
                    after(pe, x3t_ready, b, lag=1)
                    for t in range(G):
                        last = pe.transpose(p_x[:, t, :], x3[:, b.slot(2), t, :], k["ident"][:])
                    last.then_inc(x3_turned, 1)
                if b := at(6):
                    after(pe, x3t_ready, b)
                    after(pe, z_ready, b, lag=-3, n=NB)
                    after(pe, hs_ready, b, lag=1)
                    for t in range(G):
                        last = pe.matmul(p_y[:, t, :], x3t[:, b.slot(2), t, :], k["w1_l3"][:], start=True, stop=True)
                    last.then_inc(y_done, 1)
            pipeline(pe, NB, U, DEPTH, step)

        @block.scalar
        def _(act):
            def step(at):
                if b := at(2):
                    s = b.slot(2)
                    after(act, gate_in, b)
                    act.activation(gate[:, s], gate[:, s], ACT.Sigmoid).then_inc(beta_ready, 1)
                if b := at(3):
                    after(act, mix_turned, b)
                    after(act, m_done, b, lag=2)
                    act.activation(mixt[:, b.slot(2)], p_mix[:], ACT.Copy).then_inc(mixt_ready, 1)
                if b := at(0):
                    after(act, x_turned, b)
                    after(act, r_done, b, lag=2)
                    act.activation(xt[:, b.slot(2)], p_x[:], ACT.Copy).then_inc(xt_ready, 1)
                if b := at(4):
                    s = b.slot(2)
                    after(act, scale_ready, b)
                    freed(act, x3_stored, b, 16)
                    after(act, x3_turned, b, lag=2)
                    for t in range(G):
                        last = act.activation(x3[:, s, t, :], z[:, s, t, :], ACT.Identity, scale=r[:, s, t:t + 1], bias=nm[:, s, t:t + 1])
                    last.then_inc(x3_ready, 1)
                if b := at(5):
                    after(act, x3_turned, b)
                    after(act, y_done, b, lag=2)
                    act.activation(x3t[:, b.slot(2)], p_x[:], ACT.Copy).then_inc(x3t_ready, 1)
            pipeline(act, NB, U, DEPTH, step)

        @block.vector
        def _(dve):
            gates, mixes, steps = Steps(dve, gate_steps, 1), Steps(dve, mix_steps, 1), Steps(dve, steps_, 3)

            def step(at):
                if b := at(2):
                    s, u = b.slot(2), b.slot(U)
                    mixes.start(b.n)
                    after(dve, r_done, b)
                    after(dve, mix_turned, b, lag=2)
                    mixes.made(dve.tensor_tensor(mix[:, s], p_r[:, :, 0:M], msg[:, u], ALU.subtract))
                    after(dve, beta_ready, b)
                    dve.tensor_tensor(mix[:, s], mix[:, s], over_width(gate[:, s], M), ALU.mult).then_inc(diff_ready, 1)
                    mixes.end()
                if b := at(4):
                    s = b.slot(2)
                    after(dve, root, b)
                    dve.scalar_tensor_tensor(nm[:, s], mv[:, s, :, 0], -0.5, r[:, s], ALU.mult, ALU.mult).then_inc(scale_ready, 1)
                if b := at(3):
                    s, u = b.slot(2), b.slot(U)
                    after(dve, m_done, b)
                    after(dve, x3_ready, b, lag=2)
                    dve.tensor_tensor(z[:, s].rearrange("p (q h) d -> p q h d", h=2), p_y[:].rearrange("p (h q) d -> p q h d", h=2),
                                      x[:, u].rearrange("p (q h) d -> p q h d", h=2), ALU.add).then_inc(z_ready, 1)
                    after(dve, z_ready, b)
                    steps.start(b.n)
                    node_stats(dve, steps, z[:, s], stats, mv[:, s], diff[:]).then_inc(var, 1)
                    steps.end()
                if b := at(1):
                    s = b.slot(2)
                    gates.start(b.n)
                    after(dve, gated, b)
                    after(dve, diff_ready, b, lag=2)
                    gates.made(dve.tensor_reduce(gate[:, s], prod[:, s], mybir.AxisListType.X, ALU.add))
                    gates.end()
                    after(dve, r_done, b)
                    dve.tensor_tensor(gate[:, s], gate[:, s], p_r[:, :, M], ALU.add).then_inc(gate_in, 1)
                if b := at(6):
                    after(dve, y_done, b)
                    freed(dve, hs_stored, b, 32)
                    dve.tensor_tensor(hs[:, b.slot(2)], p_y[:], over_width(k["dinv_dst"][:, bass.ds(b.n * G, G)]), ALU.mult).then_inc(hs_ready, 1)
            pipeline(dve, NB, U, DEPTH, step)


def nodes_layer3_middle(nc, k, a):
    with ExitStack() as ctx:
        sb = lambda n, shape, dt=F32: ctx.enter_context(nc.sbuf_tensor("n3_" + n, shape, dt))
        ps = lambda n, shape: ctx.enter_context(nc.psum_tensor("n3_" + n, shape, F32))
        sem = pass_semaphores(nc, ctx, "n3_")
        sum_ready, scaled, g_ready, turned, gt_ready, y_done, y_ready = map(sem, ("sum", "scaled", "g", "turned", "gt", "y_done", "y"))
        U = 6
        source = NodeInput(sem, 1, U)
        stored = [sem(f"stored{i}") for i in range(2)]
        h = sb("h", [P, U, G, D])
        gt, y = sb("gt", [P, 3, G, D]), sb("y", [P, 2, G, D])
        p_t, p_y = [ps(f"p_t{i}", [P, G, D]) for i in range(2)], [ps(f"p_y{i}", [P, G, D]) for i in range(2)]
        block = ctx.enter_context(nc.Block())
        DEPTH = 4

        @block.sync
        def _(sp):
            def step(at):
                if b := at(0):
                    u = b.slot(U)
                    after(sp, turned, b, lag=U)
                    source.load(sp, h[:, u], k["acc"], b)
                if b := at(4 + AHEAD):
                    after(sp, y_ready, b)
                    sp.dma_start(table_rows(k["hs4"], b.n), flat(y[:, b.slot(2)])).then_inc(stored[b.slot(2)], 16)
            pipeline(sp, NB, U, DEPTH + AHEAD, step)
            all_landed(sp, stored, NB, 16)

        @block.gpsimd
        def _(pool):
            def step(at):
                if b := at(0):
                    u = b.slot(U)
                    source.landed(pool, b)
                    pool.tensor_tensor(h[:, u], h[:, u], over_width(k["dinv_dst"][:, bass.ds(b.n * G, G)]), ALU.mult).then_inc(sum_ready, 1)
            pipeline(pool, NB, U, DEPTH, step)

        @block.tensor
        def _(pe):
            def step(at):
                if b := at(4):
                    s = b.slot(2)
                    after(pe, gt_ready, b)
                    after(pe, y_ready, b, lag=2)
                    for t in range(G):
                        last = pe.matmul(p_y[s][:, t, :], gt[:, b.slot(3), t, :], k["w2_l3"][:], start=True, stop=True)
                    last.then_inc(y_done, 1)
                if b := at(2):
                    s = b.slot(2)
                    after(pe, g_ready, b)
                    after(pe, gt_ready, b, lag=2)
                    for t in range(G):
                        last = pe.transpose(p_t[s][:, t, :], h[:, b.slot(U), t, :], k["ident"][:])
                    last.then_inc(turned, 1)
            pipeline(pe, NB, U, DEPTH, step)

        @block.scalar
        def _(act):
            def step(at):
                if b := at(4):
                    s = b.slot(2)
                    after(act, y_done, b)
                    freed(act, stored, b, 16)
                    act.activation(y[:, s], p_y[s][:], ACT.Copy).then_inc(y_ready, 1)
                if b := at(2):
                    s = b.slot(2)
                    after(act, turned, b)
                    after(act, y_done, b, lag=3)
                    act.activation(gt[:, b.slot(3)], p_t[s][:], ACT.Copy).then_inc(gt_ready, 1)
            pipeline(act, NB, U, DEPTH, step)

        @block.vector
        def _(dve):
            def step(at):
                if b := at(1):
                    u = b.slot(U)
                    after(dve, sum_ready, b)
                    dve.tensor_tensor(h[:, u], h[:, u], over_tiles(k["b1_l3_r"][:]), ALU.add).then_inc(scaled, 1)
                    after(dve, scaled, b)
                    dve.scalar_tensor_tensor(h[:, u], h[:, u], 0.0, over_width(k["dinv_dst"][:, bass.ds(b.n * G, G)]), ALU.max, ALU.mult).then_inc(g_ready, 1)
            pipeline(dve, NB, U, DEPTH, step)


def nodes_layer3_out(nc, k, a):
    with ExitStack() as ctx:
        sb = lambda n, shape, dt=F32: ctx.enter_context(nc.sbuf_tensor("n4_" + n, shape, dt))
        sem = pass_semaphores(nc, ctx, "n4_")
        z_ready, var, root, scale_ready, out_ready, steps_, norm_steps = map(
            sem, ("z", "var", "root", "scale", "out", "steps", "norm_steps"))
        U = 6
        source = NodeInput(sem, 2, U)
        stored = [sem(f"stored{i}") for i in range(2)]
        part, agg = sb("part", [P, U, G, D]), sb("agg", [P, U, G, D])
        z, out = sb("z", [P, 3, G, D]), sb("out", [P, 2, G, D])
        diff = sb("diff", [P, G])
        stats, mv, r, nm = sb("stats", [P, G, 6]), sb("mv", [P, 2, G, 2]), sb("r", [P, 2, G]), sb("nm", [P, 2, G])
        block = ctx.enter_context(nc.Block())
        DEPTH = 1

        @block.sync
        def _(sp):
            def step(at):
                if b := at(0):
                    u = b.slot(U)
                    after(sp, z_ready, b, lag=U)
                    source.load(sp, part[:, u], k["part"], b)
                    source.load(sp, agg[:, u], k["agg"], b)
                if b := at(1 + AHEAD):
                    s = b.slot(2)
                    after(sp, out_ready, b)
                    if b.is_last(NB):
                        rest = a["out"][(NB - 1) * P * G:N, :].rearrange("(p k) d -> p (k d)", k=G)
                        sp.dma_start(rest[0:96], flat(out[0:96, s])).then_inc(stored[s], 16)
                        sp.dma_start(rest[96:LASTP], flat(out[96:LASTP, s])).then_inc(stored[s], 16)
                    else:
                        sp.dma_start(table_rows(a["out"], b.n), flat(out[:, s])).then_inc(stored[s], 16)
            pipeline(sp, NB, U, DEPTH + AHEAD, step)
            for s in range(2):
                sp.wait_ge(stored[s], 16 * ((NB + 1 - s) // 2 + ((NB - 1) % 2 == s)))

        @block.scalar
        def _(act):
            def step(at):
                if b := at(1):
                    s = b.slot(2)
                    after(act, var, b)
                    act.activation(r[:, s], mv[:, s, :, 1], ACT.Sqrt, bias=k["eps"][:]).then_inc(root, 1)
                    after(act, scale_ready, b)
                    freed(act, stored, b, 16)
                    for t in range(G):
                        last = act.activation(out[:, s, t, :], z[:, b.slot(3), t, :], ACT.Identity, scale=r[:, s, t:t + 1], bias=nm[:, s, t:t + 1])
                    last.then_inc(out_ready, 1)
            pipeline(act, NB, U, DEPTH, step)

        @block.vector
        def _(dve):
            steps, norm = Steps(dve, steps_, 3), Steps(dve, norm_steps, 1)

            def step(at):
                if b := at(0):
                    s, u = b.slot(2), b.slot(U)
                    source.landed(dve, b)
                    after(dve, out_ready, b, lag=3)
                    for t in range(G):
                        last = dve.scalar_tensor_tensor(z[:, b.slot(3), t, :], agg[:, u, t, :], k["dinv_dst"][:, bass.ds(b.n * G + t, 1)], part[:, u, t, :],
                                                        ALU.mult, ALU.add)
                    last.then_inc(z_ready, 1)
                if b := at(1):
                    s = b.slot(2)
                    norm.start(b.n)
                    after(dve, root, b)
                    norm.made(dve.reciprocal(r[:, s], r[:, s]))
                    norm.end()
                    dve.scalar_tensor_tensor(nm[:, s], mv[:, s, :, 0], -0.5, r[:, s], ALU.mult, ALU.mult).then_inc(scale_ready, 1)
                if b := at(0):
                    s = b.slot(2)
                    after(dve, z_ready, b)
                    steps.start(b.n)
                    node_stats(dve, steps, z[:, b.slot(3)], stats, mv[:, s], diff[:]).then_inc(var, 1)
                    steps.end()
            pipeline(dve, NB, U, DEPTH, step)


def build(nc, a):
    with ExitStack() as ctx:
        made = {}
        for name, shape, dt in (
                ("ident", [P, P], F32), ("zero", [P, G * D], F32), ("eps", [P, 1], F32), ("keep", [P, EPAD], BF16), ("count_iota", [P, COLS], F32),
                ("valid", [P, COLS], F32), ("dinv_src", [P, COLS], F32), ("dinv_dst", [P, COLS], F32),
                ("sum_w", [P, COLS], F32),
                ("src_lo", [P, ET], F32), ("src_hi", [P, ET], F32), ("src_c", [P, ET], F32), ("weight_c", [P, ET], F32),
                ("dst_lo", [P, ET], F32), ("dst_hi", [P, ET], F32), ("last_c", [P, ET], F32), ("dst_c", [P, ET], F32),
                ("gather_i", [P, ET], I32), ("scatter_i", [P, ET], I32), ("accumulate_i", [P, ET], I32), ("dst_i", [P, ET], I32),
                ("w_pre", [P, D], F32), ("w1", [P, D], F32), ("w2", [P, D], F32), ("w_l1", [P, D], F32),
                ("w_m2n", [P, D], F32), ("w1_l3", [P, D], F32), ("w2_l3", [P, D], F32),
                ("w_q", [P, 2 * M], F32), ("w_vk", [P, 2 * M], F32), ("w_ev", [R + 1, 2 * M], F32), ("w_r", [P, M + 1], F32),
                ("b_q", [P, 1], F32), ("b_r", [P, M + 1], F32), ("w_out", [P, M], F32),
                ("head_sum", [P, H], F32), ("head_spread", [H, M], F32),
                ("b_pre_c", [P, 1], F32), ("b1_c", [P, 1], F32), ("gamma1_r", [P, D], F32), ("beta1_r", [P, D], F32),
                ("b2_r", [P, D], F32), ("none0_r", [P, D], F32), ("gamma0_r", [P, D], F32), ("beta0_r", [P, D], F32),
                ("b_pre_r", [P, D], F32), ("b_l1_r", [P, D], F32), ("b1_l3_r", [P, D], F32), ("b2_l3_r", [P, D], F32),
                ("ones_b", [P, P], BF16), ("bias_h", [P, 4, D], BF16), ("bias_l1", [P, 4, D], BF16), ("bias_r", [P, 4, M + 1], BF16),
                ("bn_scale_r", [P, D], F32), ("bn_shift_r", [P, D], F32)):
            made[name] = ctx.enter_context(nc.sbuf_tensor("k_" + name, shape, dt))
        for name, width in (("agg", D), ("agg_m", M), ("x1", D), ("hs1", D), ("x2", D), ("x3", D), ("hs3", D), ("hs4", D), ("part", D), ("acc", D)):
            made[name] = nc.dram_tensor("t_" + name, [ACC if name == "acc" else NPAD, width], F32).ap()
        k = made
        k["keep_dram"] = nc.dram_tensor("t_keep", [EPAD], BF16).ap()
        k["agg_zeroed"] = [ctx.enter_context(nc.semaphore(f"agg_zeroed{i}")) for i in range(3)]
        todo = [
            lambda: prepare(nc, k, a),
            lambda: edges_layer0(nc, k, a),
            lambda: nodes_layer0(nc, k, a),
            lambda: edges_sum(nc, k, "e1_", k["hs1"], True, onto_source=True),
            lambda: nodes_batch_stats(nc, k, a),
            lambda: nodes_layer1(nc, k, a),
            lambda: edges_attention(nc, k, a),
            lambda: nodes_layer2(nc, k, a),
            lambda: edges_sum(nc, k, "e3_", k["hs3"], False, onto_source=True),
            lambda: nodes_layer3_middle(nc, k, a),
            lambda: edges_sum(nc, k, "e4_", k["hs4"], False, with_residual=True),
            lambda: nodes_layer3_out(nc, k, a),
        ]
        for run in todo:
            run()


def kernel(**inputs):
    import numpy as np
    import concourse.bacc as bacc
    from concourse.bass_utils import run_bass_kernel_spmd

    pad = EPAD - E
    dst = np.concatenate([np.asarray(inputs["dst"]), np.full(pad, NPAD - 1, np.int32)])
    arrays = {
        "x": inputs["x"],
        "src": np.concatenate([np.asarray(inputs["src"]), np.full(pad, NPAD - 1, np.int32)]),
        "dst_ext": np.concatenate([np.full(1, -1, np.int32), dst, np.full(1, -1, np.int32)]),
        "edge_weight": np.pad(np.asarray(inputs["edge_weight"]), (0, pad)),
        "edge_attr_t": np.pad(np.asarray(inputs["edge_attr_50"]).T, ((0, 0), (0, pad))),
    }
    arrays.update({n: v for n, v in inputs.items() if n.startswith("L")})
    arrays = {n: np.ascontiguousarray(v) for n, v in arrays.items()}
    nc = bacc.Bacc("TRN2", target_bir_lowering=False, num_devices=1)
    a = {n: nc.dram_tensor("in_" + n, v.shape, mybir.dt.from_np(v.dtype), kind="ExternalInput").ap()
                           for n, v in arrays.items()}
    a["out"] = nc.dram_tensor("out", (N, D), F32, kind="ExternalOutput").ap()
    build(nc, a)
    r = run_bass_kernel_spmd(nc, [{"in_" + n: v for n, v in arrays.items()}], core_ids=[0])
    return r.results[0]["out"]
```
